# Optimizing a Trainium2 kernel written in Bass

```python
import numpy as np
import jax
import jax.numpy as jnp

def _softmax(x, axis=-1):
    return jax.nn.softmax(x, axis=axis)

def _gelu(x):
    return jax.nn.gelu(x, approximate=True)

def _silu(x):
    return jax.nn.silu(x)

def _sigmoid(x):
    return jax.nn.sigmoid(x)

def _layernorm(x, axis=-1, eps=1e-05):
    m = jnp.mean(x, axis=axis, keepdims=True)
    v = jnp.var(x, axis=axis, keepdims=True)
    return (x - m) / jnp.sqrt(v + eps)

def _scatter_add(tgt, idx, src, axis=0):
    return tgt.at[idx].add(src)

def _segment_sum(src, seg, n):
    return jax.ops.segment_sum(src, seg, n)
kernel_name = 'mk_prb_d2_jaxref_r8_ee508c'

def setup_inputs(seed: int=0):
    np.random.seed(seed)
    _w = jnp.asarray

    def _L0_attn_setup():
        import jax, jax.numpy as jnp
        import numpy as np
        from jax import lax
        H = 128
        EXPAND = 2
        I = EXPAND * H
        N = 16
        K = 4
        R = 64
        EPS = 1e-06
        B_SZ, L = (2, 128)

        def rmsnorm(x, w):
            v = jnp.mean(x.astype(jnp.float32) ** 2, axis=-1, keepdims=True)
            return w * (x * jax.lax.rsqrt(v + EPS)).astype(x.dtype)
        key = jax.random.key(seed)
        ks = jax.random.split(key, 10)
        s = 0.02
        inp = {'hidden_states': jax.random.normal(ks[0], (B_SZ, L, H), jnp.float32), 'in_proj_w': jax.random.normal(ks[1], (2 * I, H), jnp.float32) * s, 'conv_w': jax.random.normal(ks[2], (I, 1, K), jnp.float32) * s, 'conv_b': jnp.zeros((I,), jnp.float32), 'x_proj_w': jax.random.normal(ks[3], (R + 2 * N, I), jnp.float32) * s, 'dt_proj_w': jax.random.normal(ks[4], (I, R), jnp.float32) * s, 'dt_proj_b': jax.random.normal(ks[5], (I,), jnp.float32) * 0.1, 'dt_ln_w': jnp.ones((R,), jnp.float32), 'b_ln_w': jnp.ones((N,), jnp.float32), 'c_ln_w': jnp.ones((N,), jnp.float32), 'A_log': jnp.log(jnp.broadcast_to(jnp.arange(1, N + 1, dtype=jnp.float32)[None, :], (I, N))), 'D': jnp.ones((I,), jnp.float32), 'out_proj_w': jax.random.normal(ks[6], (H, I), jnp.float32) * s}
        return inp
    _L0_attn_in = _L0_attn_setup()

    def _L0_ffn_setup():
        import jax, jax.numpy as jnp
        import numpy as np
        D_MODEL = 128
        D_FF = 512
        NUM_EXPERTS = 8
        key = jax.random.key(seed)
        ks = jax.random.split(key, 8)
        scale_in = 1.0 / np.sqrt(D_MODEL)
        scale_ff = 1.0 / np.sqrt(D_FF)
        x = jax.random.normal(ks[0], (4, 256, D_MODEL), dtype=jnp.float32)
        gate_w = jax.random.uniform(ks[1], (NUM_EXPERTS, D_MODEL), jnp.float32, -scale_in, scale_in)
        gate_b = jax.random.uniform(ks[2], (NUM_EXPERTS,), jnp.float32, -scale_in, scale_in)
        expert_bias = jnp.zeros((NUM_EXPERTS,), dtype=jnp.float32)
        w1 = jax.random.uniform(ks[3], (NUM_EXPERTS, D_MODEL, D_FF), jnp.float32, -scale_in, scale_in)
        b1 = jax.random.uniform(ks[4], (NUM_EXPERTS, D_FF), jnp.float32, -scale_in, scale_in)
        w2 = jax.random.uniform(ks[5], (NUM_EXPERTS, D_FF, D_MODEL), jnp.float32, -scale_ff, scale_ff)
        b2 = jax.random.uniform(ks[6], (NUM_EXPERTS, D_MODEL), jnp.float32, -scale_ff, scale_ff)
        return {'x': x, 'gate_w': gate_w, 'gate_b': gate_b, 'expert_bias': expert_bias, 'w1': w1, 'b1': b1, 'w2': w2, 'b2': b2}
    _L0_ffn_in = _L0_ffn_setup()

    def _L1_attn_setup():
        import jax, jax.numpy as jnp
        import numpy as np
        import math
        EMBED_DIM = 128
        NUM_HEADS = 16
        HEAD_DIM = EMBED_DIM // NUM_HEADS
        WINDOW_SIZE = 64
        BATCH = 2
        SEQ_LEN = 256

        def _sliding_window_mask(seq_len: int, window_size: int) -> jnp.ndarray:
            i = jnp.arange(seq_len)[:, None]
            j = jnp.arange(seq_len)[None, :]
            allowed = jnp.abs(i - j) <= window_size // 2
            return jnp.where(allowed, 0.0, -jnp.inf).astype(jnp.float32)

        def _split_heads(t):
            b, s, d = t.shape
            return t.reshape(b, s, NUM_HEADS, HEAD_DIM).transpose(0, 2, 1, 3)
        key = jax.random.key(seed)
        ks = jax.random.split(key, 9)
        s = 1.0 / math.sqrt(EMBED_DIM)
        inp = {'x': jax.random.normal(ks[0], (BATCH, SEQ_LEN, EMBED_DIM), dtype=jnp.float32), 'Wq': jax.random.normal(ks[1], (EMBED_DIM, EMBED_DIM), dtype=jnp.float32) * s, 'bq': jnp.zeros((EMBED_DIM,), dtype=jnp.float32), 'Wk': jax.random.normal(ks[2], (EMBED_DIM, EMBED_DIM), dtype=jnp.float32) * s, 'bk': jnp.zeros((EMBED_DIM,), dtype=jnp.float32), 'Wv': jax.random.normal(ks[3], (EMBED_DIM, EMBED_DIM), dtype=jnp.float32) * s, 'bv': jnp.zeros((EMBED_DIM,), dtype=jnp.float32), 'Wo': jax.random.normal(ks[4], (EMBED_DIM, EMBED_DIM), dtype=jnp.float32) * s, 'bo': jnp.zeros((EMBED_DIM,), dtype=jnp.float32)}
        return inp
    _L1_attn_in = _L1_attn_setup()

    def _L1_ffn_setup():
        import jax, jax.numpy as jnp
        import numpy as np
        DIM = 128
        HIDDEN = 384
        SCALE = 1.0 / 127.0

        def _dequant(w_int, dtype):
            return w_int.astype(dtype) * jnp.asarray(SCALE, dtype)
        key = jax.random.key(seed)
        k_x, k_g, k_u, k_d = jax.random.split(key, 4)
        x = jax.random.normal(k_x, (4, 256, DIM), dtype=jnp.float32)
        w_gate = jax.random.randint(k_g, (HIDDEN, DIM), -127, 128, dtype=jnp.int32)
        w_up = jax.random.randint(k_u, (HIDDEN, DIM), -127, 128, dtype=jnp.int32)
        w_down = jax.random.randint(k_d, (DIM, HIDDEN), -127, 128, dtype=jnp.int32)
        return {'x': x, 'w_gate': w_gate, 'w_up': w_up, 'w_down': w_down}
    _L1_ffn_in = _L1_ffn_setup()
    _d = {'L0_attn_hidden_states': _L0_attn_in['hidden_states'], 'L0_attn_in_proj_w': _L0_attn_in['in_proj_w'], 'L0_attn_conv_w': _L0_attn_in['conv_w'], 'L0_attn_conv_b': _L0_attn_in['conv_b'], 'L0_attn_x_proj_w': _L0_attn_in['x_proj_w'], 'L0_attn_dt_proj_w': _L0_attn_in['dt_proj_w'], 'L0_attn_dt_proj_b': _L0_attn_in['dt_proj_b'], 'L0_attn_dt_ln_w': _L0_attn_in['dt_ln_w'], 'L0_attn_b_ln_w': _L0_attn_in['b_ln_w'], 'L0_attn_c_ln_w': _L0_attn_in['c_ln_w'], 'L0_attn_A_log': _L0_attn_in['A_log'], 'L0_attn_D': _L0_attn_in['D'], 'L0_attn_out_proj_w': _L0_attn_in['out_proj_w'], 'L0_ffn_gate_w': _L0_ffn_in['gate_w'], 'L0_ffn_gate_b': _L0_ffn_in['gate_b'], 'L0_ffn_expert_bias': _L0_ffn_in['expert_bias'], 'L0_ffn_w1': _L0_ffn_in['w1'], 'L0_ffn_b1': _L0_ffn_in['b1'], 'L0_ffn_w2': _L0_ffn_in['w2'], 'L0_ffn_b2': _L0_ffn_in['b2'], 'L1_attn_Wq': _L1_attn_in['Wq'], 'L1_attn_bq': _L1_attn_in['bq'], 'L1_attn_Wk': _L1_attn_in['Wk'], 'L1_attn_bk': _L1_attn_in['bk'], 'L1_attn_Wv': _L1_attn_in['Wv'], 'L1_attn_bv': _L1_attn_in['bv'], 'L1_attn_Wo': _L1_attn_in['Wo'], 'L1_attn_bo': _L1_attn_in['bo'], 'L1_ffn_w_gate': _L1_ffn_in['w_gate'], 'L1_ffn_w_up': _L1_ffn_in['w_up'], 'L1_ffn_w_down': _L1_ffn_in['w_down']}
    _x0 = _d['L0_attn_hidden_states']
    _d['L0_attn_hidden_states'] = jax.random.normal(jax.random.fold_in(jax.random.key(seed), 1), (8, 512, 128), dtype=_x0.dtype)
    del _x0
    return _d

def reference(L0_attn_hidden_states, L0_attn_in_proj_w, L0_attn_conv_w, L0_attn_conv_b, L0_attn_x_proj_w, L0_attn_dt_proj_w, L0_attn_dt_proj_b, L0_attn_dt_ln_w, L0_attn_b_ln_w, L0_attn_c_ln_w, L0_attn_A_log, L0_attn_D, L0_attn_out_proj_w, L0_ffn_gate_w, L0_ffn_gate_b, L0_ffn_expert_bias, L0_ffn_w1, L0_ffn_b1, L0_ffn_w2, L0_ffn_b2, L1_attn_Wq, L1_attn_bq, L1_attn_Wk, L1_attn_bk, L1_attn_Wv, L1_attn_bv, L1_attn_Wo, L1_attn_bo, L1_ffn_w_gate, L1_ffn_w_up, L1_ffn_w_down):

    def _L0_attn_ref(hidden_states, in_proj_w, conv_w, conv_b, x_proj_w, dt_proj_w, dt_proj_b, dt_ln_w, b_ln_w, c_ln_w, A_log, D, out_proj_w):
        import jax, jax.numpy as jnp
        import numpy as np
        from jax import lax
        H = 128
        EXPAND = 2
        I = EXPAND * H
        N = 16
        K = 4
        R = 64
        EPS = 1e-06
        B_SZ, L = (2, 128)

        def rmsnorm(x, w):
            v = jnp.mean(x.astype(jnp.float32) ** 2, axis=-1, keepdims=True)
            return w * (x * jax.lax.rsqrt(v + EPS)).astype(x.dtype)
        b, l, _ = hidden_states.shape
        proj = hidden_states @ in_proj_w.T
        hs, gate = (proj[..., :I], proj[..., I:])
        x = jnp.transpose(hs, (0, 2, 1))
        x = lax.conv_general_dilated(x, conv_w, (1,), [(1, 2)], feature_group_count=I, dimension_numbers=('NCH', 'OIH', 'NCH'))
        x = x + conv_b[None, :, None]
        u = jax.nn.silu(jnp.transpose(x, (0, 2, 1)))
        x_dbl = u @ x_proj_w.T
        dt = rmsnorm(x_dbl[..., :R], dt_ln_w)
        Bm = rmsnorm(x_dbl[..., R:R + N], b_ln_w)
        Cm = rmsnorm(x_dbl[..., R + N:], c_ln_w)
        dt = jax.nn.softplus(dt @ dt_proj_w.T + dt_proj_b)
        A = -jnp.exp(A_log)
        dA = jnp.exp(dt[..., None] * A)
        dBu = (dt * u)[..., None] * Bm[:, :, None, :]

        def step(h, inp):
            dA_t, dBu_t = inp
            h = dA_t * h + dBu_t
            return (h, h)
        h0 = jnp.zeros((b, I, N), jnp.float32)
        _, h_seq = lax.scan(step, h0, (jnp.transpose(dA, (1, 0, 2, 3)), jnp.transpose(dBu, (1, 0, 2, 3))))
        y = jnp.einsum('lbin,bln->bli', h_seq, Cm)
        y = y + u * D
        y = y * jax.nn.silu(gate)
        return y @ out_proj_w.T

    def _L0_ffn_ref(x, gate_w, gate_b, expert_bias, w1, b1, w2, b2):
        import jax, jax.numpy as jnp
        import numpy as np
        D_MODEL = 128
        D_FF = 512
        NUM_EXPERTS = 8
        gate_logits = jnp.einsum('bsd,ed->bse', x, gate_w) + gate_b + expert_bias
        top_idx = jnp.argmax(gate_logits, axis=-1)
        out = jnp.zeros_like(x)
        for e in range(NUM_EXPERTS):
            mask = (top_idx == e)[..., None].astype(x.dtype)
            h = jax.nn.relu(jnp.einsum('bsd,df->bsf', x, w1[e]) + b1[e])
            y = jnp.einsum('bsf,fd->bsd', h, w2[e]) + b2[e]
            out = out + mask * y
        return out

    def _L1_attn_ref(x, Wq, bq, Wk, bk, Wv, bv, Wo, bo):
        import jax, jax.numpy as jnp
        import numpy as np
        import math
        EMBED_DIM = 128
        NUM_HEADS = 16
        HEAD_DIM = EMBED_DIM // NUM_HEADS
        WINDOW_SIZE = 64
        BATCH = 2
        SEQ_LEN = 256

        def _sliding_window_mask(seq_len: int, window_size: int) -> jnp.ndarray:
            i = jnp.arange(seq_len)[:, None]
            j = jnp.arange(seq_len)[None, :]
            allowed = jnp.abs(i - j) <= window_size // 2
            return jnp.where(allowed, 0.0, -jnp.inf).astype(jnp.float32)

        def _split_heads(t):
            b, s, d = t.shape
            return t.reshape(b, s, NUM_HEADS, HEAD_DIM).transpose(0, 2, 1, 3)
        b, s, d = x.shape
        q = _split_heads(x @ Wq + bq)
        k = _split_heads(x @ Wk + bk)
        v = _split_heads(x @ Wv + bv)
        scores = jnp.einsum('bhqd,bhkd->bhqk', q, k) / math.sqrt(HEAD_DIM)
        scores = scores + _sliding_window_mask(s, WINDOW_SIZE)
        probs = jax.nn.softmax(scores, axis=-1)
        attn = jnp.einsum('bhqk,bhkd->bhqd', probs, v)
        attn = attn.transpose(0, 2, 1, 3).reshape(b, s, d)
        return attn @ Wo + bo

    def _L1_ffn_ref(x, w_gate, w_up, w_down):
        import jax, jax.numpy as jnp
        import numpy as np
        DIM = 128
        HIDDEN = 384
        SCALE = 1.0 / 127.0

        def _dequant(w_int, dtype):
            return w_int.astype(dtype) * jnp.asarray(SCALE, dtype)
        wg = _dequant(w_gate, x.dtype)
        wu = _dequant(w_up, x.dtype)
        wd = _dequant(w_down, x.dtype)
        gate = jnp.einsum('bsd,hd->bsh', x, wg)
        up = jnp.einsum('bsd,hd->bsh', x, wu)
        h = jax.nn.silu(gate) * up
        return jnp.einsum('bsh,dh->bsd', h, wd)
    x = L0_attn_hidden_states
    xn = _layernorm(x, axis=-1)
    x = x + _L0_attn_ref(xn, L0_attn_in_proj_w, L0_attn_conv_w, L0_attn_conv_b, L0_attn_x_proj_w, L0_attn_dt_proj_w, L0_attn_dt_proj_b, L0_attn_dt_ln_w, L0_attn_b_ln_w, L0_attn_c_ln_w, L0_attn_A_log, L0_attn_D, L0_attn_out_proj_w) + _L0_ffn_ref(xn, L0_ffn_gate_w, L0_ffn_gate_b, L0_ffn_expert_bias, L0_ffn_w1, L0_ffn_b1, L0_ffn_w2, L0_ffn_b2)
    xn = _layernorm(x, axis=-1)
    x = x + _L1_attn_ref(xn, L1_attn_Wq, L1_attn_bq, L1_attn_Wk, L1_attn_bk, L1_attn_Wv, L1_attn_bv, L1_attn_Wo, L1_attn_bo) + _L1_ffn_ref(xn, L1_ffn_w_gate, L1_ffn_w_up, L1_ffn_w_down)
    return x

_drawn_inputs = setup_inputs


def setup_inputs(seed=0):
    import zlib

    import numpy as np

    out = dict(_drawn_inputs(seed))
    spreads = {'L0_attn_conv_b': (0.0, 0.543),
     'L0_attn_dt_ln_w': (1.0, 0.6),
     'L0_attn_b_ln_w': (1.0, 0.6),
     'L0_attn_c_ln_w': (1.0, 0.6),
     'L0_attn_D': (1.0, 0.6),
     'L0_ffn_expert_bias': (0.0, 0.1),
     'L1_attn_bq': (0.0, 0.8),
     'L1_attn_bk': (0.0, 2.0),
     'L1_attn_bv': (0.0, 2.0),
     'L1_attn_bo': (0.0, 2.0)}
    factors = {'L0_attn_in_proj_w': 3.955,
     'L0_attn_conv_w': 8.0,
     'L0_attn_x_proj_w': 7.174,
     'L0_attn_dt_proj_w': 8.0,
     'L0_attn_dt_proj_b': 8.0,
     'L0_attn_A_log': 8.0,
     'L0_attn_out_proj_w': 3.776,
     'L1_attn_Wq': 8.0,
     'L1_attn_Wk': 8.0,
     'L1_attn_Wv': 8.0,
     'L1_attn_Wo': 8.0,
     'L0_ffn_b1': 3.54,
     'L0_ffn_b2': 2.875}
    for name, (base, spread) in spreads.items():
        noise = np.random.default_rng([zlib.crc32(name.encode()), seed]).standard_normal(out[name].shape)
        drawn = base * np.exp(spread * noise) if base else spread * noise
        out[name] = jnp.asarray(drawn.astype(out[name].dtype))
    for name, factor in factors.items():
        out[name] = (out[name] * factor).astype(out[name].dtype)
    return out
```

```python
from contextlib import ExitStack

import numpy as np

import concourse.bass as bass
from concourse import mybir

F32 = mybir.dt.float32
BF16 = mybir.dt.bfloat16
I32 = mybir.dt.int32
ALU = mybir.AluOpType
ACT = mybir.ActivationFunctionType
AX_X = mybir.AxisListType.X

P = 128
B, L, H = 8, 512, 128
NT = L // P
I, N, R, KC = 256, 16, 64, 4
NH = I // P
E, FF = 8, 512
FC = FF // P
HEADS, HD = 16, 8
WIN = 32
GQ = 32
G = L // GQ
KW = GQ + 2 * WIN
RG = 4
HID = 384
HC = HID // P
LN_EPS = 1e-5
RMS_EPS = 1e-6
NEG = -1e30
XW = R + 2 * N

PACK = {}
_at = 0
for _name, _width in (("in_proj", 2 * I), ("x_proj", NH * XW), ("out_proj", NH * H), ("dt_proj", I),
                      ("wq", H), ("wk", H), ("wv", H), ("wo", H), ("conv_w", NH * KC), ("conv_b", NH),
                      ("dt_b", NH), ("a_log", NH * N), ("d", NH), ("gate_w", E), ("bq", 1), ("bk", 1),
                      ("bv", 1), ("bo", 1), ("b1", E * FC), ("b2", H), ("ln_row", XW), ("gate_b", E),
                      ("expert_b", E), ("ident", P), ("sel", 2 * N), ("band", 3 * KW), ("heads", RG),
                      ("expert_no", E), ("rms_n", 3)):
    PACK[_name] = (_at, _at + _width)
    _at += _width
PACK_W = _at

L0_USES = (["xnT", "gates", "hs0", "hs1", "zg0", "zg1", "xdbl", "maskT", "dtT", "bcT", "dtp0", "dtp1"]
           + [f"h{k}" for k in range(E * FC)] + ["outT0", "outT1"])
L0_N = len(L0_USES)
assert L0_N % 2 == 0
FFN_AT = {3: 0, 8: 1, 13: 2}
L1_USES = ["xnT", "q", "k"] + [f"v{j}" for j in range(4)]
for _g in range(G):
    L1_USES += [f"s{_g}", f"pT{_g}"] + ([f"o{_g // 2}"] if _g % 2 else [])
    if _g in FFN_AT:
        L1_USES += [f"gate{FFN_AT[_g]}", f"up{FFN_AT[_g]}"]
L1_USES += ["attnT", "fin", "finT"]
L1_N = len(L1_USES)


def program(nc, hidden, pack, w1_d, w2_d, ffn_d, out):
    ctx = ExitStack()
    with ctx:
        def sb(name, shape, dt=F32):
            return ctx.enter_context(nc.sbuf_tensor(name, shape, dt))

        def bank(name):
            return ctx.enter_context(nc.psum_tensor(name, [P, 512], F32))

        def sem(name):
            return ctx.enter_context(nc.semaphore(name))

        pk = sb("pk", [P, PACK_W])

        def pc(name, rows=P):
            a, z = PACK[name]
            return pk[0:rows, a:z]

        w1 = sb("w1", [P, E, FF])
        w2 = sb("w2", [P, E, FC, H])
        ffn = sb("ffn", [P, 3, HID])
        identb = sb("identb", [P, P], BF16)
        selb = sb("selb", [3 * 2 * N, 2 * N, P], BF16)
        bandb = sb("bandb", [P, 3, RG, KW], BF16)
        skipb = sb("skipb", [E, E, P], BF16)
        neg_a = sb("neg_a", [P, NH, N])
        exp_a = sb("exp_a", [P, NH * N])
        diag_d = sb("diag_d", [P, NH, P])
        gate_row = sb("gate_row", [P, E])
        bq_s = sb("bq_s", [P, 1])
        half_c = sb("half_c", [P, NH * (KC + 1)])
        minus_half = sb("minus_half", [P, 16])
        one = sb("one", [P, 1])
        tick = sb("tick", [P, 1])

        x_in = sb("x_in", [P, NT, H])
        x_res = sb("x_res", [P, NT, H])
        stats = sb("stats", [P, NT, 6])
        mv = sb("mv", [P, NT, 2])
        var_e = sb("var_e", [P, NT])
        rstd = sb("rstd", [P, NT])
        xn = sb("xn", [P, NT, H])
        xnT = sb("xnT", [P, L])
        logits = sb("logits", [P, NT, E])
        lmax = sb("lmax", [P, NT])
        leq = sb("leq", [P, NT, E])
        lcand = sb("lcand", [P, NT, E])
        lmin = sb("lmin", [P, NT])
        onehot = sb("onehot", [P, NT, E])
        maskT = sb("maskT", [E, L])
        notT = sb("notT", [E, L], BF16)
        hs = sb("hs", [P, NH, L + KC])
        u = sb("u", [P, NH, L])
        sg = sb("sg", [P, NH, L])
        xsq = sb("xsq", [P, NT, XW])
        ss = sb("ss", [P, NT, 3])
        ms = sb("ms", [P, NT, 3])
        rr = sb("rr", [P, NT, 3])
        xdr = sb("xdr", [P, NT, XW])
        xdn = sb("xdn", [P, NT, XW])
        bc3 = sb("bc3", [P, NT, 3, 2 * N], BF16)
        bc_r1 = sb("bc_r1", [P, NT, 2 * N])
        bc_r2 = sb("bc_r2", [P, NT, 2 * N])
        dtT = sb("dtT", [R, L])
        bcT = sb("bcT", [3 * 2 * N, L], BF16)
        drl = sb("drl", [P, NH, L])
        dc = sb("dc", [P, NH, L])
        dt = sb("dt", [P, NH, L])
        dtu = sb("dtu", [P, NH, L])
        dA = [sb(f"dA{k}", [P, NH, L]) for k in range(2)]
        dBu = sb("dBu", [P, NH, L])
        hst = [sb(f"hst{k}", [P, NH, L]) for k in range(2)]
        cb = [sb(f"cb{k}", [P, L]) for k in range(2)]
        hc = [sb(f"hc{k}", [P, NH, L]) for k in range(2)]
        z, th, tg = hst, hc[0], hc[1]
        dab, de, dw, dln = z[0], z[1], th, tg
        yg = dtu
        outT = dc[:, 0, :]
        hT = [sb(f"hT{k}", [P, L]) for k in range(2)]

        x1r = sb("x1r", [P, NT, H])
        stats1 = sb("stats1", [P, NT, 6])
        mv1 = sb("mv1", [P, NT, 2])
        var1 = sb("var1", [P, NT])
        rstd1 = sb("rstd1", [P, NT])
        xn1 = sb("xn1", [P, NT, H])
        xn1T = sb("xn1T", [P, L + 2 * WIN])
        qT = sb("qT", [P, L])
        qbd = sb("qbd", [P, G, RG, GQ])
        kT = sb("kT", [P, RG, L + 2 * WIN])
        vw = sb("vw", [KW, G, RG, HD * 4 + 1])
        nmax = sb("nmax", [P, G, RG])
        pexp = [sb(f"pexp{k}", [P, RG, KW]) for k in range(2)]
        pT = [sb(f"pT{k}", [KW, RG * P]) for k in range(2)]
        rden = sb("rden", [P, 2, RG])
        attn = sb("attn", [GQ, G, RG, 4, HD])
        fth = sb("fth", [P, L])
        fsg = sb("fsg", [P, L])
        fh = sb("fh", [P, HC, L])
        ffn_i = fh[:, :, 0:HID].bitcast(I32)
        attnT, finT = fsg, fth
        y_out = sb("y_out", [P, NT, H])

        work = [bank("work0"), bank("work1")]
        work1 = bank("work1_l1")
        b_bank = bank("b_bank")
        c_bank = bank("c_bank")
        y_bank = [bank("y_bank0"), bank("y_bank1")]
        out_bank = bank("out_bank")

        s_pack, s_w1, s_w2, s_ffn = sem("pack_in"), sem("w1_in"), sem("w2_in"), sem("ffn_in")
        s_const = sem("const_ready")
        s_constp = sem("constp_ready")
        s_expa = sem("expa_ready")
        s_xin, s_xres, s_out = sem("x_in_landed"), sem("x_res_landed"), sem("out_stored")
        s_full0 = sem("work_full")
        s_free0 = [sem("work0_free"), sem("work1_free")]
        s_full1 = sem("work_l1_full")
        s_free1 = sem("work_l1_free")
        s_stat = sem("stats_ready")
        s_rstd = sem("rstd_ready")
        s_xn = sem("xn_ready")
        s_xnT = sem("xnT_ready")
        s_gate = sem("gate_steps")
        s_maskT = sem("maskT_ready")
        s_conv = sem("conv_steps")
        s_th = sem("tanh_ready")
        s_u = sem("u_ready")
        s_tg = sem("gate_tanh_ready")
        s_sg = sem("gate_silu_ready")
        s_xsq = sem("xsq_ready")
        s_ss = sem("ss_ready")
        s_rr = sem("rr_ready")
        s_xdr = sem("xdr_ready")
        s_bc3 = sem("bc_steps")
        s_dtT = sem("dtT_ready")
        s_bcT = sem("bcT_ready")
        s_dab = sem("dt_abs_ready")
        s_de = sem("dt_exp_ready")
        s_drl = sem("dt_relu_ready")
        s_dw = sem("dt_w_ready")
        s_dc = sem("dt_c_ready")
        s_dln = sem("dt_ln_ready")
        s_dt = sem("dt_ready")
        s_dtu = sem("dtu_ready")
        s_bb, s_cc = sem("b_bank_full"), sem("c_bank_full")
        s_dA, s_dBu, s_h, s_cb, s_hc = sem("dA_ready"), sem("dBu_ready"), sem("h_ready"), sem("cb_ready"), sem("hc_ready")
        s_ys = sem("y_summed")
        s_hT = sem("hT_ready")
        s_w2d = sem("expert_added")
        s_yg = sem("yg_ready")
        s_outb = sem("out_bank_full")
        s_outT = sem("outT_ready")
        s_x1c = sem("x1_copied")
        s_stat1, s_rstd1, s_xn1 = sem("stats1_ready"), sem("rstd1_ready"), sem("xn1_ready")
        s_xn1T, s_q, s_qbd, s_k, s_v = sem("xn1T_ready"), sem("q_ready"), sem("qbd_ready"), sem("k_ready"), sem("v_ready")
        s_nmax, s_pexp, s_pT = sem("nmax_ready"), sem("pexp_ready"), sem("pT_ready")
        s_pv = sem("pv_done")
        s_rden, s_attn, s_attnT = sem("rden_ready"), sem("attn_ready"), sem("attnT_ready")
        s_fth, s_fsg, s_fh = sem("ffn_tanh_ready"), sem("ffn_silu_ready"), sem("ffn_h_ready")
        
        block = ctx.enter_context(nc.Block())

        def w0(key):
            return work[L0_USES.index(key) % 2]

        def full0(eng, b, key):
            eng.wait_ge(s_full0, b * L0_N + L0_USES.index(key) + 1)

        def free0(key):
            return s_free0[L0_USES.index(key) % 2]

        def take0(eng, b, key):
            k = L0_USES.index(key)
            n = b * (L0_N // 2) + k // 2
            if isinstance(b, int) and n <= 0:
                return
            eng.wait_ge(s_free0[k % 2], n)

        def done0(eng, b, key):
            k = L0_USES.index(key)
            eng.wait_ge(s_free0[k % 2], b * (L0_N // 2) + k // 2 + 1)

        def full1(eng, b, key):
            eng.wait_ge(s_full1, b * L1_N + L1_USES.index(key) + 1)

        def take1(eng, b, key):
            n = b * L1_N + L1_USES.index(key)
            if isinstance(b, int) and n <= 0:
                return
            eng.wait_ge(s_free1, n)

        def before(eng, s, n):
            if isinstance(n, int) and n <= 0:
                return
            eng.wait_ge(s, n)

        def layer0_done(eng, b):
            before(eng, s_free0[0], b * (L0_N // 2))
            before(eng, s_free0[1], b * (L0_N // 2))

        def layer1_done(eng, b):
            before(eng, s_free1, b * L1_N)

        def sequences(eng, body):
            body(0, None)
            body(1, 0)
            with eng.Fori(2, B) as b:
                body(b, b - 1)
            body(None, B - 1)

        @block.sync
        def _(sp):
            sp.dma_start(pk[:], pack).then_inc(s_pack, 16)

            def body(b0, b1):
                if b0 is not None:
                    before(sp, s_xn, b0 * NT)
                    sp.dma_start(x_in[:], hidden[b0, :, :].rearrange("(j p) d -> p j d", p=P)
                                 if isinstance(b0, int) else
                                 hidden[bass.ds(b0, 1), :, :].rearrange("o (j p) d -> p (o j) d", p=P)
                                 ).then_inc(s_xin, 16)
                    if isinstance(b0, int) and b0 == 0:
                        sp.dma_start(w1[:], w1_d).then_inc(s_w1, 16)
                        sp.dma_start(w2[:], w2_d).then_inc(s_w2, 16)
                        sp.dma_start(ffn_i, ffn_d).then_inc(s_ffn, 16)
                    before(sp, s_x1c, b0)
                    sp.dma_start(x_res[:], hidden[b0, :, :].rearrange("(j p) d -> p j d", p=P)
                                 if isinstance(b0, int) else
                                 hidden[bass.ds(b0, 1), :, :].rearrange("o (j p) d -> p (o j) d", p=P)
                                 ).then_inc(s_xres, 16)
                if b1 is not None:
                    layer1_done(sp, b1 + 1)
                    sp.dma_start(out[b1, :, :].rearrange("(j p) d -> p j d", p=P)
                                 if isinstance(b1, int) else
                                 out[bass.ds(b1, 1), :, :].rearrange("o (j p) d -> p (o j) d", p=P),
                                 y_out[:]).then_inc(s_out, 16)
            sequences(sp, body)
            sp.wait_ge(s_out, 16 * B)

        @block.vector
        def _(dve):
            v = nc.vector
            v.memset(minus_half[:], -0.5).then_inc(s_const, 1)
            v.memset(one[:], 1.0).then_inc(s_const, 1)
            v.memset(hs[:], 0.0).then_inc(s_const, 1)
            v.memset(xn1T[:], 0.0).then_inc(s_const, 1)
            v.memset(kT[:], 0.0).then_inc(s_const, 1)
            v.memset(vw[:], 1.0).then_inc(s_const, 1)
            for k in range(2):
                v.memset(dA[k][:], 0.0).then_inc(s_const, 1)
            dve.wait_ge(s_pack, 16)
            a = PACK["conv_w"][0]
            v.tensor_scalar(half_c[:], pk[:, a:a + NH * (KC + 1)], 0.5, None, ALU.mult).then_inc(s_const, 1)
            a = PACK["in_proj"][0]
            v.tensor_scalar(pk[:, a + I:a + 2 * I], pk[:, a + I:a + 2 * I], 0.5, None, ALU.mult).then_inc(s_const, 1)
            v.tensor_copy(identb[:], pc("ident")).then_inc(s_const, 1)
            v.tensor_copy(selb[:], pc("sel", 96).unsqueeze(2).to_broadcast([96, 2 * N, P])).then_inc(s_const, 1)
            v.tensor_copy(bandb[:], pc("band").rearrange("p (v k) -> p v k", v=3).unsqueeze(2)
                          .to_broadcast([P, 3, RG, KW])).then_inc(s_const, 1)
            v.tensor_scalar(skipb[:], pc("ident", E)[:, 0:E].unsqueeze(2).to_broadcast([E, E, P]), NEG, None,
                            ALU.mult).then_inc(s_const, 1)
            for h in range(NH):
                v.tensor_scalar(diag_d[:, h, :], pc("ident"), pc("d")[:, h:h + 1], None, ALU.mult).then_inc(s_const, 1)
            v.tensor_tensor(gate_row[:], pc("gate_b"), pc("expert_b"), ALU.add).then_inc(s_const, 1)
            v.tensor_scalar(bq_s[:], pc("bq"), float(HD) ** -0.5, None, ALU.mult).then_inc(s_const, 1)
            dve.wait_ge(s_expa, 1)
            v.tensor_scalar(neg_a[:], exp_a[:].rearrange("p (h n) -> p h n", h=NH), -1.0, None, ALU.mult).then_inc(s_const, 1)
            dve.wait_ge(s_ffn, 16)
            v.tensor_scalar(ffn[:], ffn_i, 1.0 / 127.0, None, ALU.mult).then_inc(s_const, 1)
            dve.wait_ge(s_const, 20)
            v.tensor_scalar(ffn[:, 0, :], ffn[:, 0, :], 0.5, None, ALU.mult).then_inc(s_const, 1)
            dve.wait_ge(s_const, 21)

            def norm(b, src, stats, mv, var_e, rstd, xn, s_stat, s_rstd, s_xn):
                for j in range(NT):
                    v.bn_stats(stats[:, j, :], src[:, j, :]).then_inc(s_stat, 1)
                dve.wait_ge(s_stat, b * 9 + 4)
                v.memset(tick[:], 0.0)
                for j in range(NT):
                    v.bn_aggr(mv[:, j, :], stats[:, j, :]).then_inc(s_stat, 1)
                dve.wait_ge(s_stat, b * 9 + 8)
                v.tensor_scalar(var_e[:], mv[:, :, 1], LN_EPS, None, ALU.add).then_inc(s_stat, 1)
                dve.wait_ge(s_rstd, b + 1)
                for j in range(NT):
                    v.tensor_scalar(xn[:, j, :], src[:, j, :], mv[:, j, 0:1], rstd[:, j:j + 1],
                                    ALU.subtract, ALU.mult).then_inc(s_xn, 1)

            def pre0(b):
                layer0_done(dve, b)
                dve.wait_ge(s_xin, b * 16 + 16)
                norm(b, x_in, stats, mv, var_e, rstd, xn, s_stat, s_rstd, s_xn)
                full0(dve, b, "gates")
                v.tensor_tensor(logits[:], w0("gates")[:, 0:NT * E].rearrange("p (j e) -> p j e", e=E),
                                gate_row[:].unsqueeze(1).to_broadcast([P, NT, E]), ALU.add).then_inc(free0("gates"), 1)
                done0(dve, b, "gates")
                v.tensor_reduce(lmax[:], logits[:], AX_X, ALU.max).then_inc(s_gate, 1)
                dve.wait_ge(s_gate, b * 5 + 1)
                v.tensor_tensor(leq[:], logits[:], lmax[:].unsqueeze(2).to_broadcast([P, NT, E]),
                                ALU.is_equal).then_inc(s_gate, 1)
                dve.wait_ge(s_gate, b * 5 + 2)
                v.scalar_tensor_tensor(lcand[:], leq[:], -100.0,
                                       pc("expert_no").unsqueeze(1).to_broadcast([P, NT, E]),
                                       ALU.mult, ALU.add).then_inc(s_gate, 1)
                dve.wait_ge(s_gate, b * 5 + 3)
                v.tensor_reduce(lmin[:], lcand[:], AX_X, ALU.min).then_inc(s_gate, 1)
                dve.wait_ge(s_gate, b * 5 + 4)
                v.tensor_tensor(onehot[:], lcand[:], lmin[:].unsqueeze(2).to_broadcast([P, NT, E]),
                                ALU.is_equal).then_inc(s_gate, 1)
                for k in range(KC):
                    for h in range(NH):
                        src = hs[:, h, k:k + L]
                        w = half_c[:, h * KC + k:h * KC + k + 1]
                        if k == 0:
                            done0(dve, b, f"hs{h}")
                            v.tensor_scalar(z[0][:, h, :], src, w, half_c[:, NH * KC + h:NH * KC + h + 1],
                                            ALU.mult, ALU.add).then_inc(s_conv, 1)
                        else:
                            dve.wait_ge(s_conv, b * NH * KC + (k - 1) * NH + h + 1)
                            v.scalar_tensor_tensor(z[k % 2][:, h, :], src, w, z[(k - 1) % 2][:, h, :],
                                                   ALU.mult, ALU.add).then_inc(s_conv, 1)
                for h in range(NH):
                    dve.wait_ge(s_th, b * NH + h + 1)
                    v.scalar_tensor_tensor(u[:, h, :], th[:, h, :], 1.0, z[1][:, h, :],
                                           ALU.add, ALU.mult).then_inc(s_u, 1)
                for h in range(NH):
                    dve.wait_ge(s_tg, b * NH + h + 1)
                    v.scalar_tensor_tensor(sg[:, h, :], tg[:, h, :], 1.0, w0(f"zg{h}")[:],
                                           ALU.add, ALU.mult).then_inc(free0(f"zg{h}"), 1)
                full0(dve, b, "maskT")
                v.tensor_copy(maskT[:], w0("maskT")[0:E, :]).then_inc(s_maskT, 1)
                v.tensor_scalar(notT[:], w0("maskT")[0:E, :], -1.0, 1.0, ALU.mult, ALU.add).then_inc(free0("maskT"), 1)
                dve.wait_ge(s_xsq, b + 1)
                for k, (a, w) in enumerate(((0, R), (R, N), (R + N, N))):
                    v.tensor_reduce(ss[:, :, k], xsq[:, :, a:a + w], AX_X, ALU.add).then_inc(s_ss, 1)
                dve.wait_ge(s_ss, b * 5 + 3)
                v.tensor_tensor(ms[:], ss[:], pc("rms_n").unsqueeze(1).to_broadcast([P, NT, 3]),
                                ALU.mult).then_inc(s_ss, 1)
                dve.wait_ge(s_ss, b * 5 + 4)
                v.tensor_scalar(ms[:], ms[:], RMS_EPS, None, ALU.add).then_inc(s_ss, 1)
                dve.wait_ge(s_rr, b + 1)
                xd = w0("xdbl")[:, 0:NT * XW].rearrange("p (j c) -> p j c", c=XW)
                for k, (a, w) in enumerate(((0, R), (R, N), (R + N, N))):
                    last = v.tensor_tensor(xdr[:, :, a:a + w], xd[:, :, a:a + w],
                                           rr[:, :, k:k + 1].to_broadcast([P, NT, w]), ALU.mult)
                    last.then_inc(free0("xdbl") if k == 2 else s_xdr, 1)
                for h in range(NH):
                    dve.wait_ge(s_dab, b * NH + h + 1)
                    v.tensor_scalar(drl[:, h, :], w0(f"dtp{h}")[:], pc("dt_b")[:, h:h + 1], 0.0,
                                    ALU.add, ALU.max).then_inc(free0(f"dtp{h}"), 1)
                dve.wait_ge(s_de, b + 1)
                v.tensor_scalar(dw[:], de[:], 1.0, None, ALU.add).then_inc(s_dw, 1)
                dve.wait_ge(s_dw, b + 1)
                v.scalar_tensor_tensor(dc[:], dw[:], -1.0, de[:], ALU.add, ALU.subtract).then_inc(s_dc, 1)
                dve.wait_ge(s_dc, b * 2 + 1)
                dve.wait_ge(s_dln, b + 1)
                v.tensor_tensor(dc[:], dln[:], dc[:], ALU.subtract).then_inc(s_dc, 1)
                dve.wait_ge(s_dc, b * 2 + 2)
                done0(dve, b, "dtp0")
                done0(dve, b, "dtp1")
                v.tensor_tensor(dt[:], dc[:], drl[:], ALU.add).then_inc(s_dt, 1)
                dve.wait_ge(s_dt, b + 1)
                dve.wait_ge(s_u, b * NH + NH)
                v.tensor_tensor(dtu[:], dt[:], u[:], ALU.mult).then_inc(s_dtu, 1)

            def pre1(b):
                layer1_done(dve, b)
                dve.wait_ge(s_x1c, b + 1)
                norm(b, x1r, stats1, mv1, var1, rstd1, xn1, s_stat1, s_rstd1, s_xn1)

            def scan_in(b, n):
                if n == 0:
                    dve.wait_ge(s_dtu, b + 1)
                dve.wait_ge(s_bb, b * N + n + 1)
                before(dve, s_h, b * N + n)
                v.tensor_tensor(dBu[:], dtu[:], b_bank[:].unsqueeze(1).to_broadcast([P, NH, L]),
                                ALU.mult).then_inc(s_dBu, 1)

            def scan(b, n):
                dve.wait_ge(s_dBu, b * N + n + 1)
                dve.wait_ge(s_dA, (b * N + n + 1) * NH)
                before(dve, s_hc, b * N + n - 1)
                v.tensor_tensor_scan(hst[n % 2][:].rearrange("p h t -> p (h t)"),
                                     dA[n % 2][:].rearrange("p h t -> p (h t)"),
                                     dBu[:].rearrange("p h t -> p (h t)"), 0.0,
                                     ALU.mult, ALU.add).then_inc(s_h, 1)

            def row_max(b, g):
                full1(dve, b, f"s{g}")
                v.tensor_reduce(nmax[:, g, :], work1[:, 0:RG * KW].rearrange("p (r k) -> p r k", r=RG), AX_X,
                                ALU.max, negate=True).then_inc(s_nmax, 1)

            def heads_out(b, g):
                full1(dve, b, f"o{g // 2}")
                o = work1[:, 0:2 * RG * 33].rearrange("p (c r d) -> p c r d", c=2, r=RG)
                v.reciprocal(rden[:], o[:, :, :, 32]).then_inc(s_rden, 1)
                dve.wait_ge(s_rden, b * (G // 2) + g // 2 + 1)
                for k in range(4):
                    q = slice(32 * k, 32 * k + 32)
                    last = v.tensor_tensor(attn[:, g - 1:g + 1, :, k, :], o[q, :, :, HD * k:HD * k + HD],
                                           rden[q, :, :].unsqueeze(3).to_broadcast([32, 2, RG, HD]), ALU.mult)
                    last.then_inc(s_free1 if k == 3 else s_attn, 1)

            def ffn_chunk(b, c):
                dve.wait_ge(s_fth, b * HC + c + 1)
                v.scalar_tensor_tensor(fsg[:], fth[:], 1.0, work1[:], ALU.add, ALU.mult).then_inc(s_free1, 1)
                full1(dve, b, f"up{c}")
                dve.wait_ge(s_free1, b * L1_N + L1_USES.index(f"up{c}"))
                v.tensor_tensor(fh[:, c, :], fsg[:], work1[:], ALU.mult).then_inc(s_free1, 1)

            def post0(b):
                dve.wait_ge(s_ys, b * (N + 1) + N + 1)
                for h in range(NH):
                    v.tensor_tensor(yg[:, h, :], y_bank[h][:], sg[:, h, :], ALU.mult).then_inc(s_yg, 1)
                dve.wait_ge(s_xres, b * 16 + 16)
                before(dve, s_x1c, b)
                for k in range(2):
                    full0(dve, b, f"outT{k}")
                    v.tensor_tensor(x_res[:, 2 * k:2 * k + 2, :], x_res[:, 2 * k:2 * k + 2, :],
                                    w0(f"outT{k}")[:, 0:256].rearrange("p (j d) -> p j d", j=2),
                                    ALU.add).then_inc(free0(f"outT{k}"), 1)

            def post1(b):
                full1(dve, b, "finT")
                before(dve, s_out, b * 16)
                v.tensor_tensor(y_out[:], x1r[:], work1[:].rearrange("p (j d) -> p j d", j=NT),
                                ALU.add).then_inc(s_free1, 1)

            def body(b0, b1):
                if b0 is not None:
                    pre0(b0)
                if b1 is not None:
                    pre1(b1)
                for n in range(N):
                    if b0 is not None:
                        scan_in(b0, n)
                    if b1 is not None:
                        row_max(b1, n)
                    if b0 is not None:
                        scan(b0, n)
                    if b1 is not None and n % 2:
                        heads_out(b1, n)
                    if b1 is not None and n in FFN_AT:
                        ffn_chunk(b1, FFN_AT[n])
                if b0 is not None:
                    post0(b0)
                if b1 is not None:
                    post1(b1)
            sequences(dve, body)

        @block.scalar
        def _(act):
            s = nc.scalar
            act.wait_ge(s_pack, 16)
            s.activation(exp_a[:], pc("a_log"), ACT.Exp).then_inc(s_expa, 1)
            act.wait_ge(s_const, 21)

            def pre0(b):
                layer0_done(act, b)
                full0(act, b, "xnT")
                s.copy(xnT[:], w0("xnT")[:]).then_inc(free0("xnT"), 1)
                for h in range(NH):
                    full0(act, b, f"hs{h}")
                    s.copy(hs[:, h, 1:1 + L], w0(f"hs{h}")[:]).then_inc(free0(f"hs{h}"), 1)
                for h in range(NH):
                    full0(act, b, f"zg{h}")
                    s.activation(tg[:, h, :], w0(f"zg{h}")[:], ACT.Tanh).then_inc(s_tg, 1)
                for h in range(NH):
                    act.wait_ge(s_conv, b * NH * KC + (KC - 1) * NH + h + 1)
                    s.activation(th[:, h, :], z[1][:, h, :], ACT.Tanh).then_inc(s_th, 1)
                full0(act, b, "xdbl")
                s.activation(xsq[:], w0("xdbl")[:, 0:NT * XW].rearrange("p (j c) -> p j c", c=XW),
                             ACT.Square).then_inc(s_xsq, 1)
                full0(act, b, "dtT")
                s.copy(dtT[:], w0("dtT")[0:R, :]).then_inc(free0("dtT"), 1)
                full0(act, b, "bcT")
                s.copy(bcT[:], w0("bcT")[0:96, :].bitcast(BF16)[:, 0:L]).then_inc(free0("bcT"), 1)
                for h in range(NH):
                    full0(act, b, f"dtp{h}")
                    s.activation(dab[:, h, :], w0(f"dtp{h}")[:], ACT.Abs, bias=pc("dt_b")[:, h:h + 1]).then_inc(s_dab, 1)
                act.wait_ge(s_dab, b * NH + NH)
                s.activation(de[:], dab[:], ACT.Exp, scale=-1.0).then_inc(s_de, 1)
                act.wait_ge(s_dw, b + 1)
                s.activation(dln[:], dw[:], ACT.Ln).then_inc(s_dln, 1)

            def pre1(b):
                layer1_done(act, b)
                full1(act, b, "xnT")
                s.copy(xn1T[:, WIN:WIN + L], work1[:]).then_inc(s_free1, 1)
                full1(act, b, "q")
                s.activation(qT[:], work1[:], ACT.Identity, bias=bq_s[:], scale=float(HD) ** -0.5).then_inc(s_free1, 1)
                full1(act, b, "k")
                for r in range(RG):
                    q = slice(32 * r, 32 * r + 32)
                    last = s.activation(kT[q, r, WIN:WIN + L], work1[q, :], ACT.Identity, bias=pc("bk")[q, :])
                last.then_inc(s_free1, 1)
                for j in range(4):
                    full1(act, b, f"v{j}")
                    s.copy(vw[:, 4 * j:4 * j + 4, :, 0:32],
                           work1[0:KW, :].rearrange("p (g r d) -> p g r d", g=4, r=RG)).then_inc(s_free1, 1)

            def c_copy(b, n):
                act.wait_ge(s_cc, b * N + n + 1)
                before(act, s_hc, b * N + n - 1)
                s.copy(cb[n % 2][:], c_bank[:]).then_inc(s_cb, 1)

            def decay(b, n):
                if n == 0:
                    act.wait_ge(s_dt, b + 1)
                before(act, s_h, b * N + n - 1)
                for h in range(NH):
                    s.activation(dA[n % 2][:, h, 1:L], dt[:, h, 1:L], ACT.Exp,
                                 scale=neg_a[:, h, n:n + 1]).then_inc(s_dA, 1)

            def relu(b, k):
                full0(act, b, f"h{k}")
                before(act, s_w2d, b * E * FC + k - 1)
                s.activation(hT[k % 2][:], w0(f"h{k}")[:], ACT.Relu, bias=pc("b1")[:, k:k + 1]).then_inc(free0(f"h{k}"), 1)

            def softmax_exp(b, g):
                act.wait_ge(s_nmax, b * G + g + 1)
                before(act, s_full1, b * L1_N + L1_USES.index(f"pT{g - 2}") + 1 if g >= 2 else
                       (b - 1) * L1_N + L1_USES.index(f"pT{G - 2 + g}") + 1)
                for r in range(RG):
                    last = s.activation(pexp[g % 2][:, r, :], work1[:, r * KW:(r + 1) * KW], ACT.Exp,
                                        bias=nmax[:, g, r:r + 1])
                last.then_inc(s_free1, 1)

            def p_copy(b, g):
                full1(act, b, f"pT{g}")
                before(act, s_full1, b * L1_N + L1_USES.index(f"o{g // 2 - 1}") + 1 if g >= 2 else 0)
                s.copy(pT[g % 2][:], work1[0:KW, :]).then_inc(s_free1, 1)

            def ffn_tanh(b, c):
                full1(act, b, f"gate{c}")
                s.activation(fth[:], work1[:], ACT.Tanh).then_inc(s_fth, 1)

            def post0(b):
                act.wait_ge(s_outb, b + 1)
                s.copy(outT, out_bank[:]).then_inc(s_outT, 1)
                layer0_done(act, b + 1)
                layer1_done(act, b)
                s.copy(x1r[:], x_res[:]).then_inc(s_x1c, 1)

            def post1(b):
                full1(act, b, "attnT")
                s.activation(attnT[:], work1[:], ACT.Identity, bias=pc("bv")).then_inc(s_free1, 1)
                full1(act, b, "fin")
                s.activation(finT[:], work1[:], ACT.Identity, bias=pc("bo")).then_inc(s_free1, 1)

            def body(b0, b1):
                if b0 is not None:
                    pre0(b0)
                if b1 is not None:
                    pre1(b1)
                if b0 is not None:
                    decay(b0, 0)
                for n in range(N):
                    if b0 is not None:
                        c_copy(b0, n)
                        if n + 1 < N:
                            decay(b0, n + 1)
                        relu(b0, 2 * n)
                    if b1 is not None:
                        softmax_exp(b1, n)
                        p_copy(b1, n)
                    if b0 is not None:
                        relu(b0, 2 * n + 1)
                    if b1 is not None and n in FFN_AT:
                        ffn_tanh(b1, FFN_AT[n])
                if b1 is not None:
                    post1(b1)
                if b0 is not None:
                    post0(b0)
            sequences(act, body)

        @block.gpsimd
        def _(pool):
            g_ = nc.gpsimd
            pool.wait_ge(s_const, 21)

            def pre0(b):
                layer0_done(pool, b)
                pool.wait_ge(s_stat, b * 9 + 9)
                g_.tensor_tensor(rstd[:], var_e[:], minus_half[:, 0:NT], ALU.pow).then_inc(s_rstd, 1)
                pool.wait_ge(s_ss, b * 5 + 5)
                g_.tensor_tensor(rr[:].rearrange("p j k -> p (j k)"), ms[:].rearrange("p j k -> p (j k)"),
                                 minus_half[:, 0:NT * 3], ALU.pow).then_inc(s_rr, 1)
                done0(pool, b, "xdbl")
                g_.tensor_tensor(xdn[:], xdr[:], pc("ln_row").unsqueeze(1).to_broadcast([P, NT, XW]),
                                 ALU.mult).then_inc(s_bc3, 1)
                bc = xdn[:, :, R:XW]
                ones = one[:].unsqueeze(1).to_broadcast([P, NT, 2 * N])
                pool.wait_ge(s_bc3, b * 6 + 1)
                g_.tensor_tensor(bc3[:, :, 0, :], bc, ones, ALU.mult).then_inc(s_bc3, 1)
                pool.wait_ge(s_bc3, b * 6 + 2)
                g_.tensor_tensor(bc_r1[:], bc, bc3[:, :, 0, :], ALU.subtract).then_inc(s_bc3, 1)
                pool.wait_ge(s_bc3, b * 6 + 3)
                g_.tensor_tensor(bc3[:, :, 1, :], bc_r1[:], ones, ALU.mult).then_inc(s_bc3, 1)
                pool.wait_ge(s_bc3, b * 6 + 4)
                g_.tensor_tensor(bc_r2[:], bc_r1[:], bc3[:, :, 1, :], ALU.subtract).then_inc(s_bc3, 1)
                pool.wait_ge(s_bc3, b * 6 + 5)
                g_.tensor_tensor(bc3[:, :, 2, :], bc_r2[:], ones, ALU.mult).then_inc(s_bc3, 1)

            def pre1(b):
                layer1_done(pool, b)
                pool.wait_ge(s_stat1, b * 9 + 9)
                g_.tensor_tensor(rstd1[:], var1[:], minus_half[:, 0:NT], ALU.pow).then_inc(s_rstd1, 1)
                pool.wait_ge(s_free1, b * L1_N + L1_USES.index("q") + 1)
                g_.tensor_tensor(qbd[:], qT[:].rearrange("p (g q) -> p g q", q=GQ).unsqueeze(2)
                                 .to_broadcast([P, G, RG, GQ]),
                                 pc("heads").unsqueeze(1).unsqueeze(3).to_broadcast([P, G, RG, GQ]),
                                 ALU.mult).then_inc(s_qbd, 1)

            def times_c(b, n):
                pool.wait_ge(s_h, b * N + n + 1)
                pool.wait_ge(s_cb, b * N + n + 1)
                before(pool, s_ys, b * (N + 1) + n - 1)
                g_.tensor_tensor(hc[n % 2][:], hst[n % 2][:], cb[n % 2][:].unsqueeze(1).to_broadcast([P, NH, L]),
                                 ALU.mult).then_inc(s_hc, 1)

            def body(b0, b1):
                if b0 is not None:
                    pre0(b0)
                if b1 is not None:
                    pre1(b1)
                if b0 is not None:
                    for n in range(N):
                        times_c(b0, n)
            sequences(pool, body)

        @block.tensor
        def _(pe):
            t = nc.tensor
            ident = pc("ident")
            pe.wait_ge(s_const, 21)
            pe.wait_ge(s_w1, 16)
            pe.wait_ge(s_w2, 16)

            def pre0(b):
                for j in range(NT):
                    if j == 0:
                        take0(pe, b, "xnT")
                    pe.wait_ge(s_xn, b * NT + j + 1)
                    last = t.transpose(w0("xnT")[:, j * P:(j + 1) * P], xn[:, j, :], ident)
                last.then_inc(s_full0, 1)
                done0(pe, b, "xnT")
                take0(pe, b, "gates")
                for j in range(NT):
                    last = t.matmul(w0("gates")[:, j * E:(j + 1) * E], xnT[:, j * P:(j + 1) * P], pc("gate_w"),
                                    start=True, stop=True)
                last.then_inc(s_full0, 1)
                for k, key in enumerate(("hs0", "hs1", "zg0", "zg1")):
                    take0(pe, b, key)
                    t.matmul(w0(key)[:], pc("in_proj")[:, k * P:(k + 1) * P], xnT[:], start=True,
                             stop=True).then_inc(s_full0, 1)
                take0(pe, b, "xdbl")
                pe.wait_ge(s_u, b * NH + NH)
                for j in range(NT):
                    for h in range(NH):
                        last = t.matmul(w0("xdbl")[:, j * XW:(j + 1) * XW], u[:, h, j * P:(j + 1) * P],
                                        pc("x_proj")[:, h * XW:(h + 1) * XW], start=(h == 0), stop=(h == NH - 1))
                last.then_inc(s_full0, 1)
                take0(pe, b, "maskT")
                pe.wait_ge(s_gate, b * 5 + 5)
                for j in range(NT):
                    last = t.transpose(w0("maskT")[0:E, j * P:(j + 1) * P], onehot[:, j, :], ident)
                last.then_inc(s_full0, 1)
                take0(pe, b, "dtT")
                pe.wait_ge(s_bc3, b * 6 + 1)
                for j in range(NT):
                    last = t.transpose(w0("dtT")[0:XW, j * P:(j + 1) * P], xdn[:, j, :], ident)
                last.then_inc(s_full0, 1)
                take0(pe, b, "bcT")
                pe.wait_ge(s_bc3, b * 6 + 6)
                for j in range(NT):
                    last = t.transpose(w0("bcT")[0:96, :].bitcast(BF16)[:, j * P:(j + 1) * P],
                                       bc3[:, j, :, :].rearrange("p k n -> p (k n)"), identb[:])
                last.then_inc(s_full0, 1)
                done0(pe, b, "dtT")
                for h in range(NH):
                    take0(pe, b, f"dtp{h}")
                    t.matmul(w0(f"dtp{h}")[:], pc("dt_proj", R)[:, h * P:(h + 1) * P], dtT[:], start=True,
                             stop=True).then_inc(s_full0, 1)
                done0(pe, b, "bcT")
                before(pe, s_outT, b)
                pe.wait_ge(s_maskT, b + 1)
                t.matmul(out_bank[:], pc("b2", E), maskT[:], start=True, stop=False)

            def pre1(b):
                take1(pe, b, "xnT")
                for j in range(NT):
                    pe.wait_ge(s_xn1, b * NT + j + 1)
                    last = t.transpose(work1[:, j * P:(j + 1) * P], xn1[:, j, :], ident)
                last.then_inc(s_full1, 1)
                for key, w in (("q", "wq"), ("k", "wk")):
                    take1(pe, b, key)
                    t.matmul(work1[:], pc(w), xn1T[:, WIN:WIN + L], start=True, stop=True).then_inc(s_full1, 1)
                for j in range(4):
                    take1(pe, b, f"v{j}")
                    for g in range(4):
                        a = (4 * j + g) * GQ
                        last = t.matmul(work1[0:KW, g * P:(g + 1) * P], xn1T[:, a:a + KW], pc("wv"),
                                        start=True, stop=True)
                    last.then_inc(s_full1, 1)
                pe.wait_ge(s_qbd, b + 1)

            def spread(b, n):
                before(pe, s_dBu, b * N + n)
                t.matmul(b_bank[:], selb[:, n, :], bcT[:], start=True, stop=True).then_inc(s_bb, 1)
                before(pe, s_cb, b * N + n)
                t.matmul(c_bank[:], selb[:, N + n, :], bcT[:], start=True, stop=True).then_inc(s_cc, 1)

            def sum_y(b, n):
                if n == 0:
                    before(pe, s_yg, NH * b)
                    for h in range(NH):
                        last = t.matmul(y_bank[h][:], diag_d[:, h, :], u[:, h, :], start=True, stop=False)
                    last.then_inc(s_ys, 1)
                pe.wait_ge(s_hc, b * N + n + 1)
                for h in range(NH):
                    last = t.matmul(y_bank[h][:], ident, hc[n % 2][:, h, :], start=False, stop=(n == N - 1))
                last.then_inc(s_ys, 1)

            def expert_in(b, k):
                e, c = k // FC, k % FC
                take0(pe, b, f"h{k}")
                bank = w0(f"h{k}")[:]
                t.matmul(bank, w1[:, e, c * P:(c + 1) * P], xnT[:], start=True, stop=False)
                t.matmul(bank, skipb[:, e, :], notT[:], start=False, stop=True).then_inc(s_full0, 1)

            def expert_out(b, k):
                done0(pe, b, f"h{k}")
                t.matmul(out_bank[:], w2[:, k // FC, k % FC, :], hT[k % 2][:], start=False,
                         stop=False).then_inc(s_w2d, 1)

            def scores(b, g):
                take1(pe, b, f"s{g}")
                v = 0 if g == 0 else (2 if g == G - 1 else 1)
                t.matmul(work1[:, 0:RG * KW], identb[:], bandb[:, v, :, :].rearrange("p r k -> p (r k)"),
                         start=True, stop=False)
                t.matmul(work1[:, 0:RG * KW], qbd[:, g, :, :].rearrange("p h q -> p (h q)"),
                         kT[:, :, g * GQ:g * GQ + KW], start=False, stop=True).then_inc(s_full1, 1)

            def probs_t(b, g):
                take1(pe, b, f"pT{g}")
                for r in range(RG):
                    last = t.transpose(work1[0:KW, r * P:(r + 1) * P], pexp[g % 2][:, r, :], ident)
                last.then_inc(s_full1, 1)

            def values(b, g):
                take1(pe, b, f"o{g // 2}")
                for c in range(2):
                    for r in range(RG):
                        a = (c * RG + r) * 33
                        last = t.matmul(work1[:, a:a + 33], pT[c][:, r * P:(r + 1) * P],
                                        vw[:, g - 1 + c, r, :], start=True, stop=True)
                last.then_inc(s_full1, 1)

            def ffn_in(b, c):
                for k, key in enumerate((f"gate{c}", f"up{c}")):
                    take1(pe, b, key)
                    t.matmul(work1[:], ffn[:, k, c * P:(c + 1) * P], xn1T[:, WIN:WIN + L], start=True,
                             stop=True).then_inc(s_full1, 1)

            def post0(b):
                expert_out(b, E * FC - 1)
                sum_y(b, N - 1)
                pe.wait_ge(s_yg, NH * b + NH)
                for h in range(NH):
                    last = t.matmul(out_bank[:], pc("out_proj")[:, h * P:(h + 1) * P], yg[:, h, :], start=False,
                                    stop=(h == NH - 1))
                last.then_inc(s_outb, 1)
                pe.wait_ge(s_outT, b + 1)
                for k in range(2):
                    take0(pe, b, f"outT{k}")
                    for j in range(2):
                        last = t.transpose(w0(f"outT{k}")[:, j * P:(j + 1) * P],
                                           outT[:, (2 * k + j) * P:(2 * k + j + 1) * P], ident)
                    last.then_inc(s_full0, 1)

            def post1(b):
                take1(pe, b, "attnT")
                t.matmul(work1[:, 0:2], identb[:], identb[:, 0:2], start=True, stop=True)
                for g in range(G):
                    last = t.transpose(work1[:, g * GQ:(g + 1) * GQ],
                                       attn[:, g, :, :, :].rearrange("p r h d -> p (r h d)"), ident[0:GQ, 0:GQ])
                last.then_inc(s_full1, 1)
                take1(pe, b, "fin")
                t.matmul(work1[:], pc("wo"), attnT[:], start=True, stop=False)
                for c in range(HC):
                    last = t.matmul(work1[:], ffn[:, 2, c * P:(c + 1) * P], fh[:, c, :], start=False,
                                    stop=(c == HC - 1))
                last.then_inc(s_full1, 1)
                take1(pe, b, "finT")
                for j in range(NT):
                    last = t.transpose(work1[:, j * P:(j + 1) * P], finT[:, j * P:(j + 1) * P], ident)
                last.then_inc(s_full1, 1)

            def body(b0, b1):
                if b0 is not None:
                    pre0(b0)
                if b1 is not None:
                    pre1(b1)
                if b0 is not None:
                    spread(b0, 0)
                for n in range(N):
                    if b0 is not None and n + 1 < N:
                        spread(b0, n + 1)
                    if b1 is not None:
                        scores(b1, n)
                    if b0 is not None:
                        expert_in(b0, 2 * n)
                        if n:
                            expert_out(b0, 2 * n - 1)
                            sum_y(b0, n - 1)
                    if b1 is not None:
                        probs_t(b1, n)
                    if b0 is not None:
                        expert_in(b0, 2 * n + 1)
                        expert_out(b0, 2 * n)
                    if b1 is not None and n % 2:
                        values(b1, n)
                    if b1 is not None and n in FFN_AT:
                        ffn_in(b1, FFN_AT[n])
                if b1 is not None:
                    post1(b1)
                if b0 is not None:
                    post0(b0)
            sequences(pe, body)


def kernel(**inputs):
    import concourse.bacc as bacc
    from concourse.bass_utils import run_bass_kernel_spmd

    a = {k: np.asarray(v) for k, v in inputs.items()}
    f = np.float32

    def cols(m):
        return np.concatenate([m[i:i + P].reshape(P, -1) for i in range(0, m.shape[0], P)], axis=1)

    def rows(m):
        return np.concatenate([m, np.zeros((P - m.shape[0], m.shape[1]), m.dtype)], axis=0)

    def spread(m):
        return np.broadcast_to(m.reshape(1, -1), (P, m.size))

    q, k = np.arange(P)[:, None] % GQ, np.arange(KW)[None, :]
    inside = (k >= q) & (k <= q + 2 * WIN)
    band = [np.where(m, 0.0, NEG).astype(f) for m in (inside & (k >= WIN), inside, inside & (k < WIN + GQ))]
    ln_row = np.concatenate([a["L0_attn_dt_ln_w"], a["L0_attn_b_ln_w"], a["L0_attn_c_ln_w"]])
    parts = {
        "in_proj": a["L0_attn_in_proj_w"].T, "x_proj": cols(a["L0_attn_x_proj_w"].T),
        "out_proj": cols(a["L0_attn_out_proj_w"].T), "dt_proj": rows(a["L0_attn_dt_proj_w"].T),
        "wq": a["L1_attn_Wq"], "wk": a["L1_attn_Wk"], "wv": a["L1_attn_Wv"], "wo": a["L1_attn_Wo"],
        "conv_w": cols(a["L0_attn_conv_w"].reshape(I, KC)), "conv_b": cols(a["L0_attn_conv_b"].reshape(I, 1)),
        "dt_b": cols(a["L0_attn_dt_proj_b"].reshape(I, 1)), "a_log": cols(a["L0_attn_A_log"]),
        "d": cols(a["L0_attn_D"].reshape(I, 1)), "gate_w": a["L0_ffn_gate_w"].T,
        "bq": a["L1_attn_bq"].reshape(H, 1), "bk": a["L1_attn_bk"].reshape(H, 1),
        "bv": a["L1_attn_bv"].reshape(H, 1), "bo": a["L1_attn_bo"].reshape(H, 1),
        "b1": a["L0_ffn_b1"].reshape(E * FC, P).T, "b2": rows(a["L0_ffn_b2"]), "ln_row": spread(ln_row),
        "gate_b": spread(a["L0_ffn_gate_b"]), "expert_b": spread(a["L0_ffn_expert_bias"]),
        "ident": np.eye(P, dtype=f), "sel": rows(np.tile(np.eye(2 * N, dtype=f), (3, 1))),
        "band": np.concatenate(band, axis=1), "heads": (np.arange(P)[:, None] % 32 // HD == np.arange(RG)).astype(f),
        "expert_no": spread(np.arange(E, dtype=f)), "rms_n": spread(np.array([1 / R, 1 / N, 1 / N], f)),
    }
    ffn = np.stack([a["L1_ffn_w_gate"].T, a["L1_ffn_w_up"].T, cols(a["L1_ffn_w_down"].T)], axis=1)
    arrays = {
        "hidden": a["L0_attn_hidden_states"],
        "pack": np.concatenate([parts[n] for n in PACK], axis=1),
        "w1": a["L0_ffn_w1"].transpose(1, 0, 2),
        "w2": a["L0_ffn_w2"].reshape(E, FC, P, H).transpose(2, 0, 1, 3),
        "ffn": ffn,
    }
    arrays = {"in_" + n: np.ascontiguousarray(m) for n, m in arrays.items()}
    nc = bacc.Bacc("TRN2", target_bir_lowering=False, num_devices=1)
    args = [nc.dram_tensor(n, m.shape, mybir.dt.from_np(m.dtype), kind="ExternalInput").ap() for n, m in arrays.items()]
    out = nc.dram_tensor("out", (B, L, H), F32, kind="ExternalOutput").ap()
    program(nc, *args, out)
    r = run_bass_kernel_spmd(nc, [arrays], core_ids=[0])
    return r.results[0]["out"]
```

```python
from contextlib import ExitStack

import numpy as np

import concourse.bass as bass
from concourse import mybir

F32 = mybir.dt.float32
BF16 = mybir.dt.bfloat16
I32 = mybir.dt.int32
U32 = mybir.dt.uint32
ALU = mybir.AluOpType
ACT = mybir.ActivationFunctionType
AX_X = mybir.AxisListType.X

P = 128
B, L, H = 8, 512, 128
NT = L // P
I, N, R, KC = 256, 16, 64, 4
NH = I // P
E, FF = 8, 512
FC = FF // P
HEADS, HD = 16, 8
WIN = 32
GQ = 32
G = L // GQ
KW = GQ + 2 * WIN
RG = 4
HID = 384
HC = HID // P
LN_EPS = 1e-5
RMS_EPS = 1e-6
NEG = -1e30
XW = R + 2 * N
TT = B * NT
MG = 4
NM = -(-(TT + E - 1) // MG) * MG

PACK = {}
_at = 0
for _name, _width in (("in_proj", 2 * I), ("x_proj", NH * XW), ("out_proj", NH * H), ("dt_proj", I),
                      ("wq", H), ("wk", H), ("wv", H), ("wo", H), ("conv_w", NH * KC), ("conv_b", NH),
                      ("dt_b", NH), ("a_log", NH * N), ("d", NH), ("gate_w", E), ("bq", 1), ("bk", 1),
                      ("bv", 1), ("bo", 1), ("b1", E * FC), ("b2", E * H), ("ln_row", XW), ("gate_b", E),
                      ("expert_b", E), ("ident", P), ("sel", 2 * N), ("band", 3 * KW), ("heads", RG),
                      ("expert_no", E), ("rms_n", 3), ("below", P), ("tile_at", NM)):
    PACK[_name] = (_at, _at + _width)
    _at += _width
PACK_W = _at

ROUTE_SLOTS, ROUTE_TILES = 22, 25

L0_USES = ["xnT", "hs0", "hs1", "zg0", "zg1", "xdbl", "dtT", "bcT", "dtp0", "dtp1", "out", "outT"]
L0_N = len(L0_USES)
assert L0_N % 2 == 0
FFN_AT = {3: 0, 8: 1, 13: 2}
L1_USES = ["xnT", "q", "k"] + [f"v{j}" for j in range(4)]
for _g in range(G):
    L1_USES += [f"s{_g}", f"pT{_g}"] + ([f"o{_g // 2}"] if _g % 2 else [])
    if _g in FFN_AT:
        L1_USES += [f"gate{FFN_AT[_g]}", f"up{FFN_AT[_g]}"]
L1_USES += ["attnT", "fin", "finT"]
L1_N = len(L1_USES)


def program(nc, hidden, pack, w1_d, w2_d, ffn_d, xn_d, xs_d, ys_d, out):
    ctx = ExitStack()
    with ctx:
        def sb(name, shape, dt=F32):
            return ctx.enter_context(nc.sbuf_tensor(name, shape, dt))

        def bank(name):
            return ctx.enter_context(nc.psum_tensor(name, [P, 512], F32))

        def sem(name):
            return ctx.enter_context(nc.semaphore(name))

        pk = sb("pk", [P, PACK_W])

        def pc(name, rows=P):
            a, z = PACK[name]
            return pk[0:rows, a:z]

        w1 = sb("w1", [P, E, FF])
        w2 = sb("w2", [P, E, FC, H])
        ffn = sb("ffn", [P, 3, HID])
        identb = sb("identb", [P, P], BF16)
        selb = sb("selb", [3 * 2 * N, 2 * N, P], BF16)
        bandb = sb("bandb", [P, 3, RG, KW], BF16)
        belowb = sb("belowb", [P, P], BF16)
        onesb = sb("onesb", [P, P], BF16)
        neg_a = sb("neg_a", [P, NH, N])
        exp_a = sb("exp_a", [P, NH * N])
        diag_d = sb("diag_d", [P, NH, P])
        gate_row = sb("gate_row", [P, E])
        bq_s = sb("bq_s", [P, 1])
        half_c = sb("half_c", [P, NH * (KC + 1)])
        minus_half = sb("minus_half", [P, 16])
        one = sb("one", [P, 1])
        tick = sb("tick", [P, 1])

        x_in = sb("x_in", [P, NT, H])
        x_res = sb("x_res", [P, NT, H])
        tick_p = sb("tick_p", [P, 1])
        stats = sb("stats", [P, 2 * NT, 6])
        mv = sb("mv", [P, 2 * NT, 2])
        var_e = sb("var_e", [P, 2 * NT])
        rstd = sb("rstd", [P, 2 * NT])
        xnT = sb("xnT", [P, L])
        hs = sb("hs", [P, NH, L + KC])
        u = sb("u", [P, NH, L])
        sg = sb("sg", [P, NH, L])
        xsq = sb("xsq", [P, NT, XW])
        ss = sb("ss", [P, NT, 3])
        ms = sb("ms", [P, NT, 3])
        rr = sb("rr", [P, NT, 3])
        xdr = sb("xdr", [P, NT, XW])
        xdn = sb("xdn", [P, NT, XW])
        bc3 = sb("bc3", [P, NT, 3, 2 * N], BF16)
        bc_r1 = sb("bc_r1", [P, NT, 2 * N])
        bc_r2 = sb("bc_r2", [P, NT, 2 * N])
        dtT = sb("dtT", [R, L])
        bcT = sb("bcT", [3 * 2 * N, L], BF16)
        drl = sb("drl", [P, NH, L])
        dc = sb("dc", [P, NH, L])
        dt = sb("dt", [P, NH, L])
        dtu = sb("dtu", [P, NH, L])
        dA = [sb(f"dA{k}", [P, NH, L]) for k in range(2)]
        dBu = sb("dBu", [P, NH, L])
        hst = [sb(f"hst{k}", [P, NH, L]) for k in range(2)]
        cb = [sb(f"cb{k}", [P, L]) for k in range(2)]
        hc = [sb(f"hc{k}", [P, NH, L]) for k in range(2)]
        logits = dBu[:, 0, 0:TT * E].rearrange("p (t e) -> p t e", e=E)
        leq = dBu[:, 0, TT * E:2 * TT * E].rearrange("p (t e) -> p t e", e=E)
        lcand = dBu[:, 1, 0:TT * E].rearrange("p (t e) -> p t e", e=E)
        lmax = sb("lmax", [P, TT])
        onehot = sb("onehot", [P, TT, E], BF16)
        ones_t = sb("ones_t", [P, TT * E])
        tot = dA[0][:, 0, 0:TT * E].rearrange("p (e t) -> p e t", e=E)
        upto = dA[0][:, 1, 0:TT * E].rearrange("p (e t) -> p e t", e=E)
        slot_e = dA[1][:, 0, 0:TT * E].rearrange("p (e t) -> p e t", e=E)
        tile_cmp = dA[1][:, 1, 0:NM * E].rearrange("p (t e) -> p t e", e=E)
        cnt = sb("cnt", [P, E])
        cnt_i = sb("cnt_i", [P, E], I32)
        padded = sb("padded", [P, E])
        pad_end = sb("pad_end", [P, E])
        off = sb("off", [P, E])
        slot_f = sb("slot_f", [P, TT])
        slot_u = sb("slot_u", [P, TT], U32)
        slot_b = sb("slot_b", [P, NT], U32)
        tile_f = sb("tile_f", [P, NM])
        tile_e = sb("tile_e", [P, NM], I32)
        xa = [hst[k][:, 0, :].rearrange("p (j d) -> p j d", d=H) for k in range(2)]
        xna = [hc[k][:, 0, :].rearrange("p (j d) -> p j d", d=H) for k in range(2)]
        xaT = [dtu[:, k, :] for k in range(2)]
        xg = [hc[0][:, k, :].rearrange("p (j d) -> p j d", d=H) for k in range(2)]
        xgT = hc[1][:, 0, :]
        h_sb = [hst[0][:, k, :] for k in range(2)]
        h_T = [hst[1][:, k, :] for k in range(2)]
        xall = [x[:].rearrange("p h (j d) -> p (h j) d", d=H) for x in hst + hc]
        ys = [dt[:, k, :].rearrange("p (j d) -> p j d", d=H) for k in range(2)]
        z, th, tg = hst, hc[0], hc[1]
        dab, de, dw, dln = z[0], z[1], th, tg
        yg = dtu
        outT = dc[:, 0, :]

        x1r = sb("x1r", [P, NT, H])
        stats1 = sb("stats1", [P, NT, 6])
        mv1 = sb("mv1", [P, NT, 2])
        var1 = sb("var1", [P, NT])
        rstd1 = sb("rstd1", [P, NT])
        xn1 = sb("xn1", [P, NT, H])
        xn1T = sb("xn1T", [P, L + 2 * WIN])
        qT = sb("qT", [P, L])
        qbd = sb("qbd", [P, G, RG, GQ])
        kT = sb("kT", [P, RG, L + 2 * WIN])
        vw = sb("vw", [KW, G, RG, HD * 4 + 1])
        nmax = sb("nmax", [P, G, RG])
        pexp = [sb(f"pexp{k}", [P, RG, KW]) for k in range(2)]
        pT = [sb(f"pT{k}", [KW, RG * P]) for k in range(2)]
        rden = sb("rden", [P, 2, RG])
        attn = sb("attn", [GQ, G, RG, 4, HD])
        fth = sb("fth", [P, L])
        fsg = sb("fsg", [P, L])
        fh = sb("fh", [P, HC, L])
        ffn_i = fh[:, :, 0:HID].bitcast(I32)
        attnT, finT = fsg, fth
        y_out = sb("y_out", [P, NT, H])

        work = [bank("work0"), bank("work1")]
        work1 = bank("work1_l1")
        b_bank = bank("b_bank")
        c_bank = bank("c_bank")
        y_bank = [bank("y_bank0"), bank("y_bank1")]
        more = bank("more")

        gates2d = more[:, 0:TT * E]
        gates_bank = gates2d.rearrange("p (t e) -> p t e", e=E)
        rank2d, tot_bank = y_bank[0][:, 0:TT * E], y_bank[1][:, 0:TT * E]
        rank_bank = rank2d
        h_bank, t_bank, y_moe = [b_bank, c_bank], y_bank, more[:]

        s_pack, s_w1, s_w2, s_ffn = sem("pack_in"), sem("w1_in"), sem("w2_in"), sem("ffn_in")
        s_const = sem("const_ready")
        s_constp = sem("constp_ready")
        s_expa = sem("expa_ready")
        s_xin, s_xres, s_out = sem("x_in_landed"), sem("x_res_landed"), sem("out_stored")
        s_full0 = sem("work_full")
        s_free0 = [sem("work0_free"), sem("work1_free")]
        s_full1 = sem("work_l1_full")
        s_free1 = sem("work_l1_free")
        s_xa = [sem("xa0_in"), sem("xa1_in")]
        s_xast = [sem("xn0_stored"), sem("xn1_stored")]
        s_astat, s_arstd, s_axn = sem("a_stats"), sem("a_rstd"), sem("a_xn_ready")
        s_axT, s_axTc, s_agate = sem("a_xT_full"), sem("a_xT_copied"), sem("a_gates_done")
        s_route = sem("route_steps")
        s_count = sem("counts_full")
        s_xall = sem("xn_all_in")
        s_zero = sem("slots_zeroed")
        s_scat = sem("tokens_scattered")
        s_xg = [sem("xg0_in"), sem("xg1_in")]
        s_xgT, s_xgTc = sem("xgT_full"), sem("xgT_copied")
        s_mh, s_mhc = sem("expert_h_full"), sem("expert_h_copied")
        s_mt, s_mr = sem("expert_hT_full"), sem("expert_relu_ready")
        s_mdn, s_myc = sem("expert_y_full"), sem("expert_y_ready")
        s_yst = [sem("ys0_stored"), sem("ys1_stored")]
        s_slot = sem("slots_of_sequence")
        s_moe = sem("expert_rows_in")
        s_stat = sem("stats_ready")
        s_rstd = sem("rstd_ready")
        s_xn = sem("xn_ready")
        s_xnT = sem("xnT_ready")
        s_conv = sem("conv_steps")
        s_th = sem("tanh_ready")
        s_u = sem("u_ready")
        s_tg = sem("gate_tanh_ready")
        s_sg = sem("gate_silu_ready")
        s_xsq = sem("xsq_ready")
        s_ss = sem("ss_ready")
        s_rr = sem("rr_ready")
        s_xdr = sem("xdr_ready")
        s_bc3 = sem("bc_steps")
        s_dtT = sem("dtT_ready")
        s_bcT = sem("bcT_ready")
        s_dab = sem("dt_abs_ready")
        s_de = sem("dt_exp_ready")
        s_drl = sem("dt_relu_ready")
        s_dw = sem("dt_w_ready")
        s_dc = sem("dt_c_ready")
        s_dln = sem("dt_ln_ready")
        s_dt = sem("dt_ready")
        s_dtu = sem("dtu_ready")
        s_bb, s_cc = sem("b_bank_full"), sem("c_bank_full")
        s_dA, s_dBu, s_h, s_cb, s_hc = sem("dA_ready"), sem("dBu_ready"), sem("h_ready"), sem("cb_ready"), sem("hc_ready")
        s_ys = sem("y_summed")
        s_yg = sem("yg_ready")
        s_outT = sem("outT_ready")
        s_x1c = sem("x1_copied")
        s_stat1, s_rstd1, s_xn1 = sem("stats1_ready"), sem("rstd1_ready"), sem("xn1_ready")
        s_xn1T, s_q, s_qbd, s_k, s_v = sem("xn1T_ready"), sem("q_ready"), sem("qbd_ready"), sem("k_ready"), sem("v_ready")
        s_nmax, s_pexp, s_pT = sem("nmax_ready"), sem("pexp_ready"), sem("pT_ready")
        s_pv = sem("pv_done")
        s_rden, s_attn, s_attnT = sem("rden_ready"), sem("attn_ready"), sem("attnT_ready")
        s_fth, s_fsg, s_fh = sem("ffn_tanh_ready"), sem("ffn_silu_ready"), sem("ffn_h_ready")
        
        block = ctx.enter_context(nc.Block())

        def seq(dram, b):
            if isinstance(b, int):
                return dram[b, :, :].rearrange("(j p) d -> p j d", p=P)
            return dram[bass.ds(b, 1), :, :].rearrange("o (j p) d -> p (o j) d", p=P)

        def tiles(dram, i):
            if isinstance(i, int):
                return dram[i, :, :, :].rearrange("j p d -> p j d")
            return dram[bass.ds(i, 1), :, :, :].rearrange("o j p d -> p (o j) d")

        def w0(key):
            return work[L0_USES.index(key) % 2]

        def full0(eng, b, key):
            eng.wait_ge(s_full0, b * L0_N + L0_USES.index(key) + 1)

        def free0(key):
            return s_free0[L0_USES.index(key) % 2]

        def take0(eng, b, key):
            k = L0_USES.index(key)
            n = b * (L0_N // 2) + k // 2
            if isinstance(b, int) and n <= 0:
                return
            eng.wait_ge(s_free0[k % 2], n)

        def done0(eng, b, key):
            k = L0_USES.index(key)
            eng.wait_ge(s_free0[k % 2], b * (L0_N // 2) + k // 2 + 1)

        def full1(eng, b, key):
            eng.wait_ge(s_full1, b * L1_N + L1_USES.index(key) + 1)

        def take1(eng, b, key):
            n = b * L1_N + L1_USES.index(key)
            if isinstance(b, int) and n <= 0:
                return
            eng.wait_ge(s_free1, n)

        def before(eng, s, n):
            if isinstance(n, int) and n <= 0:
                return
            eng.wait_ge(s, n)

        def layer0_done(eng, b):
            before(eng, s_free0[0], b * (L0_N // 2))
            before(eng, s_free0[1], b * (L0_N // 2))

        def layer1_done(eng, b):
            before(eng, s_free1, b * L1_N)

        def sequences(eng, body):
            body(0, None)
            body(1, 0)
            with eng.Fori(2, B) as b:
                body(b, b - 1)
            body(None, B - 1)

        @block.sync
        def _(sp):
            sp.dma_start(pk[:], pack).then_inc(s_pack, 16)

            def first_pass(i, first):
                for k in range(2):
                    if not first:
                        sp.wait_ge(s_axn, (2 * i + k - 1) * NT)
                    sp.dma_start(xa[k], seq(hidden, 2 * i + k)).then_inc(s_xa[k], 16)
                for k in range(2):
                    sp.wait_ge(s_axn, (2 * i + k + 1) * NT)
                    sp.dma_start(seq(xn_d, 2 * i + k), xna[k]).then_inc(s_xast[k], 16)
            first_pass(0, True)
            sp.dma_start(w1[:], w1_d).then_inc(s_w1, 16)
            sp.dma_start(w2[:], w2_d).then_inc(s_w2, 16)
            sp.dma_start(ffn_i, ffn_d).then_inc(s_ffn, 16)
            with sp.Fori(1, B // 2) as i:
                first_pass(i, False)

            sp.wait_ge(s_scat, 16 * TT)
            for k in range(2):
                sp.dma_start(xg[k], tiles(xs_d, k)).then_inc(s_xg[k], 16)

            def rounds(i, last):
                for k in range(2):
                    if not last:
                        sp.wait_ge(s_xgT, 2 * i + k + 1)
                        sp.dma_start(xg[k], tiles(xs_d, 2 * i + k + 2)).then_inc(s_xg[k], 16)
                    sp.wait_ge(s_myc, (2 * i + k + 1) * MG)
                    sp.dma_start(tiles(ys_d, 2 * i + k), ys[k]).then_inc(s_yst[k], 16)
            with sp.Fori(0, NM // MG // 2 - 1) as i:
                rounds(i, False)
            rounds(NM // MG // 2 - 1, True)

            def body(b0, b1):
                if b0 is not None:
                    before(sp, s_full0, (b0 - 1) * L0_N + 1)
                    if isinstance(b0, int) and b0 == 0:
                        sp.wait_ge(s_xast[0], 16 * B // 2)
                        sp.wait_ge(s_xast[1], 16 * B // 2)
                    sp.dma_start(x_in[:], seq(xn_d, b0)).then_inc(s_xin, 16)
                    before(sp, s_x1c, b0)
                    sp.dma_start(x_res[:], seq(hidden, b0)).then_inc(s_xres, 16)
                if b1 is not None:
                    layer1_done(sp, b1 + 1)
                    sp.dma_start(seq(out, b1), y_out[:]).then_inc(s_out, 16)
            sequences(sp, body)
            sp.wait_ge(s_out, 16 * B)

        @block.vector
        def _(dve):
            v = nc.vector
            v.memset(minus_half[:], -0.5).then_inc(s_const, 1)
            v.memset(one[:], 1.0).then_inc(s_const, 1)
            v.memset(hs[:], 0.0).then_inc(s_const, 1)
            v.memset(xn1T[:], 0.0).then_inc(s_const, 1)
            v.memset(kT[:], 0.0).then_inc(s_const, 1)
            v.memset(vw[:], 1.0).then_inc(s_const, 1)
            dve.wait_ge(s_pack, 16)
            a = PACK["conv_w"][0]
            v.tensor_scalar(half_c[:], pk[:, a:a + NH * (KC + 1)], 0.5, None, ALU.mult).then_inc(s_const, 1)
            a = PACK["in_proj"][0]
            v.tensor_scalar(pk[:, a + I:a + 2 * I], pk[:, a + I:a + 2 * I], 0.5, None, ALU.mult).then_inc(s_const, 1)
            v.tensor_copy(identb[:], pc("ident")).then_inc(s_const, 1)
            v.tensor_copy(selb[:], pc("sel", 96).unsqueeze(2).to_broadcast([96, 2 * N, P])).then_inc(s_const, 1)
            v.tensor_copy(bandb[:], pc("band").rearrange("p (v k) -> p v k", v=3).unsqueeze(2)
                          .to_broadcast([P, 3, RG, KW])).then_inc(s_const, 1)
            v.tensor_copy(belowb[:], pc("below")).then_inc(s_const, 1)
            v.memset(onesb[:], 1.0).then_inc(s_const, 1)
            v.memset(ones_t[:], 1.0).then_inc(s_const, 1)
            for h in range(NH):
                v.tensor_scalar(diag_d[:, h, :], pc("ident"), pc("d")[:, h:h + 1], None, ALU.mult).then_inc(s_const, 1)
            v.tensor_tensor(gate_row[:], pc("gate_b"), pc("expert_b"), ALU.add).then_inc(s_const, 1)
            v.tensor_scalar(bq_s[:], pc("bq"), float(HD) ** -0.5, None, ALU.mult).then_inc(s_const, 1)
            dve.wait_ge(s_expa, 1)
            v.tensor_scalar(neg_a[:], exp_a[:].rearrange("p (h n) -> p h n", h=NH), -1.0, None, ALU.mult).then_inc(s_const, 1)
            dve.wait_ge(s_const, 19)

            def first_pass(i, first):
                for k in range(2):
                    dve.wait_ge(s_xa[k], 16 * i + 16)
                    for j in range(NT):
                        v.bn_stats(stats[:, k * NT + j, :], xa[k][:, j, :]).then_inc(s_astat, 1)
                    dve.wait_ge(s_astat, i * 18 + k * 9 + 4)
                    v.memset(tick[:], 0.0)
                    for j in range(NT):
                        v.bn_aggr(mv[:, k * NT + j, :], stats[:, k * NT + j, :]).then_inc(s_astat, 1)
                    dve.wait_ge(s_astat, i * 18 + k * 9 + 8)
                    v.tensor_scalar(var_e[:, k * NT:k * NT + NT], mv[:, k * NT:k * NT + NT, 1], LN_EPS, None,
                                    ALU.add).then_inc(s_astat, 1)
                for k in range(2):
                    dve.wait_ge(s_arstd, 2 * i + k + 1)
                    if not first:
                        dve.wait_ge(s_xast[k], 16 * i)
                        dve.wait_ge(s_axT, 2 * i + k - 1)
                    for j in range(NT):
                        n = k * NT + j
                        v.tensor_scalar(xna[k][:, j, :], xa[k][:, j, :], mv[:, n, 0:1], rstd[:, n:n + 1],
                                        ALU.subtract, ALU.mult).then_inc(s_axn, 1)
            first_pass(0, True)
            with dve.Fori(1, B // 2) as i:
                first_pass(i, False)

            step = [0]

            def routed(ins):
                step[0] += 1
                ins.then_inc(s_route, 1)
                dve.wait_ge(s_route, step[0])
            dve.wait_ge(s_agate, B)
            dve.wait_ge(s_zero, 16)
            routed(v.tensor_tensor(logits, gates_bank, gate_row[:].unsqueeze(1).to_broadcast([P, TT, E]), ALU.add))
            routed(v.tensor_reduce(lmax[:], logits, AX_X, ALU.max))
            routed(v.tensor_tensor(leq, logits, lmax[:].unsqueeze(2).to_broadcast([P, TT, E]), ALU.is_equal))
            routed(v.scalar_tensor_tensor(lcand, leq, -100.0, pc("expert_no").unsqueeze(1).to_broadcast([P, TT, E]),
                                          ALU.mult, ALU.add))
            routed(v.tensor_reduce(lmax[:], lcand, AX_X, ALU.min))
            routed(v.tensor_tensor(onehot[:], lcand, lmax[:].unsqueeze(2).to_broadcast([P, TT, E]), ALU.is_equal))
            dve.wait_ge(s_count, 1)
            routed(v.tensor_copy(tot, tot_bank.rearrange("p (t e) -> p e t", e=E)))
            routed(v.tensor_tensor_scan(upto.rearrange("p e t -> p (e t)"), ones_t[:],
                                        tot.rearrange("p e t -> p (e t)"), 0.0, ALU.mult, ALU.add))
            routed(v.tensor_reduce(cnt[:], tot, AX_X, ALU.add))
            routed(v.tensor_scalar(cnt_i[:], cnt[:], float(P - 1), None, ALU.add))
            routed(v.tensor_scalar(cnt_i[:], cnt_i[:], 7, 7, ALU.arith_shift_right, ALU.arith_shift_left))
            routed(v.tensor_copy(padded[:], cnt_i[:]))
            routed(v.tensor_tensor_scan(pad_end[:], ones_t[:, 0:E], padded[:], 0.0, ALU.mult, ALU.add))
            routed(v.tensor_tensor(off[:], pad_end[:], padded[:], ALU.subtract))
            routed(v.tensor_tensor(off[:], off[:], upto[:, :, TT - 1], ALU.subtract))
            routed(v.tensor_tensor(off[:], off[:], cnt[:], ALU.add))
            routed(v.tensor_tensor(upto, upto, tot, ALU.subtract))
            routed(v.tensor_tensor(slot_e, upto, rank_bank.rearrange("p (t e) -> p e t", e=E), ALU.add))
            routed(v.tensor_tensor(slot_e, slot_e, off[:].unsqueeze(2).to_broadcast([P, E, TT]), ALU.add))
            routed(v.tensor_tensor(slot_e, slot_e, onehot[:].rearrange("p t e -> p e t"), ALU.mult))
            routed(v.tensor_reduce(slot_f[:], slot_e.rearrange("p e t -> p t e"), AX_X, ALU.add))
            routed(v.tensor_copy(slot_u[:], slot_f[:]))
            slots_at = step[0]
            routed(v.tensor_tensor(tile_cmp, pad_end[:].unsqueeze(1).to_broadcast([P, NM, E]),
                                   pc("tile_at").unsqueeze(2).to_broadcast([P, NM, E]), ALU.is_le))
            routed(v.tensor_reduce(tile_f[:], tile_cmp, AX_X, ALU.add))
            routed(v.tensor_scalar(tile_e[:], tile_f[:], float(E - 1), None, ALU.min))
            assert (slots_at, step[0]) == (ROUTE_SLOTS, ROUTE_TILES)

            def rounds(i, first):
                for k in range(2):
                    m = 2 * i + k
                    for j in range(MG):
                        dve.wait_ge(s_mh, m * MG + j + 1)
                        if not (first and k == 0 and j < 2):
                            dve.wait_ge(s_mt, m * MG + j - 1)
                        v.tensor_copy(h_sb[j % 2], h_bank[j % 2][:]).then_inc(s_mhc, 1)
                    dve.wait_ge(s_mdn, (m + 1) * MG)
                    if not first:
                        dve.wait_ge(s_yst[k], 16 * i)
                    for j in range(MG):
                        e = dve.value_load(tile_e[0:1, bass.ds(m * MG + j, 1)], min_val=0, max_val=E - 1)
                        v.tensor_tensor(ys[k][:, j, :], y_moe[:, j * H:(j + 1) * H],
                                        pc("b2").rearrange("p (e d) -> p e d", e=E)[:, bass.ds(e, 1), :]
                                        .rearrange("p o d -> p (o d)"), ALU.add).then_inc(s_myc, 1)
            rounds(0, True)
            with dve.Fori(1, NM // MG // 2) as i:
                rounds(i, False)
            dve.wait_ge(s_myc, NM)
            for k in range(2):
                v.memset(dA[k][:], 0.0).then_inc(s_const, 1)
            dve.wait_ge(s_ffn, 16)
            v.tensor_scalar(ffn[:], ffn_i, 1.0 / 127.0, None, ALU.mult).then_inc(s_const, 1)
            dve.wait_ge(s_const, 22)
            v.tensor_scalar(ffn[:, 0, :], ffn[:, 0, :], 0.5, None, ALU.mult).then_inc(s_const, 1)

            def norm(b, src, stats, mv, var_e, rstd, xn, s_stat, s_rstd, s_xn):
                for j in range(NT):
                    v.bn_stats(stats[:, j, :], src[:, j, :]).then_inc(s_stat, 1)
                dve.wait_ge(s_stat, b * 9 + 4)
                v.memset(tick[:], 0.0)
                for j in range(NT):
                    v.bn_aggr(mv[:, j, :], stats[:, j, :]).then_inc(s_stat, 1)
                dve.wait_ge(s_stat, b * 9 + 8)
                v.tensor_scalar(var_e[:], mv[:, :, 1], LN_EPS, None, ALU.add).then_inc(s_stat, 1)
                dve.wait_ge(s_rstd, b + 1)
                for j in range(NT):
                    v.tensor_scalar(xn[:, j, :], src[:, j, :], mv[:, j, 0:1], rstd[:, j:j + 1],
                                    ALU.subtract, ALU.mult).then_inc(s_xn, 1)

            def pre0(b):
                layer0_done(dve, b)
                before(dve, s_moe, b * 16 * NT)
                v.tensor_tensor(slot_b[:], slot_f[:, 4 * b:4 * b + 4] if isinstance(b, int) else
                                slot_f[:, bass.ds(b * 4, 4)],
                                one[:].to_broadcast([P, NT]), ALU.mult).then_inc(s_slot, 1)
                for k in range(KC):
                    for h in range(NH):
                        src = hs[:, h, k:k + L]
                        w = half_c[:, h * KC + k:h * KC + k + 1]
                        if k == 0:
                            done0(dve, b, f"hs{h}")
                            v.tensor_scalar(z[0][:, h, :], src, w, half_c[:, NH * KC + h:NH * KC + h + 1],
                                            ALU.mult, ALU.add).then_inc(s_conv, 1)
                        else:
                            dve.wait_ge(s_conv, b * NH * KC + (k - 1) * NH + h + 1)
                            v.scalar_tensor_tensor(z[k % 2][:, h, :], src, w, z[(k - 1) % 2][:, h, :],
                                                   ALU.mult, ALU.add).then_inc(s_conv, 1)
                for h in range(NH):
                    dve.wait_ge(s_th, b * NH + h + 1)
                    v.scalar_tensor_tensor(u[:, h, :], th[:, h, :], 1.0, z[1][:, h, :],
                                           ALU.add, ALU.mult).then_inc(s_u, 1)
                for h in range(NH):
                    dve.wait_ge(s_tg, b * NH + h + 1)
                    v.scalar_tensor_tensor(sg[:, h, :], tg[:, h, :], 1.0, w0(f"zg{h}")[:],
                                           ALU.add, ALU.mult).then_inc(free0(f"zg{h}"), 1)
                dve.wait_ge(s_xsq, b + 1)
                for k, (a, w) in enumerate(((0, R), (R, N), (R + N, N))):
                    v.tensor_reduce(ss[:, :, k], xsq[:, :, a:a + w], AX_X, ALU.add).then_inc(s_ss, 1)
                dve.wait_ge(s_ss, b * 5 + 3)
                v.tensor_tensor(ms[:], ss[:], pc("rms_n").unsqueeze(1).to_broadcast([P, NT, 3]),
                                ALU.mult).then_inc(s_ss, 1)
                dve.wait_ge(s_ss, b * 5 + 4)
                v.tensor_scalar(ms[:], ms[:], RMS_EPS, None, ALU.add).then_inc(s_ss, 1)
                dve.wait_ge(s_rr, b + 1)
                xd = w0("xdbl")[:, 0:NT * XW].rearrange("p (j c) -> p j c", c=XW)
                for k, (a, w) in enumerate(((0, R), (R, N), (R + N, N))):
                    last = v.tensor_tensor(xdr[:, :, a:a + w], xd[:, :, a:a + w],
                                           rr[:, :, k:k + 1].to_broadcast([P, NT, w]), ALU.mult)
                    last.then_inc(free0("xdbl") if k == 2 else s_xdr, 1)
                for h in range(NH):
                    dve.wait_ge(s_dab, b * NH + h + 1)
                    v.tensor_scalar(drl[:, h, :], w0(f"dtp{h}")[:], pc("dt_b")[:, h:h + 1], 0.0,
                                    ALU.add, ALU.max).then_inc(free0(f"dtp{h}"), 1)
                dve.wait_ge(s_de, b + 1)
                v.tensor_scalar(dw[:], de[:], 1.0, None, ALU.add).then_inc(s_dw, 1)
                dve.wait_ge(s_dw, b + 1)
                v.scalar_tensor_tensor(dc[:], dw[:], -1.0, de[:], ALU.add, ALU.subtract).then_inc(s_dc, 1)
                dve.wait_ge(s_dc, b * 2 + 1)
                dve.wait_ge(s_dln, b + 1)
                v.tensor_tensor(dc[:], dln[:], dc[:], ALU.subtract).then_inc(s_dc, 1)
                dve.wait_ge(s_dc, b * 2 + 2)
                done0(dve, b, "dtp0")
                done0(dve, b, "dtp1")
                v.tensor_tensor(dt[:], dc[:], drl[:], ALU.add).then_inc(s_dt, 1)
                dve.wait_ge(s_dt, b + 1)
                dve.wait_ge(s_u, b * NH + NH)
                v.tensor_tensor(dtu[:], dt[:], u[:], ALU.mult).then_inc(s_dtu, 1)

            def pre1(b):
                layer1_done(dve, b)
                dve.wait_ge(s_x1c, b + 1)
                norm(b, x1r, stats1, mv1, var1, rstd1, xn1, s_stat1, s_rstd1, s_xn1)

            def scan_in(b, n):
                if n == 0:
                    dve.wait_ge(s_dtu, b + 1)
                dve.wait_ge(s_bb, b * N + n + 1)
                before(dve, s_h, b * N + n)
                v.tensor_tensor(dBu[:], dtu[:], b_bank[:].unsqueeze(1).to_broadcast([P, NH, L]),
                                ALU.mult).then_inc(s_dBu, 1)

            def scan(b, n):
                dve.wait_ge(s_dBu, b * N + n + 1)
                dve.wait_ge(s_dA, (b * N + n + 1) * NH)
                before(dve, s_hc, b * N + n - 1)
                v.tensor_tensor_scan(hst[n % 2][:].rearrange("p h t -> p (h t)"),
                                     dA[n % 2][:].rearrange("p h t -> p (h t)"),
                                     dBu[:].rearrange("p h t -> p (h t)"), 0.0,
                                     ALU.mult, ALU.add).then_inc(s_h, 1)

            def row_max(b, g):
                full1(dve, b, f"s{g}")
                v.tensor_reduce(nmax[:, g, :], work1[:, 0:RG * KW].rearrange("p (r k) -> p r k", r=RG), AX_X,
                                ALU.max, negate=True).then_inc(s_nmax, 1)

            def heads_out(b, g):
                full1(dve, b, f"o{g // 2}")
                o = work1[:, 0:2 * RG * 33].rearrange("p (c r d) -> p c r d", c=2, r=RG)
                v.reciprocal(rden[:], o[:, :, :, 32]).then_inc(s_rden, 1)
                dve.wait_ge(s_rden, b * (G // 2) + g // 2 + 1)
                for k in range(4):
                    q = slice(32 * k, 32 * k + 32)
                    last = v.tensor_tensor(attn[:, g - 1:g + 1, :, k, :], o[q, :, :, HD * k:HD * k + HD],
                                           rden[q, :, :].unsqueeze(3).to_broadcast([32, 2, RG, HD]), ALU.mult)
                    last.then_inc(s_free1 if k == 3 else s_attn, 1)

            def ffn_chunk(b, c):
                dve.wait_ge(s_fth, b * HC + c + 1)
                v.scalar_tensor_tensor(fsg[:], fth[:], 1.0, work1[:], ALU.add, ALU.mult).then_inc(s_free1, 1)
                full1(dve, b, f"up{c}")
                dve.wait_ge(s_free1, b * L1_N + L1_USES.index(f"up{c}"))
                v.tensor_tensor(fh[:, c, :], fsg[:], work1[:], ALU.mult).then_inc(s_free1, 1)

            def post0(b):
                dve.wait_ge(s_ys, b * (N + 1) + N + 1)
                for h in range(NH):
                    v.tensor_tensor(yg[:, h, :], y_bank[h][:], sg[:, h, :], ALU.mult).then_inc(s_yg, 1)
                full0(dve, b, "outT")
                dve.wait_ge(s_moe, b * 16 * NT + 16 * NT)
                before(dve, s_x1c, b)
                v.tensor_tensor(x_res[:], x_res[:], w0("outT")[:].rearrange("p (j d) -> p j d", j=NT),
                                ALU.add).then_inc(free0("outT"), 1)

            def post1(b):
                full1(dve, b, "finT")
                before(dve, s_out, b * 16)
                v.tensor_tensor(y_out[:], x1r[:], work1[:].rearrange("p (j d) -> p j d", j=NT),
                                ALU.add).then_inc(s_free1, 1)

            def body(b0, b1):
                if b0 is not None:
                    pre0(b0)
                if b1 is not None:
                    pre1(b1)
                for n in range(N):
                    if b0 is not None:
                        scan_in(b0, n)
                    if b1 is not None:
                        row_max(b1, n)
                    if b0 is not None:
                        scan(b0, n)
                    if b1 is not None and n % 2:
                        heads_out(b1, n)
                    if b1 is not None and n in FFN_AT:
                        ffn_chunk(b1, FFN_AT[n])
                if b0 is not None:
                    post0(b0)
                if b1 is not None:
                    post1(b1)
            sequences(dve, body)

        @block.scalar
        def _(act):
            s = nc.scalar
            act.wait_ge(s_pack, 16)
            s.activation(exp_a[:], pc("a_log"), ACT.Exp).then_inc(s_expa, 1)
            act.wait_ge(s_const, 19)

            def first_pass(i, first):
                for k in range(2):
                    act.wait_ge(s_axT, 2 * i + k + 1)
                    if not first:
                        act.wait_ge(s_agate, 2 * i + k - 1)
                    s.activation(xaT[k], work[k][:], ACT.Copy).then_inc(s_axTc, 1)
            first_pass(0, True)
            with act.Fori(1, B // 2) as i:
                first_pass(i, False)

            def rounds(i, first):
                for k in range(2):
                    m = 2 * i + k
                    act.wait_ge(s_xgT, m + 1)
                    if not (first and k == 0):
                        act.wait_ge(s_mh, m * MG)
                    s.activation(xgT, work1[:], ACT.Copy).then_inc(s_xgTc, 1)
                    for j in range(MG):
                        e = act.value_load(tile_e[0:1, bass.ds(m * MG + j, 1)], min_val=0, max_val=E - 1)
                        act.wait_ge(s_mt, m * MG + j + 1)
                        if not (first and k == 0 and j < 2):
                            act.wait_ge(s_mdn, m * MG + j - 1)
                        for c in range(FC):
                            last = s.activation(h_T[j % 2][:, c * P:(c + 1) * P], t_bank[j % 2][:, c * P:(c + 1) * P],
                                                ACT.Relu, bias=pc("b1").rearrange("p (e c) -> p e c", c=FC)
                                                [:, bass.ds(e, 1), c:c + 1].rearrange("p o c -> p (o c)"))
                        last.then_inc(s_mr, 1)
            act.wait_ge(s_route, ROUTE_TILES)
            rounds(0, True)
            with act.Fori(1, NM // MG // 2) as i:
                rounds(i, False)
            act.wait_ge(s_const, 23)

            def pre0(b):
                layer0_done(act, b)
                full0(act, b, "xnT")
                s.copy(xnT[:], w0("xnT")[:]).then_inc(free0("xnT"), 1)
                for h in range(NH):
                    full0(act, b, f"hs{h}")
                    s.copy(hs[:, h, 1:1 + L], w0(f"hs{h}")[:]).then_inc(free0(f"hs{h}"), 1)
                for h in range(NH):
                    full0(act, b, f"zg{h}")
                    s.activation(tg[:, h, :], w0(f"zg{h}")[:], ACT.Tanh).then_inc(s_tg, 1)
                for h in range(NH):
                    act.wait_ge(s_conv, b * NH * KC + (KC - 1) * NH + h + 1)
                    s.activation(th[:, h, :], z[1][:, h, :], ACT.Tanh).then_inc(s_th, 1)
                full0(act, b, "xdbl")
                s.activation(xsq[:], w0("xdbl")[:, 0:NT * XW].rearrange("p (j c) -> p j c", c=XW),
                             ACT.Square).then_inc(s_xsq, 1)
                full0(act, b, "dtT")
                s.copy(dtT[:], w0("dtT")[0:R, :]).then_inc(free0("dtT"), 1)
                full0(act, b, "bcT")
                s.copy(bcT[:], w0("bcT")[0:96, :].bitcast(BF16)[:, 0:L]).then_inc(free0("bcT"), 1)
                for h in range(NH):
                    full0(act, b, f"dtp{h}")
                    s.activation(dab[:, h, :], w0(f"dtp{h}")[:], ACT.Abs, bias=pc("dt_b")[:, h:h + 1]).then_inc(s_dab, 1)
                act.wait_ge(s_dab, b * NH + NH)
                s.activation(de[:], dab[:], ACT.Exp, scale=-1.0).then_inc(s_de, 1)
                act.wait_ge(s_dw, b + 1)
                s.activation(dln[:], dw[:], ACT.Ln).then_inc(s_dln, 1)

            def pre1(b):
                layer1_done(act, b)
                full1(act, b, "xnT")
                s.copy(xn1T[:, WIN:WIN + L], work1[:]).then_inc(s_free1, 1)
                full1(act, b, "q")
                s.activation(qT[:], work1[:], ACT.Identity, bias=bq_s[:], scale=float(HD) ** -0.5).then_inc(s_free1, 1)
                full1(act, b, "k")
                for r in range(RG):
                    q = slice(32 * r, 32 * r + 32)
                    last = s.activation(kT[q, r, WIN:WIN + L], work1[q, :], ACT.Identity, bias=pc("bk")[q, :])
                last.then_inc(s_free1, 1)
                for j in range(4):
                    full1(act, b, f"v{j}")
                    s.copy(vw[:, 4 * j:4 * j + 4, :, 0:32],
                           work1[0:KW, :].rearrange("p (g r d) -> p g r d", g=4, r=RG)).then_inc(s_free1, 1)

            def c_copy(b, n):
                act.wait_ge(s_cc, b * N + n + 1)
                before(act, s_hc, b * N + n - 1)
                s.copy(cb[n % 2][:], c_bank[:]).then_inc(s_cb, 1)

            def decay(b, n):
                if n == 0:
                    act.wait_ge(s_dt, b + 1)
                before(act, s_h, b * N + n - 1)
                for h in range(NH):
                    s.activation(dA[n % 2][:, h, 1:L], dt[:, h, 1:L], ACT.Exp,
                                 scale=neg_a[:, h, n:n + 1]).then_inc(s_dA, 1)

            def softmax_exp(b, g):
                act.wait_ge(s_nmax, b * G + g + 1)
                before(act, s_full1, b * L1_N + L1_USES.index(f"pT{g - 2}") + 1 if g >= 2 else
                       (b - 1) * L1_N + L1_USES.index(f"pT{G - 2 + g}") + 1)
                for r in range(RG):
                    last = s.activation(pexp[g % 2][:, r, :], work1[:, r * KW:(r + 1) * KW], ACT.Exp,
                                        bias=nmax[:, g, r:r + 1])
                last.then_inc(s_free1, 1)

            def p_copy(b, g):
                full1(act, b, f"pT{g}")
                before(act, s_full1, b * L1_N + L1_USES.index(f"o{g // 2 - 1}") + 1 if g >= 2 else 0)
                s.copy(pT[g % 2][:], work1[0:KW, :]).then_inc(s_free1, 1)

            def ffn_tanh(b, c):
                full1(act, b, f"gate{c}")
                s.activation(fth[:], work1[:], ACT.Tanh).then_inc(s_fth, 1)

            def post0(b):
                full0(act, b, "out")
                s.copy(outT, w0("out")[:]).then_inc(free0("out"), 1)
                layer0_done(act, b + 1)
                layer1_done(act, b)
                s.copy(x1r[:], x_res[:]).then_inc(s_x1c, 1)

            def post1(b):
                full1(act, b, "attnT")
                s.activation(attnT[:], work1[:], ACT.Identity, bias=pc("bv")).then_inc(s_free1, 1)
                full1(act, b, "fin")
                s.activation(finT[:], work1[:], ACT.Identity, bias=pc("bo")).then_inc(s_free1, 1)

            def body(b0, b1):
                if b0 is not None:
                    pre0(b0)
                if b1 is not None:
                    pre1(b1)
                if b0 is not None:
                    decay(b0, 0)
                for n in range(N):
                    if b0 is not None:
                        c_copy(b0, n)
                        if n + 1 < N:
                            decay(b0, n + 1)
                    if b1 is not None:
                        softmax_exp(b1, n)
                        p_copy(b1, n)
                    if b1 is not None and n in FFN_AT:
                        ffn_tanh(b1, FFN_AT[n])
                if b1 is not None:
                    post1(b1)
                if b0 is not None:
                    post0(b0)
            sequences(act, body)

        @block.gpsimd
        def _(pool):
            g_ = nc.gpsimd
            g_.memset(dBu[:], 0.0).then_inc(s_constp, 1)
            pool.wait_ge(s_constp, 1)
            pool.dma_start(xs_d.rearrange("i j p d -> (i j p d)").rearrange("(q r n) -> q r n", q=P, n=L),
                           dBu[:, 0:1, :].to_broadcast([P, NM * H // L, L])).then_inc(s_zero, 16)
            pool.wait_ge(s_const, 19)

            def first_pass(i):
                for k in range(2):
                    pool.wait_ge(s_astat, i * 18 + k * 9 + 9)
                    g_.tensor_tensor(rstd[:, k * NT:k * NT + NT], var_e[:, k * NT:k * NT + NT],
                                     minus_half[:, 0:NT], ALU.pow).then_inc(s_arstd, 1)
            with pool.Fori(0, B // 2) as i:
                first_pass(i)
            pool.wait_ge(s_xast[0], 16 * B // 2)
            pool.wait_ge(s_xast[1], 16 * B // 2)
            pool.wait_ge(s_axT, B)
            for k in range(4):
                pool.dma_start(xall[k], xn_d[2 * k:2 * k + 2, :, :].rearrange("b (j p) d -> p (b j) d", p=P))                    .then_inc(s_xall, 16)
            pool.wait_ge(s_route, ROUTE_SLOTS)
            pool.wait_ge(s_xall, 16 * 4)
            for k in range(TT):
                g_.indirect_dma_start(xs_d.rearrange("i j p d -> (i j p) d"),
                                      bass.IndirectOffsetOnAxis(ap=slot_u[:, k:k + 1], axis=0),
                                      xall[k // 8][:, k % 8, :], None).then_inc(s_scat, 16)
            pool.wait_ge(s_yst[0], 16 * NM // MG // 2)
            pool.wait_ge(s_yst[1], 16 * NM // MG // 2)

            def pre0(b):
                layer0_done(pool, b)
                pool.wait_ge(s_xres, b * 16 + 16)
                pool.wait_ge(s_slot, b + 1)
                g_.tensor_tensor(tick_p[:], one[:], one[:], ALU.mult)
                for j in range(NT):
                    g_.indirect_dma_start(x_res[:, j, :], None, ys_d.rearrange("i j p d -> (i j p) d"),
                                          bass.IndirectOffsetOnAxis(ap=slot_b[:, j:j + 1], axis=0),
                                          compute_op=ALU.add).then_inc(s_moe, 16)
                pool.wait_ge(s_ss, b * 5 + 5)
                g_.tensor_tensor(rr[:].rearrange("p j k -> p (j k)"), ms[:].rearrange("p j k -> p (j k)"),
                                 minus_half[:, 0:NT * 3], ALU.pow).then_inc(s_rr, 1)
                done0(pool, b, "xdbl")
                g_.tensor_tensor(xdn[:], xdr[:], pc("ln_row").unsqueeze(1).to_broadcast([P, NT, XW]),
                                 ALU.mult).then_inc(s_bc3, 1)
                bc = xdn[:, :, R:XW]
                ones = one[:].unsqueeze(1).to_broadcast([P, NT, 2 * N])
                pool.wait_ge(s_bc3, b * 6 + 1)
                g_.tensor_tensor(bc3[:, :, 0, :], bc, ones, ALU.mult).then_inc(s_bc3, 1)
                pool.wait_ge(s_bc3, b * 6 + 2)
                g_.tensor_tensor(bc_r1[:], bc, bc3[:, :, 0, :], ALU.subtract).then_inc(s_bc3, 1)
                pool.wait_ge(s_bc3, b * 6 + 3)
                g_.tensor_tensor(bc3[:, :, 1, :], bc_r1[:], ones, ALU.mult).then_inc(s_bc3, 1)
                pool.wait_ge(s_bc3, b * 6 + 4)
                g_.tensor_tensor(bc_r2[:], bc_r1[:], bc3[:, :, 1, :], ALU.subtract).then_inc(s_bc3, 1)
                pool.wait_ge(s_bc3, b * 6 + 5)
                g_.tensor_tensor(bc3[:, :, 2, :], bc_r2[:], ones, ALU.mult).then_inc(s_bc3, 1)

            def pre1(b):
                layer1_done(pool, b)
                pool.wait_ge(s_stat1, b * 9 + 9)
                g_.tensor_tensor(rstd1[:], var1[:], minus_half[:, 0:NT], ALU.pow).then_inc(s_rstd1, 1)
                pool.wait_ge(s_free1, b * L1_N + L1_USES.index("q") + 1)
                g_.tensor_tensor(qbd[:], qT[:].rearrange("p (g q) -> p g q", q=GQ).unsqueeze(2)
                                 .to_broadcast([P, G, RG, GQ]),
                                 pc("heads").unsqueeze(1).unsqueeze(3).to_broadcast([P, G, RG, GQ]),
                                 ALU.mult).then_inc(s_qbd, 1)

            def times_c(b, n):
                pool.wait_ge(s_h, b * N + n + 1)
                pool.wait_ge(s_cb, b * N + n + 1)
                before(pool, s_ys, b * (N + 1) + n)
                g_.tensor_tensor(hc[n % 2][:], hst[n % 2][:], cb[n % 2][:].unsqueeze(1).to_broadcast([P, NH, L]),
                                 ALU.mult).then_inc(s_hc, 1)

            def body(b0, b1):
                if b0 is not None:
                    pre0(b0)
                if b1 is not None:
                    pre1(b1)
                if b0 is not None:
                    for n in range(N):
                        times_c(b0, n)
            sequences(pool, body)

        @block.tensor
        def _(pe):
            t = nc.tensor
            ident = pc("ident")
            pe.wait_ge(s_const, 19)

            def first_pass(i, first):
                for k in range(2):
                    for j in range(NT):
                        pe.wait_ge(s_axn, (2 * i + k) * NT + j + 1)
                        if j == 0 and not first:
                            pe.wait_ge(s_axTc, 2 * i + k - 1)
                        last = t.transpose(work[k][:, j * P:(j + 1) * P], xna[k][:, j, :], ident)
                    last.then_inc(s_axT, 1)
                for k in range(2):
                    pe.wait_ge(s_axTc, 2 * i + k + 1)
                    for j in range(NT):
                        a = ((2 * i + k) * NT + j) * E
                        o = gates2d[:, a:a + E] if isinstance(i, int) else gates2d[:, bass.ds(a, E)]
                        last = t.matmul(o, xaT[k][:, j * P:(j + 1) * P], pc("gate_w"), start=True, stop=True)
                    last.then_inc(s_agate, 1)
            first_pass(0, True)
            with pe.Fori(1, B // 2) as i:
                first_pass(i, False)
            pe.wait_ge(s_route, 6)
            oh = onehot[:].rearrange("p t e -> p (t e)")
            t.matmul(rank2d, belowb[:], oh, start=True, stop=True)
            t.matmul(tot_bank, onesb[:], oh, start=True, stop=True).then_inc(s_count, 1)

            pe.wait_ge(s_w1, 16)
            pe.wait_ge(s_w2, 16)
            pe.wait_ge(s_route, ROUTE_TILES)

            def rounds(i, first):
                for k in range(2):
                    m = 2 * i + k
                    pe.wait_ge(s_xg[k], 16 * i + 16)
                    if not (first and k == 0):
                        pe.wait_ge(s_xgTc, m)
                    for j in range(MG):
                        last = t.transpose(work1[:, j * P:(j + 1) * P], xg[k][:, j, :], ident)
                    last.then_inc(s_xgT, 1)
                    es = [pe.value_load(tile_e[0:1, bass.ds(m * MG + j, 1)], min_val=0, max_val=E - 1)
                          for j in range(MG)]

                    def up(j):
                        if not (first and k == 0 and j < 2):
                            pe.wait_ge(s_mhc, m * MG + j - 1)
                        t.matmul(h_bank[j % 2][:], xgT[:, j * P:(j + 1) * P],
                                 w1[:, bass.ds(es[j], 1), :].rearrange("p o f -> p (o f)"),
                                 start=True, stop=True).then_inc(s_mh, 1)

                    def turn(j):
                        pe.wait_ge(s_mhc, m * MG + j + 1)
                        if not (first and k == 0 and j < 2):
                            pe.wait_ge(s_mr, m * MG + j - 1)
                        for c in range(FC):
                            last = t.transpose(t_bank[j % 2][:, c * P:(c + 1) * P],
                                               h_sb[j % 2][:, c * P:(c + 1) * P], ident)
                        last.then_inc(s_mt, 1)

                    def down(j):
                        pe.wait_ge(s_mr, m * MG + j + 1)
                        if j == 0 and not (first and k == 0):
                            pe.wait_ge(s_myc, m * MG)
                        for c in range(FC):
                            last = t.matmul(y_moe[:, j * H:(j + 1) * H], h_T[j % 2][:, c * P:(c + 1) * P],
                                            w2[:, bass.ds(es[j], 1), c, :].rearrange("p o d -> p (o d)"),
                                            start=(c == 0), stop=(c == FC - 1))
                        last.then_inc(s_mdn, 1)
                    pe.wait_ge(s_xgTc, m + 1)
                    up(0)
                    up(1)
                    turn(0)
                    up(2)
                    turn(1)
                    down(0)
                    up(3)
                    turn(2)
                    down(1)
                    turn(3)
                    down(2)
                    down(3)
            rounds(0, True)
            with pe.Fori(1, NM // MG // 2) as i:
                rounds(i, False)
            pe.wait_ge(s_const, 23)

            def pre0(b):
                take0(pe, b, "xnT")
                pe.wait_ge(s_xin, b * 16 + 16)
                for j in range(NT):
                    last = t.transpose(w0("xnT")[:, j * P:(j + 1) * P], x_in[:, j, :], ident)
                last.then_inc(s_full0, 1)
                done0(pe, b, "xnT")
                for k, key in enumerate(("hs0", "hs1", "zg0", "zg1")):
                    take0(pe, b, key)
                    t.matmul(w0(key)[:], pc("in_proj")[:, k * P:(k + 1) * P], xnT[:], start=True,
                             stop=True).then_inc(s_full0, 1)
                take0(pe, b, "xdbl")
                pe.wait_ge(s_u, b * NH + NH)
                for j in range(NT):
                    for h in range(NH):
                        last = t.matmul(w0("xdbl")[:, j * XW:(j + 1) * XW], u[:, h, j * P:(j + 1) * P],
                                        pc("x_proj")[:, h * XW:(h + 1) * XW], start=(h == 0), stop=(h == NH - 1))
                last.then_inc(s_full0, 1)
                take0(pe, b, "dtT")
                pe.wait_ge(s_bc3, b * 6 + 1)
                for j in range(NT):
                    last = t.transpose(w0("dtT")[0:XW, j * P:(j + 1) * P], xdn[:, j, :], ident)
                last.then_inc(s_full0, 1)
                take0(pe, b, "bcT")
                pe.wait_ge(s_bc3, b * 6 + 6)
                for j in range(NT):
                    last = t.transpose(w0("bcT")[0:96, :].bitcast(BF16)[:, j * P:(j + 1) * P],
                                       bc3[:, j, :, :].rearrange("p k n -> p (k n)"), identb[:])
                last.then_inc(s_full0, 1)
                done0(pe, b, "dtT")
                for h in range(NH):
                    take0(pe, b, f"dtp{h}")
                    t.matmul(w0(f"dtp{h}")[:], pc("dt_proj", R)[:, h * P:(h + 1) * P], dtT[:], start=True,
                             stop=True).then_inc(s_full0, 1)
                done0(pe, b, "bcT")
            def pre1(b):
                take1(pe, b, "xnT")
                for j in range(NT):
                    pe.wait_ge(s_xn1, b * NT + j + 1)
                    last = t.transpose(work1[:, j * P:(j + 1) * P], xn1[:, j, :], ident)
                last.then_inc(s_full1, 1)
                for key, w in (("q", "wq"), ("k", "wk")):
                    take1(pe, b, key)
                    t.matmul(work1[:], pc(w), xn1T[:, WIN:WIN + L], start=True, stop=True).then_inc(s_full1, 1)
                for j in range(4):
                    take1(pe, b, f"v{j}")
                    for g in range(4):
                        a = (4 * j + g) * GQ
                        last = t.matmul(work1[0:KW, g * P:(g + 1) * P], xn1T[:, a:a + KW], pc("wv"),
                                        start=True, stop=True)
                    last.then_inc(s_full1, 1)
                pe.wait_ge(s_qbd, b + 1)

            def spread(b, n):
                before(pe, s_dBu, b * N + n)
                t.matmul(b_bank[:], selb[:, n, :], bcT[:], start=True, stop=True).then_inc(s_bb, 1)
                before(pe, s_cb, b * N + n)
                t.matmul(c_bank[:], selb[:, N + n, :], bcT[:], start=True, stop=True).then_inc(s_cc, 1)

            def sum_y(b, n):
                if n == 0:
                    before(pe, s_yg, NH * b)
                    for h in range(NH):
                        last = t.matmul(y_bank[h][:], diag_d[:, h, :], u[:, h, :], start=True, stop=False)
                    last.then_inc(s_ys, 1)
                pe.wait_ge(s_hc, b * N + n + 1)
                for h in range(NH):
                    last = t.matmul(y_bank[h][:], ident, hc[n % 2][:, h, :], start=False, stop=(n == N - 1))
                last.then_inc(s_ys, 1)

            def scores(b, g):
                take1(pe, b, f"s{g}")
                v = 0 if g == 0 else (2 if g == G - 1 else 1)
                t.matmul(work1[:, 0:RG * KW], identb[:], bandb[:, v, :, :].rearrange("p r k -> p (r k)"),
                         start=True, stop=False)
                t.matmul(work1[:, 0:RG * KW], qbd[:, g, :, :].rearrange("p h q -> p (h q)"),
                         kT[:, :, g * GQ:g * GQ + KW], start=False, stop=True).then_inc(s_full1, 1)

            def probs_t(b, g):
                take1(pe, b, f"pT{g}")
                for r in range(RG):
                    last = t.transpose(work1[0:KW, r * P:(r + 1) * P], pexp[g % 2][:, r, :], ident)
                last.then_inc(s_full1, 1)

            def values(b, g):
                take1(pe, b, f"o{g // 2}")
                for c in range(2):
                    for r in range(RG):
                        a = (c * RG + r) * 33
                        last = t.matmul(work1[:, a:a + 33], pT[c][:, r * P:(r + 1) * P],
                                        vw[:, g - 1 + c, r, :], start=True, stop=True)
                last.then_inc(s_full1, 1)

            def ffn_in(b, c):
                for k, key in enumerate((f"gate{c}", f"up{c}")):
                    take1(pe, b, key)
                    t.matmul(work1[:], ffn[:, k, c * P:(c + 1) * P], xn1T[:, WIN:WIN + L], start=True,
                             stop=True).then_inc(s_full1, 1)

            def post0(b):
                sum_y(b, N - 1)
                pe.wait_ge(s_yg, NH * b + NH)
                take0(pe, b, "out")
                for h in range(NH):
                    last = t.matmul(w0("out")[:], pc("out_proj")[:, h * P:(h + 1) * P], yg[:, h, :], start=(h == 0),
                                    stop=(h == NH - 1))
                last.then_inc(s_full0, 1)
                done0(pe, b, "out")
                take0(pe, b, "outT")
                for j in range(NT):
                    last = t.transpose(w0("outT")[:, j * P:(j + 1) * P], outT[:, j * P:(j + 1) * P], ident)
                last.then_inc(s_full0, 1)

            def post1(b):
                take1(pe, b, "attnT")
                t.matmul(work1[:, 0:2], identb[:], identb[:, 0:2], start=True, stop=True)
                for g in range(G):
                    last = t.transpose(work1[:, g * GQ:(g + 1) * GQ],
                                       attn[:, g, :, :, :].rearrange("p r h d -> p (r h d)"), ident[0:GQ, 0:GQ])
                last.then_inc(s_full1, 1)
                take1(pe, b, "fin")
                t.matmul(work1[:], pc("wo"), attnT[:], start=True, stop=False)
                for c in range(HC):
                    last = t.matmul(work1[:], ffn[:, 2, c * P:(c + 1) * P], fh[:, c, :], start=False,
                                    stop=(c == HC - 1))
                last.then_inc(s_full1, 1)
                take1(pe, b, "finT")
                for j in range(NT):
                    last = t.transpose(work1[:, j * P:(j + 1) * P], finT[:, j * P:(j + 1) * P], ident)
                last.then_inc(s_full1, 1)

            def body(b0, b1):
                if b0 is not None:
                    pre0(b0)
                if b1 is not None:
                    pre1(b1)
                if b0 is not None:
                    spread(b0, 0)
                for n in range(N):
                    if b0 is not None and n + 1 < N:
                        spread(b0, n + 1)
                    if b1 is not None:
                        scores(b1, n)
                    if b0 is not None:
                        if n:
                            sum_y(b0, n - 1)
                    if b1 is not None:
                        probs_t(b1, n)
                    if b1 is not None and n % 2:
                        values(b1, n)
                    if b1 is not None and n in FFN_AT:
                        ffn_in(b1, FFN_AT[n])
                if b1 is not None:
                    post1(b1)
                if b0 is not None:
                    post0(b0)
            sequences(pe, body)


def kernel(**inputs):
    import concourse.bacc as bacc
    from concourse.bass_utils import run_bass_kernel_spmd

    a = {k: np.asarray(v) for k, v in inputs.items()}
    f = np.float32

    def cols(m):
        return np.concatenate([m[i:i + P].reshape(P, -1) for i in range(0, m.shape[0], P)], axis=1)

    def rows(m):
        return np.concatenate([m, np.zeros((P - m.shape[0], m.shape[1]), m.dtype)], axis=0)

    def spread(m):
        return np.broadcast_to(m.reshape(1, -1), (P, m.size))

    q, k = np.arange(P)[:, None] % GQ, np.arange(KW)[None, :]
    inside = (k >= q) & (k <= q + 2 * WIN)
    band = [np.where(m, 0.0, NEG).astype(f) for m in (inside & (k >= WIN), inside, inside & (k < WIN + GQ))]
    ln_row = np.concatenate([a["L0_attn_dt_ln_w"], a["L0_attn_b_ln_w"], a["L0_attn_c_ln_w"]])
    parts = {
        "in_proj": a["L0_attn_in_proj_w"].T, "x_proj": cols(a["L0_attn_x_proj_w"].T),
        "out_proj": cols(a["L0_attn_out_proj_w"].T), "dt_proj": rows(a["L0_attn_dt_proj_w"].T),
        "wq": a["L1_attn_Wq"], "wk": a["L1_attn_Wk"], "wv": a["L1_attn_Wv"], "wo": a["L1_attn_Wo"],
        "conv_w": cols(a["L0_attn_conv_w"].reshape(I, KC)), "conv_b": cols(a["L0_attn_conv_b"].reshape(I, 1)),
        "dt_b": cols(a["L0_attn_dt_proj_b"].reshape(I, 1)), "a_log": cols(a["L0_attn_A_log"]),
        "d": cols(a["L0_attn_D"].reshape(I, 1)), "gate_w": a["L0_ffn_gate_w"].T,
        "bq": a["L1_attn_bq"].reshape(H, 1), "bk": a["L1_attn_bk"].reshape(H, 1),
        "bv": a["L1_attn_bv"].reshape(H, 1), "bo": a["L1_attn_bo"].reshape(H, 1),
        "b1": a["L0_ffn_b1"].reshape(E * FC, P).T, "b2": spread(a["L0_ffn_b2"]), "ln_row": spread(ln_row),
        "gate_b": spread(a["L0_ffn_gate_b"]), "expert_b": spread(a["L0_ffn_expert_bias"]),
        "ident": np.eye(P, dtype=f), "sel": rows(np.tile(np.eye(2 * N, dtype=f), (3, 1))),
        "band": np.concatenate(band, axis=1), "heads": (np.arange(P)[:, None] % 32 // HD == np.arange(RG)).astype(f),
        "expert_no": spread(np.arange(E, dtype=f)), "rms_n": spread(np.array([1 / R, 1 / N, 1 / N], f)),
        "below": np.triu(np.ones((P, P), f), 1), "tile_at": spread(np.arange(NM, dtype=f) * P),
    }
    ffn = np.stack([a["L1_ffn_w_gate"].T, a["L1_ffn_w_up"].T, cols(a["L1_ffn_w_down"].T)], axis=1)
    arrays = {
        "hidden": a["L0_attn_hidden_states"],
        "pack": np.concatenate([parts[n] for n in PACK], axis=1),
        "w1": a["L0_ffn_w1"].transpose(1, 0, 2),
        "w2": a["L0_ffn_w2"].reshape(E, FC, P, H).transpose(2, 0, 1, 3),
        "ffn": ffn,
    }
    arrays = {"in_" + n: np.ascontiguousarray(m) for n, m in arrays.items()}
    nc = bacc.Bacc("TRN2", target_bir_lowering=False, num_devices=1)
    args = [nc.dram_tensor(n, m.shape, mybir.dt.from_np(m.dtype), kind="ExternalInput").ap() for n, m in arrays.items()]
    out = nc.dram_tensor("out", (B, L, H), F32, kind="ExternalOutput").ap()
    xn_d = nc.dram_tensor("xn_d", (B, L, H), F32, kind="Internal").ap()
    xs_d = nc.dram_tensor("xs_d", (NM // MG, MG, P, H), F32, kind="Internal").ap()
    ys_d = nc.dram_tensor("ys_d", (NM // MG, MG, P, H), F32, kind="Internal").ap()
    program(nc, *args, xn_d, xs_d, ys_d, out)
    r = run_bass_kernel_spmd(nc, [arrays], core_ids=[0])
    return r.results[0]["out"]
```

```python
from contextlib import ExitStack

import numpy as np

import concourse.bass as bass
from concourse import mybir

F32 = mybir.dt.float32
BF16 = mybir.dt.bfloat16
I32 = mybir.dt.int32
U32 = mybir.dt.uint32
ALU = mybir.AluOpType
ACT = mybir.ActivationFunctionType
AX_X = mybir.AxisListType.X

P = 128
B, L, H = 8, 512, 128
NT = L // P
I, N, R, KC = 256, 16, 64, 4
NH = I // P
E, FF = 8, 512
FC = FF // P
HEADS, HD = 16, 8
WIN = 32
GQ = 32
G = L // GQ
KW = GQ + 2 * WIN
RG = 4
HID = 384
HC = HID // P
LN_EPS = 1e-5
RMS_EPS = 1e-6
NEG = -1e30
XW = R + 2 * N
TT = B * NT
MG = 4
NM = -(-(TT + E - 1) // MG) * MG

PACK = {}
_at = 0
for _name, _width in (("in_proj", 2 * I), ("x_proj", NH * XW), ("out_proj", NH * H), ("dt_proj", I),
                      ("wq", H), ("wk", H), ("wv", H), ("wo", H), ("conv_w", NH * KC), ("conv_b", NH),
                      ("dt_b", NH), ("a_log", NH * N), ("d", NH), ("gate_w", E), ("bq", 1), ("bk", 1),
                      ("bv", 1), ("bo", 1), ("b1", E * FC), ("b2", E * H), ("ln_row", XW), ("gate_b", E),
                      ("expert_b", E), ("ident", P), ("sel", 2 * N), ("band", 3 * KW), ("heads", RG),
                      ("expert_no", E), ("rms_n", 3), ("below", P), ("tile_at", NM)):
    PACK[_name] = (_at, _at + _width)
    _at += _width
PACK_W = _at

ROUTE_SLOTS, ROUTE_TILES = 22, 25

SLOTS = 28
ATTN_AT = 10
FFN_AT = {12: 0, 16: 1, 20: 2}
PRE_AT = {0: ["xnT"], 1: ["hs0"], 2: ["hs1"], 3: ["conv0", "zg0"], 4: ["conv1", "sg0"], 5: ["conv2", "zg1"],
          6: ["conv3", "sg1"], 8: ["u"], 9: ["xdbl"], 10: ["ss"], 12: ["xdr"], 13: ["bc"], 15: ["dtT"], 16: ["bcT"],
          18: ["dtp0"], 19: ["drl0", "dtp1"], 21: ["drl1"], 22: ["de"], 23: ["dw"], 24: ["dln"], 25: ["dt"],
          26: ["dtu"], 27: ["start"]}
LAYER1_AT = {2: ["out"], 3: ["outT0", "outT1", "x1c"], 4: ["ln_a"], 5: ["ln_b"], 6: ["q", "k"], 7: ["v0", "v1"],
             8: ["v2", "v3"]}
FINISH_AT = {0: ["attnT"], 1: ["fin"], 2: ["finT0", "finT1"]}


def plan():
    units = []
    for slot in range(SLOTS):
        g = slot - ATTN_AT
        n = -(-4 * slot // 7)
        n = n if 7 * n // 4 == slot and n < N else None
        if 1 <= g <= G:
            units.append(("attn", "exp", g - 1))
        if 3 <= g <= G + 1 and g % 2:
            units.append(("attn", "values", g - 2))
        if 0 <= g < G:
            units.append(("attn", "scores", g))
        if n is not None:
            units.append(("scan", "step", n))
        if 3 <= g <= G + 1 and g % 2:
            units.append(("attn", "averages", g - 2))
        if slot == 0:
            units.append(("attn", "y_end", 0))
        if n is not None:
            units.append(("scan", "sum", n))
        if 0 <= g < G:
            units.append(("attn", "rowmax", g))
        if 1 <= g <= G:
            units.append(("attn", "turn", g - 1))
        for lane, at in (("finish", FINISH_AT), ("attn", LAYER1_AT), ("pre", PRE_AT)):
            for name in at.get(slot, []):
                units.append((lane, name, 0))
        if slot == 10:
            units.append(("scan", "rows", 0))
        if slot in FFN_AT:
            units.append(("attn", "ffn", FFN_AT[slot]))
        if n is not None:
            units.append(("scan", "spread", n))
    return units


PLAN = plan()

L0_USES = [n for lane, n, k in PLAN if lane == "pre" and n in ("xnT", "hs0", "hs1", "zg0", "zg1", "xdbl", "dtT", "bcT",
                                                                "dtp0", "dtp1")]
L1_USES = []
for _lane in ("attn", "finish"):
    for _l, _n, _k in PLAN:
        if _l == _lane:
            L1_USES += {"scores": [f"s{_k}"], "turn": [f"pT{_k}"], "values": [f"o{_k // 2}"],
                        "ffn": [f"gate{_k}", f"up{_k}"], "ln_b": ["xnT"]}.get(
                            _n, [_n] if _n in ("out", "outT0", "outT1", "q", "k", "v0", "v1", "v2", "v3", "attnT",
                                               "fin", "finT0", "finT1") else [])
L1_BANK, _turn = {}, 0
for _key in L1_USES:
    if _key[0] == "o" and _key[1:].isdigit() or _key[:2] == "pT" or _key in ("attnT", "finT1", "outT1", "k", "v2",
                                                                             "gate0", "gate1", "gate2"):
        L1_BANK[_key] = 2
    else:
        L1_BANK[_key], _turn = _turn, 1 - _turn
L1_PER = [list(L1_BANK.values()).count(_k) for _k in range(3)]
L1_NO = {_key: sum(L1_BANK[_q] == L1_BANK[_key] for _q in L1_USES[:_i]) for _i, _key in enumerate(L1_USES)}
L0_N, L1_N = len(L0_USES), len(L1_USES)
assert L0_N == 10 and L1_N == 60


def program(nc, hidden, pack, w1_d, w2_d, ffn_d, xn_d, xs_d, ys_d, out):
    ctx = ExitStack()
    with ctx:
        def sb(name, shape, dt=F32):
            return ctx.enter_context(nc.sbuf_tensor(name, shape, dt))

        def bank(name):
            return ctx.enter_context(nc.psum_tensor(name, [P, 512], F32))

        def sem(name):
            return ctx.enter_context(nc.semaphore(name))

        pk = sb("pk", [P, PACK_W])

        def pc(name, rows=P):
            a, z = PACK[name]
            return pk[0:rows, a:z]

        w1 = sb("w1", [P, E, FF])
        w2 = sb("w2", [P, E, FC, H])
        ffn = sb("ffn", [P, 3, HID])
        identb = sb("identb", [P, P], BF16)
        selb = sb("selb", [3 * 2 * N, 2 * N, P], BF16)
        bandb = sb("bandb", [P, 3, RG, KW], BF16)
        belowb = sb("belowb", [P, P], BF16)
        onesb = sb("onesb", [P, P], BF16)
        neg_a = sb("neg_a", [P, NH, N])
        exp_a = sb("exp_a", [P, NH * N])
        diag_d = sb("diag_d", [P, NH, P])
        gate_row = sb("gate_row", [P, E])
        bq_s = sb("bq_s", [P, 1])
        half_c = sb("half_c", [P, NH * (KC + 1)])
        minus_half = sb("minus_half", [P, 16])
        one = sb("one", [P, 1])
        tick = sb("tick", [P, 1])

        x_in = sb("x_in", [P, NT, H])
        x_res = sb("x_res", [P, NT, H])
        tick_p = sb("tick_p", [P, 1])
        stats = sb("stats", [P, 2 * NT, 6])
        mv = sb("mv", [P, 2 * NT, 2])
        var_e = sb("var_e", [P, 2 * NT])
        rstd = sb("rstd", [P, 2 * NT])
        xnT = sb("xnT", [P, L])
        hs = sb("hs", [P, NH, L + KC])
        u = sb("u", [P, NH, L])
        xsq = sb("xsq", [P, NT, XW])
        ss = sb("ss", [P, NT, 3])
        ms = sb("ms", [P, NT, 3])
        rr = sb("rr", [P, NT, 3])
        xdr = sb("xdr", [P, NT, XW])
        xdn = sb("xdn", [P, NT, XW])
        bc3 = sb("bc3", [P, NT, 3, 2 * N], BF16)
        bc_r1 = sb("bc_r1", [P, NT, 2 * N])
        bc_r2 = sb("bc_r2", [P, NT, 2 * N])
        dtT = sb("dtT", [R, L])
        bcT = [sb(f"bcT{k}", [3 * 2 * N, L], BF16) for k in range(2)]
        dc = sb("dc", [P, NH, L])
        old1 = w1[:].rearrange("p e f -> p (e f)").rearrange("p (k h t) -> p k h t", k=4, h=NH)
        old2 = w2[:].rearrange("p e c d -> p (e c d)").rearrange("p (k h t) -> p k h t", k=4, h=NH)
        z, th, tg = [old1[:, 0, :, :], old1[:, 1, :, :]], old1[:, 2, :, :], old1[:, 3, :, :]
        dt0 = sb("dt", [P, NH, L])
        dtu0 = sb("dtu", [P, NH, L])
        sg0 = sb("sg", [P, NH, L])
        dt, dtu, sg = [dt0[:], old2[:, 0, :, :]], [dtu0[:], old2[:, 1, :, :]], [sg0[:], old2[:, 2, :, :]]
        drl = old2[:, 3, :, :]
        dab, de, dw, dln = z[0], z[1], th, tg
        yg = dtu
        dA = [sb(f"dA{k}", [P, NH, L]) for k in range(2)]
        dBu = sb("dBu", [P, NH, L])
        hst = [sb(f"hst{k}", [P, NH, L]) for k in range(2)]
        cb = [sb(f"cb{k}", [P, L]) for k in range(2)]
        hc = [sb(f"hc{k}", [P, NH, L]) for k in range(2)]
        logits = dBu[:, 0, 0:TT * E].rearrange("p (t e) -> p t e", e=E)
        leq = dBu[:, 0, TT * E:2 * TT * E].rearrange("p (t e) -> p t e", e=E)
        lcand = dBu[:, 1, 0:TT * E].rearrange("p (t e) -> p t e", e=E)
        lmax = sb("lmax", [P, TT])
        onehot = sb("onehot", [P, TT, E], BF16)
        ones_t = sb("ones_t", [P, TT * E])
        tot = dA[0][:, 0, 0:TT * E].rearrange("p (e t) -> p e t", e=E)
        upto = dA[0][:, 1, 0:TT * E].rearrange("p (e t) -> p e t", e=E)
        slot_e = dA[1][:, 0, 0:TT * E].rearrange("p (e t) -> p e t", e=E)
        tile_cmp = dA[1][:, 1, 0:NM * E].rearrange("p (t e) -> p t e", e=E)
        cnt = sb("cnt", [P, E])
        cnt_i = sb("cnt_i", [P, E], I32)
        padded = sb("padded", [P, E])
        pad_end = sb("pad_end", [P, E])
        off = sb("off", [P, E])
        slot_f = sb("slot_f", [P, TT])
        slot_u = sb("slot_u", [P, TT], U32)
        slot_b = sb("slot_b", [P, NT], U32)
        tile_f = sb("tile_f", [P, NM])
        tile_e = sb("tile_e", [P, NM], I32)
        xa = [hst[k][:, 0, :].rearrange("p (j d) -> p j d", d=H) for k in range(2)]
        xna = [hc[k][:, 0, :].rearrange("p (j d) -> p j d", d=H) for k in range(2)]
        xaT = [dtu0[:, k, :] for k in range(2)]
        xg = [hc[0][:, k, :].rearrange("p (j d) -> p j d", d=H) for k in range(2)]
        xgT = hc[1][:, 0, :]
        h_sb = [hst[0][:, k, :] for k in range(2)]
        h_T = [hst[1][:, k, :] for k in range(2)]
        xall = [x[:].rearrange("p h (j d) -> p (h j) d", d=H) for x in hst + hc]
        ys = [dt0[:, k, :].rearrange("p (j d) -> p j d", d=H) for k in range(2)]
        outT = sb("outT", [P, L])

        x1r = sb("x1r", [P, NT, H])
        stats1 = sb("stats1", [P, NT, 6])
        mv1 = sb("mv1", [P, NT, 2])
        var1 = sb("var1", [P, NT])
        rstd1 = sb("rstd1", [P, NT])
        xn1 = sb("xn1", [P, NT, H])
        xn1T = sb("xn1T", [P, L + 2 * WIN])
        qT = sb("qT", [P, L])
        qbd = sb("qbd", [P, G, RG, GQ])
        kT = sb("kT", [P, RG, L + 2 * WIN])
        vw = sb("vw", [KW, G, RG, HD * 4 + 1])
        nmax = sb("nmax", [P, G, RG])
        pexp = [sb(f"pexp{k}", [P, RG, KW]) for k in range(2)]
        pT = [sb(f"pT{k}", [KW, RG * P]) for k in range(4)]
        rden = sb("rden", [P, 2, RG])
        attn = sb("attn", [GQ, G, RG, 4, HD])
        fth = sb("fth", [P, L])
        fsg = sb("fsg", [P, L])
        fh = sb("fh", [P, HC, L])
        ffn_i = fh[:, :, 0:HID].bitcast(I32)
        attnT, finT = fsg, fth
        y_out = sb("y_out", [P, NT, H])

        work = [bank("work0"), bank("work1")]
        work1 = bank("work1_l1")
        b_bank = bank("b_bank")
        c_bank = bank("c_bank")
        y_bank = [bank("y_bank0"), bank("y_bank1")]
        more = bank("more")
        bank0 = work[0]
        bank1 = [work[1], work1, more]

        gates2d = more[:, 0:TT * E]
        gates_bank = gates2d.rearrange("p (t e) -> p t e", e=E)
        rank2d, tot_bank = y_bank[0][:, 0:TT * E], y_bank[1][:, 0:TT * E]
        rank_bank = rank2d
        h_bank, t_bank, y_moe = [b_bank, c_bank], y_bank, more[:]

        s_pack, s_w1, s_w2, s_ffn = sem("pack_in"), sem("w1_in"), sem("w2_in"), sem("ffn_in")
        s_const = sem("const_ready")
        s_constp = sem("constp_ready")
        s_expa = sem("expa_ready")
        s_xin, s_xres, s_out = sem("x_in_landed"), sem("x_res_landed"), sem("out_stored")
        s_full0 = sem("work_full")
        s_free0 = sem("bank0_free")
        s_full1 = sem("work_l1_full")
        s_free1 = [sem(f"bank1_{k}_free") for k in range(3)]
        s_xa = [sem("xa0_in"), sem("xa1_in")]
        s_xast = [sem("xn0_stored"), sem("xn1_stored")]
        s_astat, s_arstd, s_axn = sem("a_stats"), sem("a_rstd"), sem("a_xn_ready")
        s_axT, s_axTc, s_agate = sem("a_xT_full"), sem("a_xT_copied"), sem("a_gates_done")
        s_route = sem("route_steps")
        s_count = sem("counts_full")
        s_xall = sem("xn_all_in")
        s_zero = sem("slots_zeroed")
        s_scat = sem("tokens_scattered")
        s_xg = [sem("xg0_in"), sem("xg1_in")]
        s_xgT, s_xgTc = sem("xgT_full"), sem("xgT_copied")
        s_mh, s_mhc = sem("expert_h_full"), sem("expert_h_copied")
        s_mt, s_mr = sem("expert_hT_full"), sem("expert_relu_ready")
        s_mdn, s_myc = sem("expert_y_full"), sem("expert_y_ready")
        s_yst = [sem("ys0_stored"), sem("ys1_stored")]
        s_slot = sem("slots_of_sequence")
        s_moe = sem("expert_rows_in")
        s_conv = sem("conv_steps")
        s_th = sem("tanh_ready")
        s_u = sem("u_ready")
        s_tg = sem("gate_tanh_ready")
        s_xsq = sem("xsq_ready")
        s_ss = sem("ss_ready")
        s_rr = sem("rr_ready")
        s_xdr = sem("xdr_ready")
        s_bc3 = sem("bc_steps")
        s_dab = sem("dt_abs_ready")
        s_de = sem("dt_exp_ready")
        s_dw = sem("dt_w_ready")
        s_dc = sem("dt_c_ready")
        s_dln = sem("dt_ln_ready")
        s_dt = sem("dt_ready")
        s_dtu = sem("dtu_ready")
        s_bb, s_cc = sem("b_bank_full"), sem("c_bank_full")
        s_dA, s_dBu, s_h, s_cb, s_hc = sem("dA_ready"), sem("dBu_ready"), sem("h_ready"), sem("cb_ready"), sem("hc_ready")
        s_ys = sem("y_summed")
        s_yg = sem("yg_ready")
        s_x1c = sem("x1_copied")
        s_stat1, s_rstd1, s_xn1 = sem("stats1_ready"), sem("rstd1_ready"), sem("xn1_ready")
        s_qbd = sem("qbd_ready")
        s_nmax, s_rden, s_attn, s_fth = sem("nmax_ready"), sem("rden_ready"), sem("attn_ready"), sem("ffn_tanh_ready")
        
        block = ctx.enter_context(nc.Block())

        def seq(dram, b):
            if isinstance(b, int):
                return dram[b, :, :].rearrange("(j p) d -> p j d", p=P)
            return dram[bass.ds(b, 1), :, :].rearrange("o (j p) d -> p (o j) d", p=P)

        def tiles(dram, i):
            if isinstance(i, int):
                return dram[i, :, :, :].rearrange("j p d -> p j d")
            return dram[bass.ds(i, 1), :, :, :].rearrange("o j p d -> p (o j) d")

        def full0(eng, b, key):
            eng.wait_ge(s_full0, b * L0_N + L0_USES.index(key) + 1)

        def take0(eng, b, key):
            before(eng, s_free0, b * L0_N + L0_USES.index(key))

        def done0(eng, b, key):
            eng.wait_ge(s_free0, b * L0_N + L0_USES.index(key) + 1)

        def w1k(key):
            return bank1[L1_BANK[key]]

        def free1(key):
            return s_free1[L1_BANK[key]]

        def full1(eng, b, key):
            eng.wait_ge(s_full1, b * L1_N + L1_USES.index(key) + 1)

        def take1(eng, b, key):
            before(eng, free1(key), b * L1_PER[L1_BANK[key]] + L1_NO[key])

        def done1(eng, b, key):
            before(eng, free1(key), b * L1_PER[L1_BANK[key]] + L1_NO[key] + 1)

        def take1_after(eng, b, key, *read):
            counts = [None, None, None]
            counts[L1_BANK[key]] = L1_NO[key]
            for k in read:
                counts[L1_BANK[k]] = max(counts[L1_BANK[k]] or 0, L1_NO[k] + 1)
            for k in range(3):
                if counts[k] is not None:
                    before(eng, s_free1[k], b * L1_PER[k] + counts[k])

        def before(eng, s, n):
            if isinstance(n, int) and n <= 0:
                return
            eng.wait_ge(s, n)

        def iterations(eng, body):
            body(-1, 1)
            body(0, 0)
            body(1, 1)
            with eng.Fori(1, B // 2 - 1) as i:
                body(i * 2, 0)
                body(i * 2 + 1, 1)
            for it in range(B - 2, B + 2):
                body(it, it % 2)

        def units(it):
            for lane, name, k in PLAN:
                b = it + {"pre": 1, "scan": 0, "attn": -1, "finish": -2}[lane]
                if not isinstance(b, int) or 0 <= b < B:
                    yield name, k, b

        @block.sync
        def _(sp):
            sp.dma_start(pk[:], pack).then_inc(s_pack, 16)

            def first_pass(i, first):
                for k in range(2):
                    if not first:
                        sp.wait_ge(s_axn, (2 * i + k - 1) * NT)
                    sp.dma_start(xa[k], seq(hidden, 2 * i + k)).then_inc(s_xa[k], 16)
                for k in range(2):
                    sp.wait_ge(s_axn, (2 * i + k + 1) * NT)
                    sp.dma_start(seq(xn_d, 2 * i + k), xna[k]).then_inc(s_xast[k], 16)
            first_pass(0, True)
            sp.dma_start(w1[:], w1_d).then_inc(s_w1, 16)
            sp.dma_start(w2[:], w2_d).then_inc(s_w2, 16)
            sp.dma_start(ffn_i, ffn_d).then_inc(s_ffn, 16)
            with sp.Fori(1, B // 2) as i:
                first_pass(i, False)

            sp.wait_ge(s_scat, 16 * TT)
            for k in range(2):
                sp.dma_start(xg[k], tiles(xs_d, k)).then_inc(s_xg[k], 16)

            def rounds(i, last):
                for k in range(2):
                    if not last:
                        sp.wait_ge(s_xgT, 2 * i + k + 1)
                        sp.dma_start(xg[k], tiles(xs_d, 2 * i + k + 2)).then_inc(s_xg[k], 16)
                    sp.wait_ge(s_myc, (2 * i + k + 1) * MG)
                    sp.dma_start(tiles(ys_d, 2 * i + k), ys[k]).then_inc(s_yst[k], 16)
            with sp.Fori(0, NM // MG // 2 - 1) as i:
                rounds(i, False)
            rounds(NM // MG // 2 - 1, True)

            sp.wait_ge(s_xast[0], 16 * B // 2)
            sp.wait_ge(s_xast[1], 16 * B // 2)
            sp.dma_start(x_in[:], seq(xn_d, 0)).then_inc(s_xin, 16)

            def body(it, par):
                for name, k, b in units(it):
                    if name == "xnT" and (not isinstance(b, int) or b + 1 < B):
                        full0(sp, b, "xnT")
                        sp.dma_start(x_in[:], seq(xn_d, b + 1)).then_inc(s_xin, 16)
                    if name == "finT1":
                        done1(sp, b, "finT0")
                        done1(sp, b, "finT1")
                        sp.dma_start(seq(out, b), y_out[:]).then_inc(s_out, 16)
                    if name == "rows":
                        before(sp, s_x1c, b)
                        sp.dma_start(x_res[:], seq(hidden, b)).then_inc(s_xres, 16)
            iterations(sp, body)
            sp.wait_ge(s_out, 16 * B)

        @block.vector
        def _(dve):
            v = nc.vector
            v.memset(minus_half[:], -0.5).then_inc(s_const, 1)
            v.memset(one[:], 1.0).then_inc(s_const, 1)
            v.memset(hs[:], 0.0).then_inc(s_const, 1)
            v.memset(xn1T[:], 0.0).then_inc(s_const, 1)
            v.memset(kT[:], 0.0).then_inc(s_const, 1)
            v.memset(vw[:], 1.0).then_inc(s_const, 1)
            dve.wait_ge(s_pack, 16)
            a = PACK["conv_w"][0]
            v.tensor_scalar(half_c[:], pk[:, a:a + NH * (KC + 1)], 0.5, None, ALU.mult).then_inc(s_const, 1)
            a = PACK["in_proj"][0]
            v.tensor_scalar(pk[:, a + I:a + 2 * I], pk[:, a + I:a + 2 * I], 0.5, None, ALU.mult).then_inc(s_const, 1)
            v.tensor_copy(identb[:], pc("ident")).then_inc(s_const, 1)
            v.tensor_copy(selb[:], pc("sel", 96).unsqueeze(2).to_broadcast([96, 2 * N, P])).then_inc(s_const, 1)
            v.tensor_copy(bandb[:], pc("band").rearrange("p (v k) -> p v k", v=3).unsqueeze(2)
                          .to_broadcast([P, 3, RG, KW])).then_inc(s_const, 1)
            v.tensor_copy(belowb[:], pc("below")).then_inc(s_const, 1)
            v.memset(onesb[:], 1.0).then_inc(s_const, 1)
            v.memset(ones_t[:], 1.0).then_inc(s_const, 1)
            for h in range(NH):
                v.tensor_scalar(diag_d[:, h, :], pc("ident"), pc("d")[:, h:h + 1], None, ALU.mult).then_inc(s_const, 1)
            v.tensor_tensor(gate_row[:], pc("gate_b"), pc("expert_b"), ALU.add).then_inc(s_const, 1)
            v.tensor_scalar(bq_s[:], pc("bq"), float(HD) ** -0.5, None, ALU.mult).then_inc(s_const, 1)
            dve.wait_ge(s_expa, 1)
            v.tensor_scalar(neg_a[:], exp_a[:].rearrange("p (h n) -> p h n", h=NH), -1.0, None, ALU.mult).then_inc(s_const, 1)
            dve.wait_ge(s_const, 19)

            def first_pass(i, first):
                for k in range(2):
                    dve.wait_ge(s_xa[k], 16 * i + 16)
                    for j in range(NT):
                        v.bn_stats(stats[:, k * NT + j, :], xa[k][:, j, :]).then_inc(s_astat, 1)
                    dve.wait_ge(s_astat, i * 18 + k * 9 + 4)
                    v.memset(tick[:], 0.0)
                    for j in range(NT):
                        v.bn_aggr(mv[:, k * NT + j, :], stats[:, k * NT + j, :]).then_inc(s_astat, 1)
                    dve.wait_ge(s_astat, i * 18 + k * 9 + 8)
                    v.tensor_scalar(var_e[:, k * NT:k * NT + NT], mv[:, k * NT:k * NT + NT, 1], LN_EPS, None,
                                    ALU.add).then_inc(s_astat, 1)
                for k in range(2):
                    dve.wait_ge(s_arstd, 2 * i + k + 1)
                    if not first:
                        dve.wait_ge(s_xast[k], 16 * i)
                        dve.wait_ge(s_axT, 2 * i + k - 1)
                    for j in range(NT):
                        n = k * NT + j
                        v.tensor_scalar(xna[k][:, j, :], xa[k][:, j, :], mv[:, n, 0:1], rstd[:, n:n + 1],
                                        ALU.subtract, ALU.mult).then_inc(s_axn, 1)
            first_pass(0, True)
            with dve.Fori(1, B // 2) as i:
                first_pass(i, False)

            step = [0]

            def routed(ins):
                step[0] += 1
                ins.then_inc(s_route, 1)
                dve.wait_ge(s_route, step[0])
            dve.wait_ge(s_agate, B)
            dve.wait_ge(s_zero, 16)
            routed(v.tensor_tensor(logits, gates_bank, gate_row[:].unsqueeze(1).to_broadcast([P, TT, E]), ALU.add))
            routed(v.tensor_reduce(lmax[:], logits, AX_X, ALU.max))
            routed(v.tensor_tensor(leq, logits, lmax[:].unsqueeze(2).to_broadcast([P, TT, E]), ALU.is_equal))
            routed(v.scalar_tensor_tensor(lcand, leq, -100.0, pc("expert_no").unsqueeze(1).to_broadcast([P, TT, E]),
                                          ALU.mult, ALU.add))
            routed(v.tensor_reduce(lmax[:], lcand, AX_X, ALU.min))
            routed(v.tensor_tensor(onehot[:], lcand, lmax[:].unsqueeze(2).to_broadcast([P, TT, E]), ALU.is_equal))
            dve.wait_ge(s_count, 1)
            routed(v.tensor_copy(tot, tot_bank.rearrange("p (t e) -> p e t", e=E)))
            routed(v.tensor_tensor_scan(upto.rearrange("p e t -> p (e t)"), ones_t[:],
                                        tot.rearrange("p e t -> p (e t)"), 0.0, ALU.mult, ALU.add))
            routed(v.tensor_reduce(cnt[:], tot, AX_X, ALU.add))
            routed(v.tensor_scalar(cnt_i[:], cnt[:], float(P - 1), None, ALU.add))
            routed(v.tensor_scalar(cnt_i[:], cnt_i[:], 7, 7, ALU.arith_shift_right, ALU.arith_shift_left))
            routed(v.tensor_copy(padded[:], cnt_i[:]))
            routed(v.tensor_tensor_scan(pad_end[:], ones_t[:, 0:E], padded[:], 0.0, ALU.mult, ALU.add))
            routed(v.tensor_tensor(off[:], pad_end[:], padded[:], ALU.subtract))
            routed(v.tensor_tensor(off[:], off[:], upto[:, :, TT - 1], ALU.subtract))
            routed(v.tensor_tensor(off[:], off[:], cnt[:], ALU.add))
            routed(v.tensor_tensor(upto, upto, tot, ALU.subtract))
            routed(v.tensor_tensor(slot_e, upto, rank_bank.rearrange("p (t e) -> p e t", e=E), ALU.add))
            routed(v.tensor_tensor(slot_e, slot_e, off[:].unsqueeze(2).to_broadcast([P, E, TT]), ALU.add))
            routed(v.tensor_tensor(slot_e, slot_e, onehot[:].rearrange("p t e -> p e t"), ALU.mult))
            routed(v.tensor_reduce(slot_f[:], slot_e.rearrange("p e t -> p t e"), AX_X, ALU.add))
            routed(v.tensor_copy(slot_u[:], slot_f[:]))
            slots_at = step[0]
            routed(v.tensor_tensor(tile_cmp, pad_end[:].unsqueeze(1).to_broadcast([P, NM, E]),
                                   pc("tile_at").unsqueeze(2).to_broadcast([P, NM, E]), ALU.is_le))
            routed(v.tensor_reduce(tile_f[:], tile_cmp, AX_X, ALU.add))
            routed(v.tensor_scalar(tile_e[:], tile_f[:], float(E - 1), None, ALU.min))
            assert (slots_at, step[0]) == (ROUTE_SLOTS, ROUTE_TILES)

            def rounds(i, first):
                for k in range(2):
                    m = 2 * i + k
                    for j in range(MG):
                        dve.wait_ge(s_mh, m * MG + j + 1)
                        if not (first and k == 0 and j < 2):
                            dve.wait_ge(s_mt, m * MG + j - 1)
                        v.tensor_copy(h_sb[j % 2], h_bank[j % 2][:]).then_inc(s_mhc, 1)
                    dve.wait_ge(s_mdn, (m + 1) * MG)
                    if not first:
                        dve.wait_ge(s_yst[k], 16 * i)
                    for j in range(MG):
                        e = dve.value_load(tile_e[0:1, bass.ds(m * MG + j, 1)], min_val=0, max_val=E - 1)
                        v.tensor_tensor(ys[k][:, j, :], y_moe[:, j * H:(j + 1) * H],
                                        pc("b2").rearrange("p (e d) -> p e d", e=E)[:, bass.ds(e, 1), :]
                                        .rearrange("p o d -> p (o d)"), ALU.add).then_inc(s_myc, 1)
            rounds(0, True)
            with dve.Fori(1, NM // MG // 2) as i:
                rounds(i, False)
            dve.wait_ge(s_myc, NM)
            for k in range(2):
                v.memset(dA[k][:], 0.0).then_inc(s_const, 1)
            dve.wait_ge(s_ffn, 16)
            v.tensor_scalar(ffn[:], ffn_i, 1.0 / 127.0, None, ALU.mult).then_inc(s_const, 1)
            dve.wait_ge(s_const, 22)
            v.tensor_scalar(ffn[:, 0, :], ffn[:, 0, :], 0.5, None, ALU.mult).then_inc(s_const, 1)

            def step(n, b, par):
                if n == 0:
                    dve.wait_ge(s_dtu, b + 1)
                dve.wait_ge(s_bb, b * N + n + 1)
                before(dve, s_h, b * N + n)
                v.tensor_tensor(dBu[:], dtu[par], b_bank[:].unsqueeze(1).to_broadcast([P, NH, L]),
                                ALU.mult).then_inc(s_dBu, 1)
                dve.wait_ge(s_dBu, b * N + n + 1)
                dve.wait_ge(s_dA, (b * N + n + 1) * NH)
                before(dve, s_hc, b * N + n - 1)
                v.tensor_tensor_scan(hst[n % 2][:].rearrange("p h t -> p (h t)"),
                                     dA[n % 2][:].rearrange("p h t -> p (h t)"),
                                     dBu[:].rearrange("p h t -> p (h t)"), 0.0,
                                     ALU.mult, ALU.add).then_inc(s_h, 1)

            def conv(k, b):
                for h in range(NH):
                    src = hs[:, h, k:k + L]
                    w = half_c[:, h * KC + k:h * KC + k + 1]
                    if k == 0:
                        done0(dve, b, f"hs{h}")
                        before(dve, s_de, b)
                        v.tensor_scalar(z[0][:, h, :], src, w, half_c[:, NH * KC + h:NH * KC + h + 1],
                                        ALU.mult, ALU.add).then_inc(s_conv, 1)
                    else:
                        dve.wait_ge(s_conv, b * NH * KC + (k - 1) * NH + h + 1)
                        v.scalar_tensor_tensor(z[k % 2][:, h, :], src, w, z[(k - 1) % 2][:, h, :],
                                               ALU.mult, ALU.add).then_inc(s_conv, 1)

            def pre(name, b, par):
                if name.startswith("conv"):
                    conv(int(name[4:]), b)
                elif name in ("sg0", "sg1"):
                    h = int(name[2:])
                    dve.wait_ge(s_tg, b * NH + h + 1)
                    before(dve, s_yg, (b - 1) * NH)
                    v.scalar_tensor_tensor(sg[par][:, h, :], tg[:, h, :], 1.0, bank0[:],
                                           ALU.add, ALU.mult).then_inc(s_free0, 1)
                elif name == "u":
                    before(dve, s_ys, (b - 1) * (N + 1) + 1)
                    for h in range(NH):
                        dve.wait_ge(s_th, b * NH + h + 1)
                        v.scalar_tensor_tensor(u[:, h, :], th[:, h, :], 1.0, z[1][:, h, :],
                                               ALU.add, ALU.mult).then_inc(s_u, 1)
                elif name == "ss":
                    dve.wait_ge(s_xsq, b + 1)
                    for k, (a, w) in enumerate(((0, R), (R, N), (R + N, N))):
                        v.tensor_reduce(ss[:, :, k], xsq[:, :, a:a + w], AX_X, ALU.add).then_inc(s_ss, 1)
                    dve.wait_ge(s_ss, b * 5 + 3)
                    v.tensor_tensor(ms[:], ss[:], pc("rms_n").unsqueeze(1).to_broadcast([P, NT, 3]),
                                    ALU.mult).then_inc(s_ss, 1)
                    dve.wait_ge(s_ss, b * 5 + 4)
                    v.tensor_scalar(ms[:], ms[:], RMS_EPS, None, ALU.add).then_inc(s_ss, 1)
                elif name == "xdr":
                    dve.wait_ge(s_rr, b + 1)
                    before(dve, s_bc3, (b - 1) * 6 + 1)
                    xd = bank0[:, 0:NT * XW].rearrange("p (j c) -> p j c", c=XW)
                    for k, (a, w) in enumerate(((0, R), (R, N), (R + N, N))):
                        last = v.tensor_tensor(xdr[:, :, a:a + w], xd[:, :, a:a + w],
                                               rr[:, :, k:k + 1].to_broadcast([P, NT, w]), ALU.mult)
                        last.then_inc(s_free0 if k == 2 else s_xdr, 1)
                elif name in ("drl0", "drl1"):
                    h = int(name[3:])
                    dve.wait_ge(s_dab, b * NH + h + 1)
                    v.tensor_scalar(drl[:, h, :], bank0[:], pc("dt_b")[:, h:h + 1], 0.0,
                                    ALU.add, ALU.max).then_inc(s_free0, 1)
                elif name == "dw":
                    dve.wait_ge(s_de, b + 1)
                    v.tensor_scalar(dw, de, 1.0, None, ALU.add).then_inc(s_dw, 1)
                    dve.wait_ge(s_dw, b + 1)
                    v.scalar_tensor_tensor(dc[:], dw, -1.0, de, ALU.add, ALU.subtract).then_inc(s_dc, 1)
                elif name == "dt":
                    dve.wait_ge(s_dc, b * 2 + 1)
                    dve.wait_ge(s_dln, b + 1)
                    v.tensor_tensor(dc[:], dln, dc[:], ALU.subtract).then_inc(s_dc, 1)
                    dve.wait_ge(s_dc, b * 2 + 2)
                    done0(dve, b, "dtp1")
                    v.tensor_tensor(dt[par], dc[:], drl, ALU.add).then_inc(s_dt, 1)
                elif name == "dtu":
                    dve.wait_ge(s_dt, b + 1)
                    dve.wait_ge(s_u, b * NH + NH)
                    if not isinstance(b, int) or b >= 2:
                        full1(dve, b - 2, "out")
                    v.tensor_tensor(dtu[par], dt[par], u[:], ALU.mult).then_inc(s_dtu, 1)

            def layer1(name, k, b, par):
                if name == "y_end":
                    dve.wait_ge(s_ys, b * (N + 1) + N + 1)
                    for h in range(NH):
                        v.tensor_tensor(yg[par][:, h, :], y_bank[h][:], sg[par][:, h, :], ALU.mult).then_inc(s_yg, 1)
                elif name in ("outT0", "outT1"):
                    c = int(name[4:])
                    full1(dve, b, name)
                    dve.wait_ge(s_moe, b * 16 * NT + 16 * NT)
                    v.tensor_tensor(x_res[:, 2 * c:2 * c + 2, :], x_res[:, 2 * c:2 * c + 2, :],
                                    w1k(name)[:, 0:2 * P].rearrange("p (j d) -> p j d", j=2),
                                    ALU.add).then_inc(free1(name), 1)
                elif name == "ln_a":
                    dve.wait_ge(s_x1c, b + 1)
                    for j in range(NT):
                        v.bn_stats(stats1[:, j, :], x1r[:, j, :]).then_inc(s_stat1, 1)
                    dve.wait_ge(s_stat1, b * 9 + 4)
                    v.memset(tick[:], 0.0)
                    for j in range(NT):
                        v.bn_aggr(mv1[:, j, :], stats1[:, j, :]).then_inc(s_stat1, 1)
                    dve.wait_ge(s_stat1, b * 9 + 8)
                    v.tensor_scalar(var1[:], mv1[:, :, 1], LN_EPS, None, ALU.add).then_inc(s_stat1, 1)
                elif name == "ln_b":
                    dve.wait_ge(s_rstd1, b + 1)
                    for j in range(NT):
                        v.tensor_scalar(xn1[:, j, :], x1r[:, j, :], mv1[:, j, 0:1], rstd1[:, j:j + 1],
                                        ALU.subtract, ALU.mult).then_inc(s_xn1, 1)
                elif name == "rowmax":
                    if k == 4:
                        before(dve, s_out, b * 16)
                    full1(dve, b, f"s{k}")
                    v.tensor_reduce(nmax[:, k, :], w1k(f"s{k}")[:, 0:RG * KW].rearrange("p (r k) -> p r k", r=RG),
                                    AX_X, ALU.max, negate=True).then_inc(s_nmax, 1)
                elif name == "averages":
                    key = f"o{k // 2}"
                    full1(dve, b, key)
                    if k > 1:
                        done1(dve, b, f"o{k // 2 - 1}")
                    else:
                        done1(dve, b - 1, f"o{G // 2 - 1}")
                    o = w1k(key)[:, 0:2 * RG * 33].rearrange("p (c r d) -> p c r d", c=2, r=RG)
                    v.reciprocal(rden[:], o[:, :, :, 32]).then_inc(s_rden, 1)
                    dve.wait_ge(s_rden, b * (G // 2) + k // 2 + 1)
                    for j in range(4):
                        q = slice(32 * j, 32 * j + 32)
                        last = v.tensor_tensor(attn[:, k - 1:k + 1, :, j, :], o[q, :, :, HD * j:HD * j + HD],
                                               rden[q, :, :].unsqueeze(3).to_broadcast([32, 2, RG, HD]), ALU.mult)
                        last.then_inc(free1(key) if j == 3 else s_attn, 1)
                elif name == "ffn":
                    dve.wait_ge(s_fth, b * HC + k + 1)
                    v.scalar_tensor_tensor(fsg[:], fth[:], 1.0, w1k(f"gate{k}")[:], ALU.add,
                                           ALU.mult).then_inc(free1(f"gate{k}"), 1)
                    full1(dve, b, f"up{k}")
                    done1(dve, b, f"gate{k}")
                    v.tensor_tensor(fh[:, k, :], fsg[:], w1k(f"up{k}")[:], ALU.mult).then_inc(free1(f"up{k}"), 1)
                elif name in ("finT0", "finT1"):
                    c = int(name[4:])
                    full1(dve, b, name)
                    v.tensor_tensor(y_out[:, 2 * c:2 * c + 2, :], x1r[:, 2 * c:2 * c + 2, :],
                                    w1k(name)[:, 0:2 * P].rearrange("p (j d) -> p j d", j=2),
                                    ALU.add).then_inc(free1(name), 1)

            def body(it, par):
                for name, k, b in units(it):
                    if name == "step":
                        step(k, b, par)
                    elif name == "rows":
                        before(dve, s_moe, b * 16 * NT)
                        v.tensor_tensor(slot_b[:], slot_f[:, 4 * b:4 * b + 4] if isinstance(b, int) else
                                        slot_f[:, bass.ds(b * 4, 4)],
                                        one[:].to_broadcast([P, NT]), ALU.mult).then_inc(s_slot, 1)
                    else:
                        pre(name, b, 1 - par)
                        layer1(name, k, b, 1 - par)
            iterations(dve, body)

        @block.scalar
        def _(act):
            s = nc.scalar
            act.wait_ge(s_pack, 16)
            s.activation(exp_a[:], pc("a_log"), ACT.Exp).then_inc(s_expa, 1)
            act.wait_ge(s_const, 19)

            def first_pass(i, first):
                for k in range(2):
                    act.wait_ge(s_axT, 2 * i + k + 1)
                    if not first:
                        act.wait_ge(s_agate, 2 * i + k - 1)
                    s.activation(xaT[k], work[k][:], ACT.Copy).then_inc(s_axTc, 1)
            first_pass(0, True)
            with act.Fori(1, B // 2) as i:
                first_pass(i, False)

            def rounds(i, first):
                for k in range(2):
                    m = 2 * i + k
                    act.wait_ge(s_xgT, m + 1)
                    if not (first and k == 0):
                        act.wait_ge(s_mh, m * MG)
                    s.activation(xgT, work1[:], ACT.Copy).then_inc(s_xgTc, 1)
                    for j in range(MG):
                        e = act.value_load(tile_e[0:1, bass.ds(m * MG + j, 1)], min_val=0, max_val=E - 1)
                        act.wait_ge(s_mt, m * MG + j + 1)
                        if not (first and k == 0 and j < 2):
                            act.wait_ge(s_mdn, m * MG + j - 1)
                        for c in range(FC):
                            last = s.activation(h_T[j % 2][:, c * P:(c + 1) * P], t_bank[j % 2][:, c * P:(c + 1) * P],
                                                ACT.Relu, bias=pc("b1").rearrange("p (e c) -> p e c", c=FC)
                                                [:, bass.ds(e, 1), c:c + 1].rearrange("p o c -> p (o c)"))
                        last.then_inc(s_mr, 1)
            act.wait_ge(s_route, ROUTE_TILES)
            rounds(0, True)
            with act.Fori(1, NM // MG // 2) as i:
                rounds(i, False)
            act.wait_ge(s_const, 23)

            def copy_c(n, b):
                act.wait_ge(s_cc, b * N + n + 1)
                before(act, s_hc, b * N + n - 1)
                s.copy(cb[n % 2][:], c_bank[:]).then_inc(s_cb, 1)

            def decays(n, b, par):
                if n == 0:
                    act.wait_ge(s_dt, b + 1)
                before(act, s_h, b * N + n - 1)
                for h in range(NH):
                    s.activation(dA[n % 2][:, h, 1:L], dt[par][:, h, 1:L], ACT.Exp,
                                 scale=neg_a[:, h, n:n + 1]).then_inc(s_dA, 1)

            def pre(name, b, par):
                if name == "xnT":
                    full0(act, b, name)
                    s.copy(xnT[:], bank0[:]).then_inc(s_free0, 1)
                elif name in ("hs0", "hs1"):
                    h = int(name[2:])
                    full0(act, b, name)
                    before(act, s_conv, b * NH * KC)
                    s.copy(hs[:, h, 1:1 + L], bank0[:]).then_inc(s_free0, 1)
                elif name in ("zg0", "zg1"):
                    h = int(name[2:])
                    full0(act, b, name)
                    before(act, s_dc, 2 * b)
                    s.activation(tg[:, h, :], bank0[:], ACT.Tanh).then_inc(s_tg, 1)
                elif name == "conv3":
                    for h in range(NH):
                        act.wait_ge(s_conv, b * NH * KC + (KC - 1) * NH + h + 1)
                        s.activation(th[:, h, :], z[1][:, h, :], ACT.Tanh).then_inc(s_th, 1)
                elif name == "xdbl":
                    full0(act, b, name)
                    before(act, s_ss, b * 5)
                    s.activation(xsq[:], bank0[:, 0:NT * XW].rearrange("p (j c) -> p j c", c=XW),
                                 ACT.Square).then_inc(s_xsq, 1)
                elif name == "dtT":
                    full0(act, b, name)
                    s.copy(dtT[:], bank0[0:R, :]).then_inc(s_free0, 1)
                elif name == "bcT":
                    full0(act, b, name)
                    before(act, s_cc, (b - 1) * N)
                    s.copy(bcT[par][:], bank0[0:96, :].bitcast(BF16)[:, 0:L]).then_inc(s_free0, 1)
                elif name in ("dtp0", "dtp1"):
                    h = int(name[3:])
                    full0(act, b, name)
                    s.activation(dab[:, h, :], bank0[:], ACT.Abs, bias=pc("dt_b")[:, h:h + 1]).then_inc(s_dab, 1)
                elif name == "de":
                    act.wait_ge(s_dab, b * NH + NH)
                    act.wait_ge(s_u, b * NH + NH)
                    s.activation(de, dab, ACT.Exp, scale=-1.0).then_inc(s_de, 1)
                elif name == "dln":
                    act.wait_ge(s_dw, b + 1)
                    s.activation(dln, dw, ACT.Ln).then_inc(s_dln, 1)
                elif name == "start":
                    decays(0, b, par)
                    copy_c(0, b)

            def layer1(name, k, b):
                if name == "out":
                    full1(act, b, name)
                    s.copy(outT[:], w1k(name)[:]).then_inc(free1(name), 1)
                elif name == "x1c":
                    done1(act, b, "outT0")
                    done1(act, b, "outT1")
                    s.copy(x1r[:], x_res[:]).then_inc(s_x1c, 1)
                elif name == "ln_b":
                    full1(act, b, "xnT")
                    s.copy(xn1T[:, WIN:WIN + L], w1k("xnT")[:]).then_inc(free1("xnT"), 1)
                elif name == "q":
                    full1(act, b, name)
                    before(act, s_qbd, b)
                    s.activation(qT[:], w1k(name)[:], ACT.Identity, bias=bq_s[:],
                                 scale=float(HD) ** -0.5).then_inc(free1(name), 1)
                elif name == "k":
                    full1(act, b, name)
                    for r in range(RG):
                        q = slice(32 * r, 32 * r + 32)
                        last = s.activation(kT[q, r, WIN:WIN + L], w1k(name)[q, :], ACT.Identity, bias=pc("bk")[q, :])
                    last.then_inc(free1(name), 1)
                elif name in ("v0", "v1", "v2", "v3"):
                    j = int(name[1:])
                    full1(act, b, name)
                    s.copy(vw[:, 4 * j:4 * j + 4, :, 0:32],
                           w1k(name)[0:KW, :].rearrange("p (g r d) -> p g r d", g=4, r=RG)).then_inc(free1(name), 1)
                elif name == "exp":
                    act.wait_ge(s_nmax, b * G + k + 1)
                    before(act, s_full1, b * L1_N + L1_USES.index(f"pT{k - 2}") + 1 if k >= 2 else
                           (b - 1) * L1_N + L1_USES.index(f"pT{G - 2 + k}") + 1)
                    for r in range(RG):
                        last = s.activation(pexp[k % 2][:, r, :], w1k(f"s{k}")[:, r * KW:(r + 1) * KW], ACT.Exp,
                                            bias=nmax[:, k, r:r + 1])
                    last.then_inc(free1(f"s{k}"), 1)
                elif name == "turn":
                    full1(act, b, f"pT{k}")
                    s.copy(pT[k % 4][:], w1k(f"pT{k}")[0:KW, :]).then_inc(free1(f"pT{k}"), 1)
                elif name == "ffn":
                    full1(act, b, f"gate{k}")
                    s.activation(fth[:], w1k(f"gate{k}")[:], ACT.Tanh).then_inc(s_fth, 1)
                elif name == "attnT":
                    full1(act, b, name)
                    s.activation(attnT[:], w1k(name)[:], ACT.Identity, bias=pc("bv")).then_inc(free1(name), 1)
                elif name == "fin":
                    full1(act, b, name)
                    s.activation(finT[:], w1k(name)[:], ACT.Identity, bias=pc("bo")).then_inc(free1(name), 1)

            def body(it, par):
                for name, k, b in units(it):
                    if name == "step":
                        if k + 1 < N:
                            decays(k + 1, b, par)
                    elif name == "spread":
                        if k + 1 < N:
                            copy_c(k + 1, b)
                    else:
                        pre(name, b, 1 - par)
                        layer1(name, k, b)
            iterations(act, body)

        @block.gpsimd
        def _(pool):
            g_ = nc.gpsimd
            g_.memset(dBu[:], 0.0).then_inc(s_constp, 1)
            pool.wait_ge(s_constp, 1)
            pool.dma_start(xs_d.rearrange("i j p d -> (i j p d)").rearrange("(q r n) -> q r n", q=P, n=L),
                           dBu[:, 0:1, :].to_broadcast([P, NM * H // L, L])).then_inc(s_zero, 16)
            pool.wait_ge(s_const, 19)

            def first_pass(i):
                for k in range(2):
                    pool.wait_ge(s_astat, i * 18 + k * 9 + 9)
                    g_.tensor_tensor(rstd[:, k * NT:k * NT + NT], var_e[:, k * NT:k * NT + NT],
                                     minus_half[:, 0:NT], ALU.pow).then_inc(s_arstd, 1)
            with pool.Fori(0, B // 2) as i:
                first_pass(i)
            pool.wait_ge(s_xast[0], 16 * B // 2)
            pool.wait_ge(s_xast[1], 16 * B // 2)
            pool.wait_ge(s_axT, B)
            for k in range(4):
                pool.dma_start(xall[k], xn_d[2 * k:2 * k + 2, :, :].rearrange("b (j p) d -> p (b j) d", p=P))                    .then_inc(s_xall, 16)
            pool.wait_ge(s_route, ROUTE_SLOTS)
            pool.wait_ge(s_xall, 16 * 4)
            for k in range(TT):
                g_.indirect_dma_start(xs_d.rearrange("i j p d -> (i j p) d"),
                                      bass.IndirectOffsetOnAxis(ap=slot_u[:, k:k + 1], axis=0),
                                      xall[k // 8][:, k % 8, :], None).then_inc(s_scat, 16)
            pool.wait_ge(s_yst[0], 16 * NM // MG // 2)
            pool.wait_ge(s_yst[1], 16 * NM // MG // 2)

            def rows(b):
                pool.wait_ge(s_xres, b * 16 + 16)
                pool.wait_ge(s_slot, b + 1)
                g_.tensor_tensor(tick_p[:], one[:], one[:], ALU.mult)
                for j in range(NT):
                    g_.indirect_dma_start(x_res[:, j, :], None, ys_d.rearrange("i j p d -> (i j p) d"),
                                          bass.IndirectOffsetOnAxis(ap=slot_b[:, j:j + 1], axis=0),
                                          compute_op=ALU.add).then_inc(s_moe, 16)

            def bc(b):
                done0(pool, b, "xdbl")
                if not isinstance(b, int) or b >= 1:
                    full0(pool, b - 1, "bcT")
                g_.tensor_tensor(xdn[:], xdr[:], pc("ln_row").unsqueeze(1).to_broadcast([P, NT, XW]),
                                 ALU.mult).then_inc(s_bc3, 1)
                val = xdn[:, :, R:XW]
                ones = one[:].unsqueeze(1).to_broadcast([P, NT, 2 * N])
                pool.wait_ge(s_bc3, b * 6 + 1)
                g_.tensor_tensor(bc3[:, :, 0, :], val, ones, ALU.mult).then_inc(s_bc3, 1)
                pool.wait_ge(s_bc3, b * 6 + 2)
                g_.tensor_tensor(bc_r1[:], val, bc3[:, :, 0, :], ALU.subtract).then_inc(s_bc3, 1)
                pool.wait_ge(s_bc3, b * 6 + 3)
                g_.tensor_tensor(bc3[:, :, 1, :], bc_r1[:], ones, ALU.mult).then_inc(s_bc3, 1)
                pool.wait_ge(s_bc3, b * 6 + 4)
                g_.tensor_tensor(bc_r2[:], bc_r1[:], bc3[:, :, 1, :], ALU.subtract).then_inc(s_bc3, 1)
                pool.wait_ge(s_bc3, b * 6 + 5)
                g_.tensor_tensor(bc3[:, :, 2, :], bc_r2[:], ones, ALU.mult).then_inc(s_bc3, 1)

            def times_c(b, n):
                pool.wait_ge(s_h, b * N + n + 1)
                pool.wait_ge(s_cb, b * N + n + 1)
                before(pool, s_ys, b * (N + 1) + n)
                g_.tensor_tensor(hc[n % 2][:], hst[n % 2][:], cb[n % 2][:].unsqueeze(1).to_broadcast([P, NH, L]),
                                 ALU.mult).then_inc(s_hc, 1)

            def body(it, par):
                for name, k, b in units(it):
                    if name == "step":
                        times_c(b, k)
                    elif name == "rows":
                        rows(b)
                    elif name == "ss":
                        pool.wait_ge(s_ss, b * 5 + 5)
                        g_.tensor_tensor(rr[:].rearrange("p j k -> p (j k)"), ms[:].rearrange("p j k -> p (j k)"),
                                         minus_half[:, 0:NT * 3], ALU.pow).then_inc(s_rr, 1)
                    elif name == "bc":
                        bc(b)
                    elif name == "ln_a":
                        pool.wait_ge(s_stat1, b * 9 + 9)
                        g_.tensor_tensor(rstd1[:], var1[:], minus_half[:, 0:NT], ALU.pow).then_inc(s_rstd1, 1)
                    elif name == "q":
                        done1(pool, b, "q")
                        g_.tensor_tensor(qbd[:], qT[:].rearrange("p (g q) -> p g q", q=GQ).unsqueeze(2)
                                         .to_broadcast([P, G, RG, GQ]),
                                         pc("heads").unsqueeze(1).unsqueeze(3).to_broadcast([P, G, RG, GQ]),
                                         ALU.mult).then_inc(s_qbd, 1)
            iterations(pool, body)

        @block.tensor
        def _(pe):
            t = nc.tensor
            ident = pc("ident")
            pe.wait_ge(s_const, 19)

            def first_pass(i, first):
                for k in range(2):
                    for j in range(NT):
                        pe.wait_ge(s_axn, (2 * i + k) * NT + j + 1)
                        if j == 0 and not first:
                            pe.wait_ge(s_axTc, 2 * i + k - 1)
                        last = t.transpose(work[k][:, j * P:(j + 1) * P], xna[k][:, j, :], ident)
                    last.then_inc(s_axT, 1)
                for k in range(2):
                    pe.wait_ge(s_axTc, 2 * i + k + 1)
                    for j in range(NT):
                        a = ((2 * i + k) * NT + j) * E
                        o = gates2d[:, a:a + E] if isinstance(i, int) else gates2d[:, bass.ds(a, E)]
                        last = t.matmul(o, xaT[k][:, j * P:(j + 1) * P], pc("gate_w"), start=True, stop=True)
                    last.then_inc(s_agate, 1)
            first_pass(0, True)
            with pe.Fori(1, B // 2) as i:
                first_pass(i, False)
            pe.wait_ge(s_route, 6)
            oh = onehot[:].rearrange("p t e -> p (t e)")
            t.matmul(rank2d, belowb[:], oh, start=True, stop=True)
            t.matmul(tot_bank, onesb[:], oh, start=True, stop=True).then_inc(s_count, 1)

            pe.wait_ge(s_w1, 16)
            pe.wait_ge(s_w2, 16)
            pe.wait_ge(s_route, ROUTE_TILES)

            def rounds(i, first):
                for k in range(2):
                    m = 2 * i + k
                    pe.wait_ge(s_xg[k], 16 * i + 16)
                    if not (first and k == 0):
                        pe.wait_ge(s_xgTc, m)
                    for j in range(MG):
                        last = t.transpose(work1[:, j * P:(j + 1) * P], xg[k][:, j, :], ident)
                    last.then_inc(s_xgT, 1)
                    es = [pe.value_load(tile_e[0:1, bass.ds(m * MG + j, 1)], min_val=0, max_val=E - 1)
                          for j in range(MG)]

                    def up(j):
                        if not (first and k == 0 and j < 2):
                            pe.wait_ge(s_mhc, m * MG + j - 1)
                        t.matmul(h_bank[j % 2][:], xgT[:, j * P:(j + 1) * P],
                                 w1[:, bass.ds(es[j], 1), :].rearrange("p o f -> p (o f)"),
                                 start=True, stop=True).then_inc(s_mh, 1)

                    def turn(j):
                        pe.wait_ge(s_mhc, m * MG + j + 1)
                        if not (first and k == 0 and j < 2):
                            pe.wait_ge(s_mr, m * MG + j - 1)
                        for c in range(FC):
                            last = t.transpose(t_bank[j % 2][:, c * P:(c + 1) * P],
                                               h_sb[j % 2][:, c * P:(c + 1) * P], ident)
                        last.then_inc(s_mt, 1)

                    def down(j):
                        pe.wait_ge(s_mr, m * MG + j + 1)
                        if j == 0 and not (first and k == 0):
                            pe.wait_ge(s_myc, m * MG)
                        for c in range(FC):
                            last = t.matmul(y_moe[:, j * H:(j + 1) * H], h_T[j % 2][:, c * P:(c + 1) * P],
                                            w2[:, bass.ds(es[j], 1), c, :].rearrange("p o d -> p (o d)"),
                                            start=(c == 0), stop=(c == FC - 1))
                        last.then_inc(s_mdn, 1)
                    pe.wait_ge(s_xgTc, m + 1)
                    up(0)
                    up(1)
                    turn(0)
                    up(2)
                    turn(1)
                    down(0)
                    up(3)
                    turn(2)
                    down(1)
                    turn(3)
                    down(2)
                    down(3)
            rounds(0, True)
            with pe.Fori(1, NM // MG // 2) as i:
                rounds(i, False)
            pe.wait_ge(s_const, 23)

            def spread(b, n, par):
                before(pe, s_dBu, b * N + n)
                t.matmul(b_bank[:], selb[:, n, :], bcT[par][:], start=True, stop=True).then_inc(s_bb, 1)
                before(pe, s_cb, b * N + n)
                t.matmul(c_bank[:], selb[:, N + n, :], bcT[par][:], start=True, stop=True).then_inc(s_cc, 1)

            def sum_y(b, n):
                if n == 0:
                    before(pe, s_yg, NH * b)
                    for h in range(NH):
                        last = t.matmul(y_bank[h][:], diag_d[:, h, :], u[:, h, :], start=True, stop=False)
                    last.then_inc(s_ys, 1)
                pe.wait_ge(s_hc, b * N + n + 1)
                for h in range(NH):
                    last = t.matmul(y_bank[h][:], ident, hc[n % 2][:, h, :], start=False, stop=(n == N - 1))
                last.then_inc(s_ys, 1)

            def pre(name, b, par):
                if name == "xnT":
                    take0(pe, b, name)
                    pe.wait_ge(s_xin, b * 16 + 16)
                    for j in range(NT):
                        last = t.transpose(bank0[:, j * P:(j + 1) * P], x_in[:, j, :], ident)
                    last.then_inc(s_full0, 1)
                elif name in ("hs0", "hs1", "zg0", "zg1"):
                    k = ("hs0", "hs1", "zg0", "zg1").index(name)
                    take0(pe, b, name)
                    t.matmul(bank0[:], pc("in_proj")[:, k * P:(k + 1) * P], xnT[:], start=True,
                             stop=True).then_inc(s_full0, 1)
                elif name == "xdbl":
                    take0(pe, b, name)
                    pe.wait_ge(s_u, b * NH + NH)
                    for j in range(NT):
                        for h in range(NH):
                            last = t.matmul(bank0[:, j * XW:(j + 1) * XW], u[:, h, j * P:(j + 1) * P],
                                            pc("x_proj")[:, h * XW:(h + 1) * XW], start=(h == 0), stop=(h == NH - 1))
                    last.then_inc(s_full0, 1)
                elif name == "dtT":
                    take0(pe, b, name)
                    pe.wait_ge(s_bc3, b * 6 + 1)
                    for j in range(NT):
                        last = t.transpose(bank0[0:XW, j * P:(j + 1) * P], xdn[:, j, :], ident)
                    last.then_inc(s_full0, 1)
                elif name == "bcT":
                    take0(pe, b, name)
                    pe.wait_ge(s_bc3, b * 6 + 6)
                    for j in range(NT):
                        last = t.transpose(bank0[0:96, :].bitcast(BF16)[:, j * P:(j + 1) * P],
                                           bc3[:, j, :, :].rearrange("p k n -> p (k n)"), identb[:])
                    last.then_inc(s_full0, 1)
                elif name in ("dtp0", "dtp1"):
                    h = int(name[3:])
                    take0(pe, b, name)
                    t.matmul(bank0[:], pc("dt_proj", R)[:, h * P:(h + 1) * P], dtT[:], start=True,
                             stop=True).then_inc(s_full0, 1)
                elif name == "start":
                    spread(b, 0, par)

            def layer1(name, k, b, par):
                if name == "y_end":
                    sum_y(b, N - 1)
                elif name == "out":
                    take1(pe, b, name)
                    pe.wait_ge(s_yg, NH * b + NH)
                    for h in range(NH):
                        last = t.matmul(w1k(name)[:], pc("out_proj")[:, h * P:(h + 1) * P], yg[par][:, h, :],
                                        start=(h == 0), stop=(h == NH - 1))
                    last.then_inc(s_full1, 1)
                elif name in ("outT0", "outT1", "finT0", "finT1"):
                    c, src = int(name[4:]), outT if name.startswith("out") else finT
                    take1_after(pe, b, name, name[:3])
                    for j in range(2):
                        last = t.transpose(w1k(name)[:, j * P:(j + 1) * P],
                                           src[:, (2 * c + j) * P:(2 * c + j + 1) * P], ident)
                    last.then_inc(s_full1, 1)
                elif name == "ln_b":
                    take1(pe, b, "xnT")
                    for j in range(NT):
                        pe.wait_ge(s_xn1, b * NT + j + 1)
                        last = t.transpose(w1k("xnT")[:, j * P:(j + 1) * P], xn1[:, j, :], ident)
                    last.then_inc(s_full1, 1)
                elif name in ("q", "k"):
                    take1_after(pe, b, name, "xnT")
                    t.matmul(w1k(name)[:], pc("w" + name), xn1T[:, WIN:WIN + L], start=True,
                             stop=True).then_inc(s_full1, 1)
                elif name in ("v0", "v1", "v2", "v3"):
                    j = int(name[1:])
                    take1(pe, b, name)
                    for g in range(4):
                        a = (4 * j + g) * GQ
                        last = t.matmul(w1k(name)[0:KW, g * P:(g + 1) * P], xn1T[:, a:a + KW], pc("wv"),
                                        start=True, stop=True)
                    last.then_inc(s_full1, 1)
                elif name == "scores":
                    key = f"s{k}"
                    if k == 0:
                        pe.wait_ge(s_qbd, b + 1)
                        done1(pe, b, "k")
                    take1(pe, b, key)
                    v = 0 if k == 0 else (2 if k == G - 1 else 1)
                    t.matmul(w1k(key)[:, 0:RG * KW], identb[:], bandb[:, v, :, :].rearrange("p r k -> p (r k)"),
                             start=True, stop=False)
                    t.matmul(w1k(key)[:, 0:RG * KW], qbd[:, k, :, :].rearrange("p h q -> p (h q)"),
                             kT[:, :, k * GQ:k * GQ + KW], start=False, stop=True).then_inc(s_full1, 1)
                elif name == "turn":
                    key = f"pT{k}"
                    take1_after(pe, b, key, f"s{k}")
                    for r in range(RG):
                        last = t.transpose(w1k(key)[0:KW, r * P:(r + 1) * P], pexp[k % 2][:, r, :], ident)
                    last.then_inc(s_full1, 1)
                elif name == "values":
                    key = f"o{k // 2}"
                    take1_after(pe, b, key, f"v{k // 4}", f"pT{k - 1}", f"pT{k}")
                    for c in range(2):
                        for r in range(RG):
                            a = (c * RG + r) * 33
                            last = t.matmul(w1k(key)[:, a:a + 33], pT[(k - 1 + c) % 4][:, r * P:(r + 1) * P],
                                            vw[:, k - 1 + c, r, :], start=True, stop=True)
                    last.then_inc(s_full1, 1)
                elif name == "ffn":
                    for j, key in enumerate((f"gate{k}", f"up{k}")):
                        take1(pe, b, key)
                        t.matmul(w1k(key)[:], ffn[:, j, k * P:(k + 1) * P], xn1T[:, WIN:WIN + L], start=True,
                                 stop=True).then_inc(s_full1, 1)
                elif name == "attnT":
                    take1_after(pe, b, name, f"o{G // 2 - 1}")
                    t.matmul(w1k(name)[:, 0:2], identb[:], identb[:, 0:2], start=True, stop=True)
                    for g in range(G):
                        last = t.transpose(w1k(name)[:, g * GQ:(g + 1) * GQ],
                                           attn[:, g, :, :, :].rearrange("p r h d -> p (r h d)"), ident[0:GQ, 0:GQ])
                    last.then_inc(s_full1, 1)
                elif name == "fin":
                    take1_after(pe, b, name, *[f"up{c}" for c in range(HC)])
                    for c in range(HC):
                        t.matmul(w1k(name)[:], ffn[:, 2, c * P:(c + 1) * P], fh[:, c, :], start=(c == 0), stop=False)
                    done1(pe, b, "attnT")
                    t.matmul(w1k(name)[:], pc("wo"), attnT[:], start=False, stop=True).then_inc(s_full1, 1)

            def body(it, par):
                for name, k, b in units(it):
                    if name == "spread":
                        if k + 1 < N:
                            spread(b, k + 1, par)
                    elif name == "sum":
                        if k:
                            sum_y(b, k - 1)
                    else:
                        pre(name, b, 1 - par)
                        layer1(name, k, b, 1 - par)
            iterations(pe, body)


def kernel(**inputs):
    import concourse.bacc as bacc
    from concourse.bass_utils import run_bass_kernel_spmd

    a = {k: np.asarray(v) for k, v in inputs.items()}
    f = np.float32

    def cols(m):
        return np.concatenate([m[i:i + P].reshape(P, -1) for i in range(0, m.shape[0], P)], axis=1)

    def rows(m):
        return np.concatenate([m, np.zeros((P - m.shape[0], m.shape[1]), m.dtype)], axis=0)

    def spread(m):
        return np.broadcast_to(m.reshape(1, -1), (P, m.size))

    q, k = np.arange(P)[:, None] % GQ, np.arange(KW)[None, :]
    inside = (k >= q) & (k <= q + 2 * WIN)
    band = [np.where(m, 0.0, NEG).astype(f) for m in (inside & (k >= WIN), inside, inside & (k < WIN + GQ))]
    ln_row = np.concatenate([a["L0_attn_dt_ln_w"], a["L0_attn_b_ln_w"], a["L0_attn_c_ln_w"]])
    parts = {
        "in_proj": a["L0_attn_in_proj_w"].T, "x_proj": cols(a["L0_attn_x_proj_w"].T),
        "out_proj": cols(a["L0_attn_out_proj_w"].T), "dt_proj": rows(a["L0_attn_dt_proj_w"].T),
        "wq": a["L1_attn_Wq"], "wk": a["L1_attn_Wk"], "wv": a["L1_attn_Wv"], "wo": a["L1_attn_Wo"],
        "conv_w": cols(a["L0_attn_conv_w"].reshape(I, KC)), "conv_b": cols(a["L0_attn_conv_b"].reshape(I, 1)),
        "dt_b": cols(a["L0_attn_dt_proj_b"].reshape(I, 1)), "a_log": cols(a["L0_attn_A_log"]),
        "d": cols(a["L0_attn_D"].reshape(I, 1)), "gate_w": a["L0_ffn_gate_w"].T,
        "bq": a["L1_attn_bq"].reshape(H, 1), "bk": a["L1_attn_bk"].reshape(H, 1),
        "bv": a["L1_attn_bv"].reshape(H, 1), "bo": a["L1_attn_bo"].reshape(H, 1),
        "b1": a["L0_ffn_b1"].reshape(E * FC, P).T, "b2": spread(a["L0_ffn_b2"]), "ln_row": spread(ln_row),
        "gate_b": spread(a["L0_ffn_gate_b"]), "expert_b": spread(a["L0_ffn_expert_bias"]),
        "ident": np.eye(P, dtype=f), "sel": rows(np.tile(np.eye(2 * N, dtype=f), (3, 1))),
        "band": np.concatenate(band, axis=1), "heads": (np.arange(P)[:, None] % 32 // HD == np.arange(RG)).astype(f),
        "expert_no": spread(np.arange(E, dtype=f)), "rms_n": spread(np.array([1 / R, 1 / N, 1 / N], f)),
        "below": np.triu(np.ones((P, P), f), 1), "tile_at": spread(np.arange(NM, dtype=f) * P),
    }
    ffn = np.stack([a["L1_ffn_w_gate"].T, a["L1_ffn_w_up"].T, cols(a["L1_ffn_w_down"].T)], axis=1)
    arrays = {
        "hidden": a["L0_attn_hidden_states"],
        "pack": np.concatenate([parts[n] for n in PACK], axis=1),
        "w1": a["L0_ffn_w1"].transpose(1, 0, 2),
        "w2": a["L0_ffn_w2"].reshape(E, FC, P, H).transpose(2, 0, 1, 3),
        "ffn": ffn,
    }
    arrays = {"in_" + n: np.ascontiguousarray(m) for n, m in arrays.items()}
    nc = bacc.Bacc("TRN2", target_bir_lowering=False, num_devices=1)
    args = [nc.dram_tensor(n, m.shape, mybir.dt.from_np(m.dtype), kind="ExternalInput").ap() for n, m in arrays.items()]
    out = nc.dram_tensor("out", (B, L, H), F32, kind="ExternalOutput").ap()
    xn_d = nc.dram_tensor("xn_d", (B, L, H), F32, kind="Internal").ap()
    xs_d = nc.dram_tensor("xs_d", (NM // MG, MG, P, H), F32, kind="Internal").ap()
    ys_d = nc.dram_tensor("ys_d", (NM // MG, MG, P, H), F32, kind="Internal").ap()
    program(nc, *args, xn_d, xs_d, ys_d, out)
    r = run_bass_kernel_spmd(nc, [arrays], core_ids=[0])
    return r.results[0]["out"]
```
